# Optimizing a Trainium2 kernel written in Bass

```python
import numpy as np
import jax
import jax.numpy as jnp

def _softmax(x, axis=-1):
    return jax.nn.softmax(x, axis=axis)

def _gelu(x):
    return jax.nn.gelu(x, approximate=True)

def _silu(x):
    return jax.nn.silu(x)

def _sigmoid(x):
    return jax.nn.sigmoid(x)

def _layernorm(x, axis=-1, eps=1e-05):
    m = jnp.mean(x, axis=axis, keepdims=True)
    v = jnp.var(x, axis=axis, keepdims=True)
    return (x - m) / jnp.sqrt(v + eps)

def _scatter_add(tgt, idx, src, axis=0):
    return tgt.at[idx].add(src)

def _segment_sum(src, seg, n):
    return jax.ops.segment_sum(src, seg, n)
kernel_name = 'mk_gps_d1_gnn_r8_78e2d6'

def setup_inputs(seed: int=0):
    np.random.seed(seed)
    _w = jnp.asarray

    def _rec_inputs():
        import jax
        import jax.numpy as jnp
        _gk = jax.random.key(seed)
        x = -8.776e-05 + 1 * jax.random.normal(jax.random.fold_in(_gk, 1), (2500, 256), jnp.float32)
        _s = jax.random.randint(jax.random.fold_in(_gk, 2), (20000,), 0, 2500, jnp.int32)
        _d = jax.random.randint(jax.random.fold_in(_gk, 3), (20000,), 0, 2500, jnp.int32)
        _loop = jnp.arange(2500, dtype=jnp.int32)
        src = jnp.concatenate([_s, _d, _loop])
        dst = jnp.concatenate([_d, _s, _loop])
        _o = jnp.argsort(dst, stable=True)
        src = src[_o]
        dst = dst[_o]
        return (x, src, dst)
    x, src, dst = _rec_inputs()

    def _L0_gnn_setup():
        import jax, jax.numpy as jnp
        import numpy as np
        N = 2500
        E = 40000
        DIN = 256
        DOUT = 256
        L = 3

        def _edge_conv(x, src, dst, W, b):
            xi = x[dst]
            xj = x[src]
            m = jnp.concatenate([xi, xj - xi], axis=-1) @ W + b
            s = jax.ops.segment_sum(m, dst, num_segments=N)
            cnt = jax.ops.segment_sum(jnp.ones((dst.shape[0],), m.dtype), dst, num_segments=N)
            return s / jnp.maximum(cnt, 1.0)[:, None]
        key = jax.random.key(seed)
        ks = jax.random.split(key, 4 + 2 * L)
        x = jax.random.normal(ks[0], (N, DIN), dtype=jnp.float32)
        edge_index = jax.random.randint(ks[1], (2, E), 0, N, dtype=jnp.int64)
        scale = 0.05
        inp = {'x': x, 'edge_index': edge_index}
        din = DIN
        for l in range(L):
            inp[f'W{l}'] = jax.random.normal(ks[2 + l], (2 * din, DOUT), dtype=jnp.float32) * scale
            inp[f'b{l}'] = jnp.zeros((DOUT,), dtype=jnp.float32)
            din = DOUT
        cat_dim = DIN + L * DOUT
        inp['Wf'] = jax.random.normal(ks[2 + L], (cat_dim, DOUT), dtype=jnp.float32) * scale
        inp['bf'] = jnp.zeros((DOUT,), dtype=jnp.float32)
        return inp
    _L0_gnn_all = _L0_gnn_setup()
    _L0_gnn_in = {k: v for k, v in _L0_gnn_all.items() if k in ('W0', 'b0', 'W1', 'b1', 'W2', 'b2', 'Wf', 'bf')}
    del _L0_gnn_all

    def _L0_mix_setup():
        import jax, jax.numpy as jnp
        import numpy as np
        MIDC = 256
        HEADS = 8
        HEADC = MIDC // HEADS
        EPS = 1e-05

        def _ln(x, gamma, beta):
            mu = jnp.mean(x, axis=-1, keepdims=True)
            var = jnp.var(x, axis=-1, keepdims=True)
            return (x - mu) * jax.lax.rsqrt(var + EPS) * gamma + beta
        key = jax.random.key(seed)
        ks = jax.random.split(key, 8)
        B, HW, C = (8, 512, MIDC)
        s = 1.0 / np.sqrt(C)
        return {'x': jax.random.normal(ks[0], (B, HW, C), jnp.float32), 'w_qkv': jax.random.normal(ks[1], (C, 3 * C), jnp.float32) * s, 'b_qkv': jnp.zeros((3 * C,), jnp.float32), 'kln_g': jnp.ones((HEADC,), jnp.float32), 'kln_b': jnp.zeros((HEADC,), jnp.float32), 'vln_g': jnp.ones((HEADC,), jnp.float32), 'vln_b': jnp.zeros((HEADC,), jnp.float32), 'w1': jax.random.normal(ks[2], (C, C), jnp.float32) * s, 'b1': jnp.zeros((C,), jnp.float32), 'w2': jax.random.normal(ks[3], (C, C), jnp.float32) * s, 'b2': jnp.zeros((C,), jnp.float32)}
    _L0_mix_all = _L0_mix_setup()
    _L0_mix_in = {k: v for k, v in _L0_mix_all.items() if k in ('w_qkv', 'b_qkv', 'kln_g', 'kln_b', 'vln_g', 'vln_b', 'w1', 'b1', 'w2', 'b2')}
    del _L0_mix_all

    def _L0_ffn_setup():
        import jax, jax.numpy as jnp
        import numpy as np
        TOP_K = 2
        LN_EPS = 1e-05
        key = jax.random.key(seed)
        ks = jax.random.split(key, 8)
        B, S, D, E, H = (16, 1024, 256, 8, 1024)
        x = jax.random.normal(ks[0], (B, S, D), dtype=jnp.float32)
        Wr = jax.random.normal(ks[1], (D, E), dtype=jnp.float32) * 0.1
        br = jnp.zeros((E,), dtype=jnp.float32)
        ln_g = jnp.ones((E, D), dtype=jnp.float32)
        ln_b = jnp.zeros((E, D), dtype=jnp.float32)
        W1 = jax.random.normal(ks[2], (E, D, H), dtype=jnp.float32) * (1.0 / np.sqrt(D))
        b1 = jnp.zeros((E, H), dtype=jnp.float32)
        W2 = jax.random.normal(ks[3], (E, H, D), dtype=jnp.float32) * (1.0 / np.sqrt(H))
        b2 = jnp.zeros((E, D), dtype=jnp.float32)
        return {'x': x, 'Wr': Wr, 'br': br, 'ln_g': ln_g, 'ln_b': ln_b, 'W1': W1, 'b1': b1, 'W2': W2, 'b2': b2}
    _L0_ffn_all = _L0_ffn_setup()
    _L0_ffn_in = {k: v for k, v in _L0_ffn_all.items() if k in ('Wr', 'br', 'ln_g', 'ln_b', 'W1', 'b1', 'W2', 'b2')}
    del _L0_ffn_all
    return {'x': x, 'src': src, 'dst': dst, 'L0_gnn_W0': _L0_gnn_in['W0'], 'L0_gnn_b0': _L0_gnn_in['b0'], 'L0_gnn_W1': _L0_gnn_in['W1'], 'L0_gnn_b1': _L0_gnn_in['b1'], 'L0_gnn_W2': _L0_gnn_in['W2'], 'L0_gnn_b2': _L0_gnn_in['b2'], 'L0_gnn_Wf': _L0_gnn_in['Wf'], 'L0_gnn_bf': _L0_gnn_in['bf'], 'L0_mix_w_qkv': _L0_mix_in['w_qkv'], 'L0_mix_b_qkv': _L0_mix_in['b_qkv'], 'L0_mix_kln_g': _L0_mix_in['kln_g'], 'L0_mix_kln_b': _L0_mix_in['kln_b'], 'L0_mix_vln_g': _L0_mix_in['vln_g'], 'L0_mix_vln_b': _L0_mix_in['vln_b'], 'L0_mix_w1': _L0_mix_in['w1'], 'L0_mix_b1': _L0_mix_in['b1'], 'L0_mix_w2': _L0_mix_in['w2'], 'L0_mix_b2': _L0_mix_in['b2'], 'L0_ffn_Wr': _L0_ffn_in['Wr'], 'L0_ffn_br': _L0_ffn_in['br'], 'L0_ffn_ln_g': _L0_ffn_in['ln_g'], 'L0_ffn_ln_b': _L0_ffn_in['ln_b'], 'L0_ffn_W1': _L0_ffn_in['W1'], 'L0_ffn_b1': _L0_ffn_in['b1'], 'L0_ffn_W2': _L0_ffn_in['W2'], 'L0_ffn_b2': _L0_ffn_in['b2']}

def reference(x, src, dst, L0_gnn_W0, L0_gnn_b0, L0_gnn_W1, L0_gnn_b1, L0_gnn_W2, L0_gnn_b2, L0_gnn_Wf, L0_gnn_bf, L0_mix_w_qkv, L0_mix_b_qkv, L0_mix_kln_g, L0_mix_kln_b, L0_mix_vln_g, L0_mix_vln_b, L0_mix_w1, L0_mix_b1, L0_mix_w2, L0_mix_b2, L0_ffn_Wr, L0_ffn_br, L0_ffn_ln_g, L0_ffn_ln_b, L0_ffn_W1, L0_ffn_b1, L0_ffn_W2, L0_ffn_b2):
    import jax
    import jax.numpy as jnp

    def _L0_gnn_ref(x, edge_index, W0, b0, W1, b1, W2, b2, Wf, bf):
        import jax, jax.numpy as jnp
        import numpy as np
        N = 2500
        E = 40000
        DIN = 256
        DOUT = 256
        L = 3

        def _edge_conv(x, src, dst, W, b):
            xi = x[dst]
            xj = x[src]
            m = jnp.concatenate([xi, xj - xi], axis=-1) @ W + b
            s = jax.ops.segment_sum(m, dst, num_segments=N)
            cnt = jax.ops.segment_sum(jnp.ones((dst.shape[0],), m.dtype), dst, num_segments=N)
            return s / jnp.maximum(cnt, 1.0)[:, None]
        src, dst = (edge_index[0], edge_index[1])
        xs = [x]
        h = x
        for W, b in ((W0, b0), (W1, b1), (W2, b2)):
            h = jax.nn.relu(_edge_conv(h, src, dst, W, b))
            xs.append(h)
        cat = jnp.concatenate(xs, axis=-1)
        return cat @ Wf + bf

    def _L0_mix_ref(x, w_qkv, b_qkv, kln_g, kln_b, vln_g, vln_b, w1, b1, w2, b2):
        import jax, jax.numpy as jnp
        import numpy as np
        MIDC = 256
        HEADS = 8
        HEADC = MIDC // HEADS
        EPS = 1e-05

        def _ln(x, gamma, beta):
            mu = jnp.mean(x, axis=-1, keepdims=True)
            var = jnp.var(x, axis=-1, keepdims=True)
            return (x - mu) * jax.lax.rsqrt(var + EPS) * gamma + beta
        B, HW, C = x.shape
        bias = x
        qkv = (x @ w_qkv + b_qkv).reshape(B, HW, HEADS, 3 * HEADC)
        qkv = qkv.transpose(0, 2, 1, 3)
        q, k, v = jnp.split(qkv, 3, axis=-1)
        k = _ln(k, kln_g, kln_b)
        v = _ln(v, vln_g, vln_b)
        kv = jnp.einsum('bhnd,bhne->bhde', k, v) / HW
        out = jnp.einsum('bhnd,bhde->bhne', q, kv)
        out = out.transpose(0, 2, 1, 3).reshape(B, HW, C)
        ret = out + bias
        h = jax.nn.gelu(ret @ w1 + b1, approximate=False)
        return h @ w2 + b2 + bias

    def _L0_ffn_ref(x, Wr, br, ln_g, ln_b, W1, b1, W2, b2):
        import jax, jax.numpy as jnp
        import numpy as np
        TOP_K = 2
        LN_EPS = 1e-05
        B, S, D = x.shape
        N = B * S
        xt = x.reshape(N, D)
        logits = xt @ Wr + br
        probs = jax.nn.softmax(logits, axis=-1)
        top_p, top_idx = jax.lax.top_k(probs, TOP_K)
        weights = top_p / top_p.sum(axis=-1, keepdims=True)
        mu = xt.mean(axis=-1, keepdims=True)
        var = ((xt - mu) ** 2).mean(axis=-1, keepdims=True)
        xn = (xt - mu) * jax.lax.rsqrt(var + LN_EPS)
        xe = xn[None, :, :] * ln_g[:, None, :] + ln_b[:, None, :]
        h = jax.nn.gelu(jnp.einsum('end,edh->enh', xe, W1) + b1[:, None, :], approximate=False)
        y = jnp.einsum('enh,ehd->end', h, W2) + b2[:, None, :]
        y_tok = jnp.transpose(y, (1, 0, 2))
        sel = jnp.take_along_axis(y_tok, top_idx[:, :, None], axis=1)
        out = (weights[:, :, None] * sel).sum(axis=1)
        return out.reshape(B, S, D)
    edge_index = jnp.stack([src, dst])
    xn = _layernorm(x, axis=-1)
    x = x + _L0_gnn_ref(xn, edge_index, L0_gnn_W0, L0_gnn_b0, L0_gnn_W1, L0_gnn_b1, L0_gnn_W2, L0_gnn_b2, L0_gnn_Wf, L0_gnn_bf) + _L0_mix_ref(xn[None], L0_mix_w_qkv, L0_mix_b_qkv, L0_mix_kln_g, L0_mix_kln_b, L0_mix_vln_g, L0_mix_vln_b, L0_mix_w1, L0_mix_b1, L0_mix_w2, L0_mix_b2)[0]
    x = x + _L0_ffn_ref(_layernorm(x, axis=-1)[None], L0_ffn_Wr, L0_ffn_br, L0_ffn_ln_g, L0_ffn_ln_b, L0_ffn_W1, L0_ffn_b1, L0_ffn_W2, L0_ffn_b2)[0]
    return x

_drawn_inputs = setup_inputs


def setup_inputs(seed=0):
    import zlib

    import numpy as np

    out = dict(_drawn_inputs(seed))
    spreads = {'L0_gnn_b0': (0.0, 0.1),
     'L0_gnn_b1': (0.0, 0.1),
     'L0_gnn_b2': (0.0, 0.1),
     'L0_gnn_bf': (0.0, 0.1),
     'L0_mix_b_qkv': (0.0, 0.1),
     'L0_mix_kln_g': (1.0, 0.581),
     'L0_mix_kln_b': (0.0, 0.309),
     'L0_mix_vln_g': (1.0, 0.2),
     'L0_mix_vln_b': (0.0, 0.308),
     'L0_mix_b1': (0.0, 0.1),
     'L0_mix_b2': (0.0, 0.1),
     'L0_ffn_br': (0.0, 0.1),
     'L0_ffn_ln_g': (1.0, 0.2),
     'L0_ffn_ln_b': (0.0, 0.371),
     'L0_ffn_b1': (0.0, 0.358),
     'L0_ffn_b2': (0.0, 0.1)}
    factors = {}
    for name, (base, spread) in spreads.items():
        noise = np.random.default_rng([zlib.crc32(name.encode()), seed]).standard_normal(out[name].shape)
        drawn = base * np.exp(spread * noise) if base else spread * noise
        out[name] = jnp.asarray(drawn.astype(out[name].dtype))
    for name, factor in factors.items():
        out[name] = (out[name] * factor).astype(out[name].dtype)
    return out
```

```python
import contextlib

import numpy as np

import concourse.bass as bass
from concourse import mybir

ALU = mybir.AluOpType
ACT = mybir.ActivationFunctionType
AX_X = mybir.AxisListType.X
F32, F16 = mybir.dt.float32, mybir.dt.float16
I32, U32 = mybir.dt.int32, mybir.dt.uint32

P = 128
N = 2500
D = 256
KD = D // P
NT = (N + P - 1) // P
NP = NT * P
LAST = N - (NT - 1) * P
NC = NP // 512
E_ALL = 42500
NOWHERE = 4095

GW = 16
NG = NP // GW
GB = NG // 2
STEP = 16
WIN = 3 * P
NWIN = 2688
NS = NWIN // P
EC = (E_ALL + P - 1) // P
KEYS = NT * GW
PASSES = (E_ALL + WIN - 1) // WIN

HEADS = 8
HC = D // HEADS
NE = 8
H = 1024
KH = H // P
TOPK = 2
NB = (TOPK * N + NE * (P - 1)) // P
SLOTS = NB * P
EPS = 1e-5
WS = 64.0

AT_B = NT * NP * 2
HALF = KD * NP * 2


def split_memory(mem):
    def view(off, dims, dt):
        size = 4 if dt in (F32, I32, U32) else 2
        n = int(np.prod(dims))
        v = mem[:, off // 2:(off + n * size) // 2]
        if dt != F16:
            v = v.bitcast(dt)
        if len(dims) == 2:
            v = v.rearrange("p (a b) -> p a b", b=dims[1])
        elif len(dims) == 3:
            v = v.rearrange("p (a b c) -> p a b c", b=dims[1], c=dims[2])
        elif len(dims) == 4:
            v = v.rearrange("p (a b c d) -> p a b c d", b=dims[1], c=dims[2], d=dims[3])
        return v
    return view


def build(nc, I, out):
    ctx = contextlib.ExitStack()
    with ctx:
        ctx.enter_context(nc.allow_non_contiguous_dma(reason="small parameter rows"))
        TOP = 211968
        mem = ctx.enter_context(nc.sbuf_tensor("mem", [P, TOP // 2], F16))
        view = split_memory(mem)
        ps = ctx.enter_context(nc.psum_tensor("ps", [P, 8, 512], F32))

        names = {}

        def S(name):
            if name not in names:
                names[name] = ctx.enter_context(nc.semaphore(name))
            return names[name]

        xslots = nc.dram_tensor("xslots", (SLOTS, D), F32).ap()
        yslots = nc.dram_tensor("yslots", (SLOTS, D), F32).ap()

        off = 0
        at = view(0, [NT, NP], F16)
        ht_hi = view(AT_B, [KD, NP], F16)
        ht_lo = view(AT_B + HALF, [KD, NP], F16)
        g_hi = view(AT_B + 2 * HALF, [NT, D], F16)
        g_lo = view(AT_B + 3 * HALF, [NT, D], F16)
        h1_hi = view(AT_B + 2 * HALF, [KD, NP], F16)
        h1_lo = view(AT_B + 3 * HALF, [KD, NP], F16)
        xn = view(AT_B + 2 * HALF, [NT, D], F32)
        ACC_B = AT_B + 4 * HALF
        acc = view(ACC_B, [NT, D], F32)
        WR_B = ACC_B + NT * D * 4
        wd_hi = view(WR_B, [3, KD, D], F16)
        wd_lo = view(WR_B + 3072, [3, KD, D], F16)
        wbf_hi = view(WR_B + 6144, [3, KD, 2, D], F16)
        wbf_lo = view(WR_B + 12288, [3, KD, 2, D], F16)
        wf3_hi = view(WR_B + 18432, [KD, D], F16)
        wf3_lo = view(WR_B + 19456, [KD, D], F16)
        w2_hi = view(WR_B + 20480, [KD, D], F16)
        w2_lo = view(WR_B + 21504, [KD, D], F16)
        m1_hi = view(WR_B + 22528, [KD, D], F16)
        m1_lo = view(WR_B + 23552, [KD, D], F16)
        RC_B = WR_B + 24576
        rcnt = view(RC_B, [NP], F32)
        has = view(RC_B + 10240, [NP], F16)
        src_hot = view(RC_B, [2, 3, P], F16)
        key_hot = view(RC_B + 1536, [2, 3, KEYS], F16)
        key_t = view(RC_B + 6144, [3, NG], F32)
        lo_t = view(RC_B + 8192, [3, NG], F32)
        iota_key = view(RC_B + 10240, [KEYS], F16)
        iota_p = view(RC_B + 10880, [P], F16)
        C_B = RC_B + 15360
        R_B0 = C_B + 2720
        ident = view(C_B, [P], F32)
        ones = view(C_B + 512, [P], F32)
        below = view(C_B + 1024, [P], F32)
        cols = view(C_B + 1536, [P], F32)
        ones16 = view(C_B + 2048, [2], F16)
        mv = view(C_B + 2112, [NT, 2], F32)
        rstd = view(C_B + 2304, [NT], F32)
        grp = view(C_B + 2400, [2], F32)
        cnts = view(C_B + 2416, [4], F32)
        excess = view(C_B + 2432, [2], F32)
        viol = view(C_B + 2440, [1], F32)
        widx = view(C_B + 2448, [2], U32)
        bad = view(C_B + 2456, [1], I32)
        eps = view(C_B + 2464, [1], F32)
        iota8 = view(C_B + 2496, [NE], F32)
        onesq = view(R_B0, [P], F16)
        any_s, any_d = view(AT_B + 2 * HALF, [WIN], I32), view(AT_B + 2 * HALF + 1536, [WIN], I32)
        any_k, any_lo = view(AT_B + 2 * HALF + 3072, [WIN], F32), view(AT_B + 2 * HALF + 4608, [WIN], F32)
        any_a, any_b, any_c = (view(AT_B + 2 * HALF + 6144 + 3072 * i, [2, WIN], F32) for i in range(3))
        any_i = view(AT_B + 2 * HALF + 15360, [WIN], I32)
        ident16 = view(AT_B + 2 * HALF + 17408, [P], F16)
        blockdiag = view(R_B0 + 256, [P], F32)
        onecol = view(C_B + 2528, [1], F32)
        b1p = view(C_B + 2536, [KD], F32)
        retb = view(C_B + 2544, [KD], F32)
        nmr = view(C_B + 2560, [NT], F32)
        std = view(C_B + 2640, [NT], F32)
        R_B = C_B + 2720 + 768
        tmp_t = view(R_B, [2, 512], F32)
        tmp_p = view(WR_B + 20480, [2, 512], F32)

        spot = [0]

        def temp(dims, dt):
            v = view(spot[0], dims, dt)
            spot[0] += -(-int(np.prod(dims)) * (2 if dt == F16 else 4) // 32) * 32
            assert spot[0] <= AT_B
            return v

        stg = temp([3, 6, D], F32)
        stg3 = temp([KD, D], F32)
        stgw2 = temp([KD, D], F32)
        w1 = temp([KD, D], F32)
        wqkv = temp([KD, 3 * D], F32)
        wkvc = temp([KD, 512], F32)
        wkv_hi = temp([KD, 512], F16)
        wkv_lo = temp([KD, 512], F16)
        wq = temp([KD, D], F32)
        wqT = temp([KD, D + 1], F32)
        bkv = temp([512], F32)
        bias_kv = temp([512], F32)
        gbkv = temp([4, HC], F32)
        bout = temp([2, D], F32)
        msum = temp([KD, 16], F32)
        bsum = temp([16], F32)
        kvm = temp([KD, P], F32)
        mT = temp([KD, D + 1], F32)
        sk = temp([KD], F32)
        kvt = temp([KD, P], F32)
        h1f = temp([2, 512], F32)
        kv_z = temp([4, 512], F32)
        kv_sq = temp([4, 512], F32)
        kv_n = temp([4, 512], F32)
        kst = temp([4, 16], F32)
        kst2 = temp([4, 16], F32)
        stack = temp([P], F32)
        samp_i = temp([NS], I32)
        samp = temp([NS], F32)
        lt = temp([NS, NG + 2], F16)
        bounds = temp([NG + 2], F16)
        pair = temp([EC + 1], I32)
        cmp = temp([EC], F32)
        win_s = temp([2, WIN], I32)
        win_d = temp([2, WIN], I32)
        zero = temp([D], F32)
        ka, kb, kc, klo = (view(i * 3072, [2, WIN], F32) for i in range(4))
        ki = view(4 * 3072, [2, WIN], I32)
        st6 = view(R_B, [NT, 6], F32)

        EW = 16384
        w_e = [[view(EW * e, [KD, H], F16), view(EW * e + 4096, [KD, H], F16),
                view(EW * e + 8192, [KH, D], F16), view(EW * e + 12288, [KH, D], F16)] for e in range(NE)]
        W1_HI, W1_LO, W2_HI, W2_LO = (i * 2048 for i in range(4))
        EWN = EW // 2
        b2_all = view(NE * EW, [NE, D], F32)
        ew_raw = [view(8192 * i + 12288, [2048], F32) for i in range(2 * NE)]
        assert 8192 * (2 * NE - 1) + 12288 + 8192 <= ACC_B
        RAW_IN_AT = (AT_B - 12288) // 8192
        rt = [RC_B]

        def small(dims, dt=F32):
            v = view(rt[0], dims, dt)
            rt[0] += -(-int(np.prod(dims)) * 4 // 32) * 32
            return v

        logit, mx = small([NT, NE]), small([NT, NE])
        hot1, hot2, hot12 = small([NT, NE]), small([NT, NE]), small([NT, NE])
        top = small([NT, NE], U32)
        assert rt[0] <= RC_B + 12288
        rt[0] = R_B
        tot_a, tot_b, rank = small([NT, NE]), small([NT, NE]), small([NT, NE])
        topf = small([NT, 2])
        slot_f, slot = small([TOPK, NT]), small([TOPK, NT], U32)
        wgt = small([TOPK, NT])
        nblk, cum, cum2, base = small([NE]), small([NE]), small([NE]), small([NE])
        nblk_i = small([NE], I32)
        valid = small([1])
        blk = small([NB])
        blk_e = small([NB], I32)
        assert rt[0] <= TOP, rt[0]
        wr, br = view(R_B + 4096, [KD, NE], F32), view(R_B + 4096 + 64, [NE], F32)
        blk_ge = view(RC_B + 12288, [NB, NE], F32)
        xn2 = view(WR_B, [NT, D], F32)
        yT = view(RC_B + 12288, [2, KD, P], F32)
        xe = view(WR_B, [KD, P], F32)
        xe_hi, xe_lo = view(WR_B + 1024, [2, KD, P], F16), view(WR_B + 2048, [2, KD, P], F16)
        hf = view(WR_B + 3072, [2, KH, P], F32)
        h_hi, h_lo = view(WR_B + 11264, [2, KH, P], F16), view(WR_B + 15360, [2, KH, P], F16)
        x_in, y_out = view(WR_B + 19456, [2, D], F32), view(WR_B + 21504, [2, D], F32)
        w1_now = view(WR_B + 23552, [2, 2, KD, H], F16)
        assert WR_B + 23552 + 16384 <= C_B
        y1, y2 = view(0, [NT, D], F32), view(NT * D * 4, [NT, D], F32)

        PHASES1 = 3
        NPAIR = NB // 2
        BIAS_DMAS = 8

        def barrier(e):
            NBAR_i[e] = NBAR_i.get(e, 0) + 1
            e.drain().then_inc(S("phase"), 1)
            e.wait_ge(S("phase"), 5 * NBAR_i[e])
        NBAR_i = {}

        def unsorted(e):
            return e.value_load(bad[0:1, 0:1], min_val=0, max_val=1 << 20)

        block = ctx.enter_context(nc.Block())

        HALF_LIST = [(wd_hi[:, l], wd_lo[:, l], stg[:, l, 0:2]) for l in range(3)]
        HALF_LIST += [(wbf_hi[:, l, :, w], wbf_lo[:, l, :, w], stg[:, l, 2 + 2 * w:4 + 2 * w]) for l in range(3) for w in range(2)]
        HALF_LIST += [(wf3_hi, wf3_lo, stg3), (w2_hi, w2_lo, stgw2), (wkv_hi, wkv_lo, wkvc)]
        NSPLIT = len(HALF_LIST)

        def heads(v, first, n=8):
            return v.rearrange("p (h c) -> p h c", c=HC)

        def bc(v, dims):
            return v.to_broadcast(dims)

        @block.sync
        def _(sp):
            x = I["x"]
            sp.dma_start(samp_i, I["dsamp"]).then_inc(S("samp_in"), 16)
            sp.dma_start(pair, I["dpair"]).then_inc(S("pair_in"), 16)
            sp.dma_start(acc[:, 0:NT - 1, :], x[0:(NT - 1) * P, :].rearrange("(t p) d -> p t d", p=P)).then_inc(S("x_in"), 16)
            sp.wait_ge(S("pad0"), 1)
            sp.dma_start(acc[0:LAST, NT - 1, :], x[(NT - 1) * P:N, :]).then_inc(S("x_in"), 16)
            sp.dma_start(wqkv, I["L0_mix_w_qkv"].rearrange("(r p) d -> p r d", p=P)).then_inc(S("wqkv_in"), 16)
            sp.dma_start(w1, I["L0_mix_w1"].rearrange("(r p) d -> p r d", p=P)).then_inc(S("w1_in"), 16)
            for l in range(3):
                sp.dma_start(stg[:, l, 0:4, :], I[f"L0_gnn_W{l}"].rearrange("(r p) d -> p r d", p=P)).then_inc(S("w_in"), 16)
                sp.dma_start(stg[:, l, 4:6, :], I["L0_gnn_Wf"][l * D:(l + 1) * D, :].rearrange("(r p) d -> p r d", p=P)).then_inc(S("w_in"), 16)
            sp.dma_start(stg3, I["L0_gnn_Wf"][3 * D:4 * D, :].rearrange("(r p) d -> p r d", p=P)).then_inc(S("w_in"), 16)
            sp.dma_start(stgw2, I["L0_mix_w2"].rearrange("(r p) d -> p r d", p=P)).then_inc(S("w_in"), 16)
            sp.wait_ge(S("consts"), 1)
            sp.dma_start(xslots.rearrange("(b p) d -> p b d", p=P), zero.rearrange("p (b d) -> p b d", b=1).to_broadcast([P, NB, D])).then_inc(S("slots_zero"), 16)
            sp.wait_ge(S("slots_zero"), 16)
            barrier(sp)
            with sp.If(unsorted(sp) > 0):
                with sp.Fori(0, PASSES) as q:
                    sp.wait_ge(S("any_read"), q + 1)
                    for tab, dst in ((I["srcw"], any_s), (I["dstw"], any_d)):
                        sp.dma_start(dst[0:GB], tab[bass.ds(q * (WIN // STEP), 1), :].to_broadcast([GB, WIN])).then_inc(S("any_in"), 16)
            sp.nop()
            barrier(sp)
            sp.dma_start(wr, I["L0_ffn_Wr"].rearrange("(k p) e -> p k e", p=P)).then_inc(S("wr_in"), 16)
            sp.dma_start(br, I["L0_ffn_br"].partition_broadcast(P)).then_inc(S("wr_in"), 16)
            sp.wait_ge(S("agg"), 3 * NC)
            for i in range(2 * NE):
                e, w = divmod(i, 2)
                if i == RAW_IN_AT:
                    sp.wait_ge(S("f3"), NT)
                src = (I["L0_ffn_W1"], I["L0_ffn_W2"])[w][e].rearrange("(k p) n -> p k n", p=P)
                sp.dma_start(ew_raw[i].rearrange("p (k n) -> p k n", k=(KD, KH)[w]), src).then_inc(S(f"ew_in{e}"), 16)
            barrier(sp)
            sp.wait_ge(S("ew_lo"), 2 * NE)
            sp.dma_start(b2_all, I["L0_ffn_b2"].rearrange("e d -> (e d)").partition_broadcast(P)).then_inc(S("b2_in"), 16)
            barrier(sp)

            def load(b, u):
                sp.wait_ge(S("e_turned"), b + 1)
                sp.dma_start(x_in[:, u], xslots[bass.ds(b * P, P), :]).then_inc(S(f"e_x{u}"), 16)

            load(0, 0)
            load(1, 1)
            with sp.Fori(0, NPAIR - 1) as bb:
                for u in range(2):
                    load(2 * bb + 2 + u, u)
            load(NB - 1, 0)
            barrier(sp)
            for t in range(NT):
                n = P if t < NT - 1 else LAST
                sp.wait_ge(S("final"), t + 1)
                sp.dma_start(out[t * P:t * P + n, :], acc[0:n, t, :]).then_inc(S("out"), 16)
            sp.wait_ge(S("out"), 16 * NT)

        @block.gpsimd
        def _(pool):
            pool.memset(ident, 0.0)
            pool.memset(below, 1.0)
            pool.memset(ones, 1.0)
            pool.memset(ones16, 1.0)
            pool.memset(onesq, 1.0)
            pool.memset(blockdiag, 1.0 / N)
            pool.memset(zero, 0.0)
            pool.memset(stack, 0.0)
            pool.memset(eps, EPS).then_inc(S("fill"), 1)
            pool.iota(bounds, [[GW, NG + 2]], base=0, channel_multiplier=0, allow_small_or_imprecise_dtypes=True)
            pool.iota(iota_key, [[1, KEYS]], base=1, channel_multiplier=0, allow_small_or_imprecise_dtypes=True)
            pool.iota(iota_p, [[1, P]], base=0, channel_multiplier=0, allow_small_or_imprecise_dtypes=True)
            pool.iota(iota8, [[1, NE]], base=0, channel_multiplier=0, allow_small_or_imprecise_dtypes=True)
            pool.iota(grp, [[-GW * GB, 2]], base=0, channel_multiplier=-GW, allow_small_or_imprecise_dtypes=True)
            pool.wait_ge(S("fill"), 1)
            pool.affine_select(out=ident, in_=ident, compare_op=ALU.not_equal, fill=1.0, base=0,
                               pattern=[[-1, P]], channel_multiplier=1)
            bd = blockdiag.rearrange("p (a c) -> p a c", c=HC)
            pool.affine_select(out=bd, in_=bd, compare_op=ALU.is_ge, fill=0.0, base=0,
                               pattern=[[-HC, 4], [0, HC]], channel_multiplier=1).then_inc(S("fill"), 1)
            pool.wait_ge(S("fill"), 2)
            pool.affine_select(out=bd, in_=bd, compare_op=ALU.is_ge, fill=0.0, base=HC - 1,
                               pattern=[[HC, 4], [0, HC]], channel_multiplier=-1)
            pool.affine_select(out=below, in_=below, compare_op=ALU.is_gt, fill=0.0, base=0,
                               pattern=[[1, P]], channel_multiplier=-1).then_inc(S("consts"), 1)
            pool.wait_ge(S("widx"), 1)
            for b in range(2):
                for tab, dst in ((I["srcw"], win_s), (I["dstw"], win_d)):
                    pool.indirect_dma_start(out=dst[0:GB, b, :], out_offset=None, in_=tab,
                                            in_offset=bass.IndirectOffsetOnAxis(ap=widx[0:GB, b:b + 1], axis=0)).then_inc(S("win_in"), 16)
            pool.wait_ge(S("w_in"), 128)
            for l in range(3):
                pool.tensor_tensor(stg[:, l, 0:2], stg[:, l, 0:2], stg[:, l, 2:4], ALU.subtract).then_inc(S("wd"), 1)
            pool.wait_ge(S("xn"), 1)
            pool.tensor_tensor(acc, acc, xn, ALU.add).then_inc(S("acc"), 1)
            pool.wait_ge(S("bias_in"), 16 * BIAS_DMAS)
            pool.tensor_tensor(bout[:, 0], bout[:, 0], bout[:, 1], ALU.add).then_inc(S("acc"), 1)
            pool.wait_ge(S("acc"), 2)
            pool.tensor_tensor(acc, acc, bout[:, 0:1, :].to_broadcast([P, NT, D]), ALU.add).then_inc(S("acc"), 1)
            for b in range(NT // 4):
                pool.wait_ge(S("kn"), b + 1)
                for t in range(4):
                    k3 = kv_n[:, t, 0:256].rearrange("p (h c) -> p h c", c=HC)
                    ins = pool.tensor_tensor(k3, k3, gbkv[:, 0:1, :].to_broadcast([P, HEADS, HC]), ALU.mult)
                ins.then_inc(S("kg"), 1)
                pool.wait_ge(S("kg"), b + 1)
                for t in range(4):
                    k3 = kv_n[:, t, 0:256].rearrange("p (h c) -> p h c", c=HC)
                    ins = pool.tensor_tensor(k3, k3, gbkv[:, 1:2, :].to_broadcast([P, HEADS, HC]), ALU.add)
                ins.then_inc(S("k_ready"), 1)
            barrier(pool)
            barrier(pool)
            with pool.Fori(0, 3) as l:
                for c in range(NC):
                    for f in range(2):
                        pool.wait_ge(S("own"), 2 * NC * l + 2 * c + f + 1)
                        pool.tensor_tensor(tmp_p[:, f], tmp_p[:, f], has[:, c * 512:(c + 1) * 512], ALU.mult).then_inc(S("own_has"), 1)
            barrier(pool)
            pool.iota(blk, [[1, NB]], base=0, channel_multiplier=0, allow_small_or_imprecise_dtypes=True)
            pool.iota(valid, [[0, 1]], base=0, channel_multiplier=1, allow_small_or_imprecise_dtypes=True).then_inc(S("blk"), 1)
            pool.wait_ge(S("slots"), 1)
            pool.wait_ge(S("slots_zero"), 16)
            for t in range(NT):
                n = P if t < NT - 1 else LAST
                pool.wait_ge(S("xn2"), t + 1)
                for q in range(TOPK):
                    pool.indirect_dma_start(out=xslots, out_offset=bass.IndirectOffsetOnAxis(ap=slot[0:n, q, t:t + 1], axis=0),
                                            in_=xn2[0:n, t, :], in_offset=None).then_inc(S("scattered"), 16)
            pool.wait_ge(S("scattered"), 16 * NT * TOPK)
            barrier(pool)

            def store(b, u):
                pool.wait_ge(S("e_out"), b + 3)
                pool.dma_start(yslots[bass.ds(b * P, P), :], y_out[:, u]).then_inc(S(f"e_y{u}"), 16)

            with pool.Fori(0, NPAIR) as bb:
                for u in range(2):
                    store(2 * bb + u, u)
            store(NB - 1, 0)
            pool.wait_ge(S("e_y0"), 16 * (NPAIR + 1))
            pool.wait_ge(S("e_y1"), 16 * NPAIR)
            barrier(pool)
            for t in range(NT):
                n = P if t < NT - 1 else LAST
                for q, y_ in enumerate((y1, y2)):
                    pool.indirect_dma_start(out=y_[0:n, t, :], out_offset=None, in_=yslots,
                                            in_offset=bass.IndirectOffsetOnAxis(ap=slot[0:n, q, t:t + 1], axis=0)).then_inc(S(f"y_in{t // 2}"), 16)

        @block.vector
        def _(v):
            steps = [0]

            def step(ins):
                steps[0] += 1
                ins.then_inc(S("v_step"), 1)
                v.wait_ge(S("v_step"), steps[0])

            v.memset(acc[:, NT - 1, :], 0.0).then_inc(S("pad0"), 1)
            v.wait_ge(S("samp_in"), 16)
            step(v.tensor_copy(samp, samp_i))
            v.wait_ge(S("consts"), 1)
            for c in range(NS):
                ins = v.tensor_scalar(lt[:, c, :], bounds, samp[:, c:c + 1], None, ALU.is_gt)
            ins.then_inc(S("lt"), 1)
            v.wait_ge(S("pair_in"), 16)
            step(v.tensor_tensor(cmp, pair[:, 0:EC], pair[:, 1:EC + 1], ALU.is_gt))
            step(v.tensor_reduce(viol, cmp, AX_X, ALU.add))
            v.wait_ge(S("counted"), 1)
            step(v.tensor_copy(cnts[0:GB, :], ps[0:GB, 0, 0:4]))
            step(v.tensor_scalar(cnts[0:GB, 0:2], cnts[0:GB, 0:2], -1.0, 0.0, ALU.add, ALU.max))
            v.tensor_copy(widx[0:GB, :], cnts[0:GB, 0:2]).then_inc(S("widx"), 1)
            step(v.tensor_tensor(excess[0:GB, :], cnts[0:GB, 2:4], cnts[0:GB, 0:2], ALU.subtract))
            v.tensor_scalar(excess[0:GB, :], excess[0:GB, :], float(WIN // STEP), None, ALU.is_gt).then_inc(S("excess"), 1)
            v.wait_ge(S("badsum"), 1)
            v.tensor_copy(bad[0:1, :], ps[0:1, 1, 0:1]).then_inc(S("bad"), 1)

            v.wait_ge(S("x_in"), 32)
            for t in range(NT):
                ins = v.bn_stats(st6[:, t, :], acc[:, t, :])
            step(ins)
            for t in range(NT):
                ins = v.bn_aggr(mv[:, t, :], st6[:, t, :])
            ins.then_inc(S("stats"), 1)
            v.wait_ge(S("std"), 1)
            step(v.reciprocal(rstd, std))
            for t in range(NT):
                ins = v.tensor_scalar(xn[:, t, :], acc[:, t, :], mv[:, t, 0:1], rstd[:, t:t + 1], ALU.subtract, ALU.mult)
            ins.then_inc(S("xn"), 1)
            v.wait_ge(S("wqkv_in"), 16)
            v.wait_ge(S("bias_in"), 16 * BIAS_DMAS)
            for k in range(KD):
                v.tensor_reduce(msum[:, k].rearrange("p (s h) -> p h s", s=2),
                                wqkv[:, k].rearrange("p (h s c) -> p h s c", s=3, c=HC)[:, :, 1:3, :], AX_X, ALU.add)
            step(v.tensor_reduce(bsum, bkv.rearrange("p (s c) -> p s c", c=HC), AX_X, ALU.add))
            v.tensor_scalar(msum, msum, 1.0 / HC, None, ALU.mult)
            step(v.tensor_scalar(bsum, bsum, 1.0 / HC, None, ALU.mult))
            for k in range(KD):
                for s_ in range(2):
                    v.tensor_tensor(wkvc[:, k, s_ * 256:(s_ + 1) * 256].rearrange("p (h c) -> p h c", c=HC),
                                    wqkv[:, k].rearrange("p (h s c) -> p h s c", s=3, c=HC)[:, :, 1 + s_, :],
                                    msum[:, k, 8 * s_:8 * s_ + 8].rearrange("p (h o) -> p h o", o=1).to_broadcast([P, HEADS, HC]), ALU.subtract)
                v.tensor_copy(heads(wq[:, k], 0), wqkv[:, k].rearrange("p (h s c) -> p h s c", s=3, c=HC)[:, :, 0, :])
            v.tensor_tensor(bias_kv.rearrange("p (s c) -> p s c", c=HC), bkv.rearrange("p (s c) -> p s c", c=HC),
                            bsum.rearrange("p (s o) -> p s o", o=1).to_broadcast([P, 16, HC]), ALU.subtract).then_inc(S("wkvc"), 1)
            for i, (hi, lo, raw) in enumerate(HALF_LIST):
                v.wait_ge(S("w_hi"), i + 1)
                ins = v.scalar_tensor_tensor(lo, raw, WS, hi, ALU.mult, ALU.subtract)
            ins.then_inc(S("w_lo"), 1)
            for i in range(2 * NC):
                k, c = divmod(i, NC)
                v.wait_ge(S("xt_hi"), i + 1)
                v.tensor_tensor(ht_lo[:, k, c * 512:(c + 1) * 512], ps[:, 2 + i % 2, :],
                                ht_hi[:, k, c * 512:(c + 1) * 512], ALU.subtract).then_inc(S("xt_lo"), 1)
            v.wait_ge(S("colsT"), 1)
            step(v.tensor_copy(cols, ps[:, 0, 0:P]))
            v.wait_ge(S("wqT"), 1)
            for G in range(KD):
                v.tensor_copy(wqT[:, G, 0:D], ps[:, 1, G * D:(G + 1) * D])
                ins = v.tensor_copy(wqT[:, G, D:D + 1], cols[:, 104 + G:105 + G])
            ins.then_inc(S("wqT_in"), 1)
            for b in range(NT // 4):
                v.wait_ge(S("kv"), b + 1)
                if b:
                    v.wait_ge(S("kn"), b)
                for t in range(4):
                    ins = v.scalar_tensor_tensor(kv_z[:, t], ps[:, t, :], 1.0 / WS, bias_kv, ALU.mult, ALU.add)
                ins.then_inc(S("kv_z"), 1)
                v.wait_ge(S("kv_sq"), b + 1)
                v.tensor_reduce(kst, kv_sq.rearrange("p t (s c) -> p (t s) c", c=HC), AX_X, ALU.add).then_inc(S("kv_var"), 1)
                v.wait_ge(S("kv_std"), b + 1)
                step(v.reciprocal(kst2, kst))
                if b:
                    v.wait_ge(S("kv_used"), b)
                v.tensor_tensor(kv_n.rearrange("p t (s c) -> p (t s) c", c=HC), kv_z.rearrange("p t (s c) -> p (t s) c", c=HC),
                                kst2.rearrange("p t (s o) -> p (t s) o", o=1).to_broadcast([P, 64, HC]), ALU.mult).then_inc(S("kn"), 1)
            v.wait_ge(S("kv_used"), NT // 4)
            for G in range(KD):
                v.tensor_copy(sk[:, G:G + 1], ps[:, 6 + G, 0:1])
                ins = v.tensor_tensor(kvt[:, G].rearrange("p (a c) -> p a c", c=HC), ps[:, 4 + G, 0:P].rearrange("p (a c) -> p a c", c=HC),
                                      gbkv[:, 2:3, :].to_broadcast([P, 4, HC]), ALU.mult)
            step(ins)
            for G in range(KD):
                ins = v.scalar_tensor_tensor(kvt[:, G].rearrange("p (a c) -> p a c", c=HC), gbkv[:, 3:4, :].to_broadcast([P, 4, HC]),
                                             sk[:, G:G + 1], kvt[:, G].rearrange("p (a c) -> p a c", c=HC), ALU.mult, ALU.add)
            step(ins)
            v.tensor_tensor(kvm, kvt, blockdiag.rearrange("p (o c) -> p o c", o=1).to_broadcast([P, KD, P]), ALU.mult).then_inc(S("kvm"), 1)
            v.wait_ge(S("mT"), 1)
            for G in range(KD):
                v.tensor_copy(retb[:, G:G + 1], ps[:, 2 + G, D:D + 1])
                ins = v.tensor_copy(mT[:, G, :], ps[:, 2 + G, 0:D + 1])
            step(ins)
            for G in range(KD):
                ins = v.tensor_tensor(mT[:, G, G * P:(G + 1) * P], mT[:, G, G * P:(G + 1) * P], ident, ALU.add)
            ins.then_inc(S("mT_in"), 1)
            v.wait_ge(S("m1_hi"), 1)
            v.scalar_tensor_tensor(m1_lo, ps[:, 0, :].rearrange("p (k d) -> p k d", k=KD), WS, m1_hi, ALU.mult, ALU.subtract)
            v.tensor_tensor(b1p, ps[:, 1, 0:KD], cols[:, 102:104], ALU.add).then_inc(S("m1_lo"), 1)
            for i in range(2 * NC):
                c, f = divmod(i, 2)
                v.wait_ge(S("h1_hi"), i + 1)
                v.tensor_tensor(h1_lo[:, f, c * 512:(c + 1) * 512], h1f[:, f], h1_hi[:, f, c * 512:(c + 1) * 512], ALU.subtract).then_inc(S("h1_lo"), 1)
            v.wait_ge(S("acc"), 3)
            for t in range(NT):
                v.wait_ge(S("mix_out"), t + 1)
                v.scalar_tensor_tensor(acc[:, t], ps[:, 6 + t % 2, 0:D], 1.0 / WS, acc[:, t], ALU.mult, ALU.add).then_inc(S("mix_acc"), 1)
            v.wait_ge(S("win_in"), 64)
            g = slice(0, GB)
            v.tensor_scalar(ki[g], win_s[g], 7, 4, ALU.logical_shift_right, ALU.logical_shift_left)
            for b in range(2):
                v.tensor_scalar(ka[g, b], win_d[g, b], grp[g, b:b + 1], None, ALU.add)
            step(v.tensor_scalar(win_s[g], win_s[g], 127, None, ALU.bitwise_and))
            v.tensor_scalar(kb[g], ka[g], 0.0, None, ALU.is_ge)
            v.tensor_copy(klo[g], win_s[g])
            step(v.tensor_tensor(kc[g], ki[g], ka[g], ALU.add))
            step(v.scalar_tensor_tensor(ka[g], ka[g], float(GW), kb[g], ALU.is_lt, ALU.mult))
            v.scalar_tensor_tensor(kc[g], kc[g], 1.0, ka[g], ALU.add, ALU.mult).then_inc(S("keys"), 1)
            v.wait_ge(S("keysT"), 1)
            v.tensor_copy(key_t, ps[:, 4, 0:3 * NG].rearrange("p (j g) -> p j g", j=3))
            v.tensor_copy(lo_t, ps[:, 5, 0:3 * NG].rearrange("p (j g) -> p j g", j=3)).then_inc(S("keycols"), 1)
            barrier(v)
            v.wait_ge(S("keycols"), 1)
            with v.If(unsorted(v) > 0):
                v.memset(at, 0.0)
                v.tensor_copy(ident16, ident).then_inc(S("any_zero"), 1)
                v.sem_inc(S("any_read"), 1)
                v.sem_inc(S("any_out"), 1)
                with v.Fori(0, PASSES) as q:
                    v.wait_ge(S("any_in"), 32 * (q + 1))
                    v.wait_ge(S("any_out"), NG * q + 1)
                    v.tensor_scalar(any_i[g], any_s[g], 7, 4, ALU.logical_shift_right, ALU.logical_shift_left)
                    for b in range(2):
                        v.tensor_scalar(any_a[g, b], any_d[g], grp[g, b:b + 1], None, ALU.add)
                    v.tensor_scalar(any_s[g], any_s[g], 127, None, ALU.bitwise_and).then_inc(S("any_step"), 1)
                    v.wait_ge(S("any_step"), 4 * q + 1)
                    v.tensor_copy(any_k[g], any_i[g])
                    v.tensor_copy(any_lo[g], any_s[g]).then_inc(S("any_read"), 1)
                    v.tensor_scalar(any_b[g], any_a[g], 0.0, None, ALU.is_ge).then_inc(S("any_step"), 1)
                    v.wait_ge(S("any_step"), 4 * q + 2)
                    v.tensor_tensor(any_c[g], any_a[g], any_k[g].rearrange("p (o w) -> p o w", o=1).to_broadcast([GB, 2, WIN]), ALU.add).then_inc(S("any_step"), 1)
                    v.wait_ge(S("any_step"), 4 * q + 3)
                    v.scalar_tensor_tensor(any_a[g], any_a[g], float(GW), any_b[g], ALU.is_lt, ALU.mult).then_inc(S("any_step"), 1)
                    v.wait_ge(S("any_step"), 4 * q + 4)
                    v.scalar_tensor_tensor(any_c[g], any_c[g], 1.0, any_a[g], ALU.add, ALU.mult).then_inc(S("any_keys"), 1)
                    v.wait_ge(S("any_keysT"), q + 1)
                    v.tensor_copy(key_t, ps[:, 4, 0:3 * NG].rearrange("p (j g) -> p j g", j=3))
                    v.tensor_copy(lo_t, ps[:, 5, 0:3 * NG].rearrange("p (j g) -> p j g", j=3)).then_inc(S("any_cols"), 1)
                    with v.Fori(0, NG) as gi:
                        v.wait_ge(S("any_cols"), q + 1)
                        v.wait_ge(S("any_out"), NG * q + gi + 1)
                        for j in range(3):
                            v.tensor_scalar(src_hot[:, 0, j, :], iota_p, lo_t[:, j, bass.ds(gi, 1)], None, ALU.is_equal)
                            ins = v.tensor_scalar(key_hot[:, 0, j, :], iota_key, key_t[:, j, bass.ds(gi, 1)], None, ALU.is_equal)
                        ins.then_inc(S("any_hot"), 1)
            with v.Else():
                with v.Fori(0, NG // 2) as gg:
                    for u in range(2):
                        gi = 2 * gg + u
                        v.wait_ge(S("grp_free"), gi + 1)
                        for j in range(3):
                            v.tensor_scalar(src_hot[:, u, j, :], iota_p, lo_t[:, j, bass.ds(gi, 1)], None, ALU.is_equal)
                            ins = v.tensor_scalar(key_hot[:, u, j, :], iota_key, key_t[:, j, bass.ds(gi, 1)], None, ALU.is_equal)
                        ins.then_inc(S("hot"), 1)
            v.nop()
            v.sem_inc(S("g_lo"), 2)
            v.sem_inc(S("f3_acc"), 2)
            v.sem_inc(S("h_lo"), 4)
            v.sem_inc(S("pre"), 2)
            barrier(v)
            for c in range(NC):
                v.wait_ge(S("deg"), c + 1)
                v.tensor_scalar(has[:, c * 512:(c + 1) * 512], ps[:, c, :], 1.0, None, ALU.min)
                ins = v.tensor_scalar(rcnt[:, c * 512:(c + 1) * 512], ps[:, c, :], 1.0, None, ALU.max)
            step(ins)
            v.reciprocal(rcnt, rcnt).then_inc(S("rcnt"), 1)
            v.wait_ge(S("rcnt"), 1)
            for l in range(3):
                with v.Fori(0, NT // 2) as tt:
                    for u in range(2):
                        t = 2 * tt + u
                        v.wait_ge(S("g_hi"), NT * l + t + 1)
                        v.scalar_tensor_tensor(g_lo[:, bass.ds(t, 1), :], ps[:, u:u + 1, 0:D], 1.0 / WS, g_hi[:, bass.ds(t, 1), :], ALU.mult, ALU.subtract)
                        v.scalar_tensor_tensor(acc[:, bass.ds(t, 1), :], ps[:, u:u + 1, D:2 * D], 1.0 / WS, acc[:, bass.ds(t, 1), :], ALU.mult, ALU.add).then_inc(S("g_lo"), 1)
                with v.Fori(0, NC) as c:
                    for f in range(2):
                        i = 2 * NC * l + 2 * c + f
                        v.wait_ge(S("agg"), NC * l + c + 1)
                        v.wait_ge(S("h_lo"), i + 3)
                        v.tensor_tensor(tmp_t[:, f:f + 1], ps[:, bass.ds(2 * (c % 2) + f, 1), :],
                                        rcnt.rearrange("p (o n) -> p o n", o=1)[:, :, bass.ds(c * 512, 512)], ALU.mult).then_inc(S("mean"), 1)
                        v.wait_ge(S("mean"), i + 1)
                        v.wait_ge(S("own_has"), i + 1)
                        v.tensor_tensor(tmp_t[:, f], tmp_t[:, f], tmp_p[:, f], ALU.add).then_inc(S("pre"), 1)
                        v.wait_ge(S("h_hi"), i + 1)
                        v.scalar_tensor_tensor(ht_lo[:, f, bass.ds(c * 512, 512)], tmp_t[:, f], 0.0,
                                               ht_hi[:, f, bass.ds(c * 512, 512)], ALU.max, ALU.subtract).then_inc(S("h_lo"), 1)
            for t in range(NT + 2):
                if t < NT:
                    v.wait_ge(S("f3"), t + 1)
                    v.scalar_tensor_tensor(acc[:, t], ps[:, t % 2, 0:D], 1.0 / WS, acc[:, t], ALU.mult, ALU.add).then_inc(S("f3_acc"), 1)
                if 1 <= t <= NT:
                    v.wait_ge(S("f3_acc"), t + 2)
                    v.bn_stats(st6[:, t - 1, :], acc[:, t - 1, :]).then_inc(S("bn1"), 1)
                if t >= 2:
                    v.wait_ge(S("bn1"), t - 1)
                    ins = v.bn_aggr(mv[:, t - 2, :], st6[:, t - 2, :])
            ins.then_inc(S("stats"), 1)
            barrier(v)

            v.wait_ge(S("std"), 2)
            step(v.reciprocal(rstd, std))
            for t in range(NT):
                v.tensor_scalar(xn2[:, t, :], acc[:, t, :], mv[:, t, 0:1], rstd[:, t:t + 1], ALU.subtract, ALU.mult).then_inc(S("y"), 1)
            for t in range(NT):
                v.wait_ge(S("y"), t + 1)
                v.bn_stats(st6[:, t, :], xn2[:, t, :]).then_inc(S("bn2"), 1)
            v.wait_ge(S("bn2"), NT)
            v.wait_ge(S("y"), NT)
            for t in range(NT):
                ins = v.bn_aggr(mv[:, t, :], st6[:, t, :])
            ins.then_inc(S("stats"), 1)
            v.wait_ge(S("std"), 3)
            step(v.reciprocal(rstd, std))
            v.scalar_tensor_tensor(nmr, mv[:, :, 0], -1.0, rstd, ALU.mult, ALU.mult).then_inc(S("nmr"), 1)
            v.wait_ge(S("logits"), NT)
            v.wait_ge(S("wr_in"), 32)
            step(v.tensor_tensor(logit, ps[:, 2, 0:NT * NE].rearrange("p (t e) -> p t e", e=NE),
                                 br.rearrange("p (o e) -> p o e", o=1).to_broadcast([P, NT, NE]), ALU.add))
            for t in range(NT):
                ins = v.max(mx[:, t, :], logit[:, t, :])
            step(ins)
            for t in range(NT):
                ins = v.max_index(top[:, t, :], mx[:, t, :], logit[:, t, :])
            step(ins)
            v.tensor_copy(topf, top[:, :, 0:2])
            v.wait_ge(S("blk"), 1)
            v.tensor_scalar(valid, valid, float(LAST), None, ALU.is_lt)
            step(v.tensor_tensor(wgt[:, 1], mx[:, :, 1], mx[:, :, 0], ALU.subtract))
            for q, hot in enumerate((hot1, hot2)):
                ins = v.tensor_tensor(hot, iota8.rearrange("p (o e) -> p o e", o=1).to_broadcast([P, NT, NE]),
                                      topf[:, :, q:q + 1].to_broadcast([P, NT, NE]), ALU.is_equal)
            ins.then_inc(S("diff"), 1)
            v.wait_ge(S("diff"), 1)
            step(v.tensor_tensor(hot12, hot1, hot2, ALU.add))
            v.tensor_scalar(hot12[:, NT - 1], hot12[:, NT - 1], valid, None, ALU.mult).then_inc(S("hot12"), 1)
            v.wait_ge(S("ranks"), 1)
            totals = ps[:, 4, 0:NT * NE].rearrange("p (t e) -> p t e", e=NE)
            step(v.tensor_copy(tot_a, totals))
            src, dst = tot_a, tot_b
            s_ = 1
            while s_ < NT:
                v.tensor_tensor(dst[:, s_:NT], src[:, s_:NT], src[:, 0:NT - s_], ALU.add)
                step(v.tensor_copy(dst[:, 0:s_], src[:, 0:s_]))
                src, dst = dst, src
                s_ *= 2
            v.tensor_tensor(rank, src, totals, ALU.subtract)
            step(v.tensor_scalar(nblk_i, src[:, NT - 1], float(P - 1), None, ALU.add))
            step(v.tensor_tensor(rank, rank, ps[:, 3, 0:NT * NE].rearrange("p (t e) -> p t e", e=NE), ALU.add))
            step(v.tensor_scalar(nblk_i, nblk_i, 7, None, ALU.logical_shift_right))
            step(v.tensor_copy(nblk, nblk_i))
            step(v.tensor_copy(cum, nblk))
            cs, cd = cum, cum2
            for s_ in (1, 2, 4):
                v.tensor_tensor(cd[:, s_:NE], cs[:, s_:NE], cs[:, 0:NE - s_], ALU.add)
                step(v.tensor_copy(cd[:, 0:s_], cs[:, 0:s_]))
                cs, cd = cd, cs
            step(v.tensor_tensor(base, cs, nblk, ALU.subtract))
            step(v.tensor_scalar(base, base, float(P), None, ALU.mult))
            step(v.tensor_tensor(rank, rank, base.rearrange("p (o e) -> p o e", o=1).to_broadcast([P, NT, NE]), ALU.add))
            v.tensor_tensor(hot1, hot1, rank, ALU.mult)
            step(v.tensor_tensor(hot2, hot2, rank, ALU.mult))
            v.tensor_reduce(slot_f[:, 0], hot1, AX_X, ALU.add)
            step(v.tensor_reduce(slot_f[:, 1], hot2, AX_X, ALU.add))
            v.tensor_copy(slot, slot_f).then_inc(S("slots"), 1)
            step(v.tensor_tensor(blk_ge, blk.rearrange("p (b o) -> p b o", o=1).to_broadcast([P, NB, NE]),
                                 cs.rearrange("p (o e) -> p o e", o=1).to_broadcast([P, NB, NE]), ALU.is_ge))
            step(v.tensor_reduce(blk, blk_ge, AX_X, ALU.add))
            v.tensor_scalar(blk_e, blk, float(NE - 1), None, ALU.min).then_inc(S("blk_e"), 1)
            v.wait_ge(S("blk_e"), 1)
            v.wait_ge(S("wexp"), 1)
            step(v.tensor_scalar(wgt[:, 0], wgt[:, 1], 1.0, None, ALU.add))
            step(v.reciprocal(wgt[:, 0], wgt[:, 0]))
            step(v.tensor_tensor(wgt[:, 1], wgt[:, 1], wgt[:, 0], ALU.mult))
            for i in range(2 * NE):
                e, w = divmod(i, 2)
                v.wait_ge(S("ew_hi"), i + 1)
                if i:
                    v.wait_ge(S("ew_lo"), i)
                v.scalar_tensor_tensor(w_e[e][2 * w + 1].rearrange("p k n -> p (k n)"), ew_raw[i], WS,
                                       w_e[e][2 * w].rearrange("p k n -> p (k n)"), ALU.mult, ALU.subtract).then_inc(S("ew_lo"), 1)
            v.sem_inc(S("e_xe"), 2)
            v.sem_inc(S("e_lo"), 2)
            v.sem_inc(S("e_out"), 2)
            barrier(v)

            def widen(b, u):
                e = v.value_load(blk_e[0:1, bass.ds(b, 1)], min_val=0, max_val=NE - 1)
                v.wait_ge(S("e_turned"), b + 3)
                v.wait_ge(S("e_h"), b + 1)
                v.wait_ge(S("e_xe"), b + 2)
                for k in range(KD):
                    gcol, bcol = cols[:, bass.ds(64 + KD * e + k, 1)], cols[:, bass.ds(80 + KD * e + k, 1)]
                    ins = v.tensor_scalar(xe[:, k], ps[:, 4 + u, k * P:(k + 1) * P], gcol, bcol, ALU.mult, ALU.add)
                ins.then_inc(S("e_xf"), 1)
                v.wait_ge(S("e_xf"), b + 1)
                v.tensor_copy(xe_hi[:, u], xe).then_inc(S("e_xw"), 1)
                v.wait_ge(S("e_xw"), b + 1)
                v.tensor_tensor(xe_lo[:, u], xe, xe_hi[:, u], ALU.subtract).then_inc(S("e_xe"), 1)

            def fetch(b, u):
                e = v.value_load(blk_e[0:1, bass.ds(b, 1)], min_val=0, max_val=NE - 1)
                v.wait_ge(S("e_h"), b + 1)
                v.tensor_copy(w1_now[:, u].rearrange("p s k h -> p (s k h)"), mem[:, bass.ds(e * EWN + W1_HI, 2 * KD * H)]).then_inc(S("e_w1"), 1)

            def low(b, u):
                v.wait_ge(S("e_hi"), b + 1)
                v.tensor_tensor(h_lo[:, u], hf[:, u], h_hi[:, u], ALU.subtract).then_inc(S("e_lo"), 1)

            def result(b, bb, u):
                e = v.value_load(blk_e[0:1, bass.ds(b, 1)], min_val=0, max_val=NE - 1)
                v.wait_ge(S("e_yp"), b + 3)
                if bb is not None:
                    v.wait_ge(S(f"e_y{u}"), 16 * bb)
                v.scalar_tensor_tensor(y_out[:, u:u + 1], ps[:, 6 + u:7 + u, 0:D], 1.0 / WS, b2_all[:, bass.ds(e, 1), :], ALU.mult, ALU.add).then_inc(S("e_out"), 1)

            v.wait_ge(S("b2_in"), 16)
            widen(0, 0)
            fetch(0, 0)
            widen(1, 1)
            fetch(1, 1)
            low(0, 0)

            def two_blocks(bb, stores):
                fetch(2 * bb + 2, 0)
                widen(2 * bb + 2, 0)
                low(2 * bb + 1, 1)
                result(2 * bb, stores, 0)
                fetch(2 * bb + 3, 1)
                widen(2 * bb + 3, 1)
                low(2 * bb + 2, 0)
                result(2 * bb + 1, stores, 1)

            two_blocks(0, None)
            with v.Fori(1, NPAIR - 1) as bb:
                two_blocks(bb, bb)
            widen(NB - 1, 0)
            fetch(NB - 1, 0)
            low(NB - 2, 1)
            result(NB - 3, NPAIR - 1, 0)
            low(NB - 1, 0)
            result(NB - 2, NPAIR - 1, 1)
            result(NB - 1, NPAIR, 0)
            barrier(v)
            for t in range(NT):
                n = P if t < NT - 1 else LAST
                v.wait_ge(S(f"y_in{t // 2}"), 32 * TOPK)
                step(v.scalar_tensor_tensor(acc[0:n, t], y1[0:n, t], wgt[0:n, 0, t:t + 1], acc[0:n, t], ALU.mult, ALU.add))
                v.scalar_tensor_tensor(acc[0:n, t], y2[0:n, t], wgt[0:n, 1, t:t + 1], acc[0:n, t], ALU.mult, ALU.add).then_inc(S("final"), 1)

        @block.scalar
        def _(a):
            a.wait_ge(S("consts"), 1)
            rows = [(I["L0_ffn_b1"].rearrange("e (j p) -> (e j) p", p=P), 0, NE * KH),
                    (I["L0_ffn_ln_g"].rearrange("e (j p) -> (e j) p", p=P), 64, NE * KD),
                    (I["L0_ffn_ln_b"].rearrange("e (j p) -> (e j) p", p=P), 80, NE * KD),
                    (I["L0_gnn_b0"].rearrange("(j p) -> j p", p=P), 96, KD), (I["L0_gnn_b1"].rearrange("(j p) -> j p", p=P), 98, KD),
                    (I["L0_gnn_b2"].rearrange("(j p) -> j p", p=P), 100, KD), (I["L0_mix_b1"].rearrange("(j p) -> j p", p=P), 102, KD)]
            for src, r, n in rows:
                a.dma_start(stack[r:r + n, :], src).then_inc(S("rows_in"), 16)
            bq = I["L0_mix_b_qkv"].rearrange("(h s c) -> s h c", s=3, c=HC)
            for G in range(KD):
                a.dma_start(stack[104 + G:105 + G, :].rearrange("o (h c) -> o h c", c=HC), bq[0:1, 4 * G:4 * G + 4, :]).then_inc(S("rows_in"), 16)
            for s_ in range(2):
                a.dma_start(bkv[:, s_ * 256:(s_ + 1) * 256].rearrange("p (h c) -> p h c", c=HC), bq[1 + s_:2 + s_, :, :].to_broadcast([P, HEADS, HC])).then_inc(S("bias_in"), 16)
            for i, n in enumerate(("kln_g", "kln_b", "vln_g", "vln_b")):
                a.dma_start(gbkv[:, i], I[f"L0_mix_{n}"].partition_broadcast(P)).then_inc(S("bias_in"), 16)
            a.dma_start(bout[:, 0], I["L0_gnn_bf"].partition_broadcast(P)).then_inc(S("bias_in"), 16)
            a.dma_start(bout[:, 1], I["L0_mix_b2"].partition_broadcast(P)).then_inc(S("bias_in"), 16)

            a.wait_ge(S("stats"), 1)
            a.activation(std, mv[:, :, 1], ACT.Sqrt, bias=eps[:, 0:1]).then_inc(S("std"), 1)
            a.wait_ge(S("w_in"), 128)
            for i, (hi, lo, raw) in enumerate(HALF_LIST):
                if i < 3:
                    a.wait_ge(S("wd"), i + 1)
                if i == NSPLIT - 1:
                    a.wait_ge(S("wkvc"), 1)
                a.activation(hi, raw, ACT.Copy, scale=WS).then_inc(S("w_hi"), 1)
            for i in range(2 * NC):
                k, c = divmod(i, NC)
                a.wait_ge(S("xt"), i + 1)
                a.activation(ht_hi[:, k, c * 512:(c + 1) * 512], ps[:, 2 + i % 2, :], ACT.Copy).then_inc(S("xt_hi"), 1)
            for b in range(NT // 4):
                a.wait_ge(S("kv_z"), b + 1)
                if b:
                    a.wait_ge(S("kv_var"), b)
                a.activation(kv_sq, kv_z, ACT.Square).then_inc(S("kv_sq"), 1)
                a.wait_ge(S("kv_var"), b + 1)
                a.activation(kst, kst, ACT.Sqrt, bias=eps[:, 0:1], scale=1.0 / HC).then_inc(S("kv_std"), 1)
            a.wait_ge(S("m1"), 1)
            a.activation(m1_hi, ps[:, 0, :].rearrange("p (k d) -> p k d", k=KD), ACT.Copy, scale=WS).then_inc(S("m1_hi"), 1)
            a.wait_ge(S("m1_lo"), 1)
            for i in range(2 * NC):
                c, f = divmod(i, 2)
                a.wait_ge(S("h1"), i + 1)
                if i >= 2:
                    a.wait_ge(S("h1_lo"), i - 1)
                a.activation(h1f[:, f], ps[:, 2 + i % 4, :], ACT.Gelu, bias=b1p[:, f:f + 1], scale=1.0 / WS).then_inc(S("h1f"), 1)
                a.wait_ge(S("h1f"), i + 1)
                a.activation(h1_hi[:, f, c * 512:(c + 1) * 512], h1f[:, f], ACT.Copy).then_inc(S("h1_hi"), 1)
            a.sem_inc(S("grp_free"), 2)
            barrier(a)
            with a.If(unsorted(a) > 0):
                with a.Fori(0, PASSES) as q:
                    with a.Fori(0, NG) as gi:
                        a.wait_ge(S("any_sum"), NG * q + gi + 1)
                        a.activation(at[:, :, bass.ds(GW * gi, GW)], ps[:, 0, 0:KEYS].rearrange("p (s d) -> p s d", d=GW),
                                     ACT.Copy).then_inc(S("any_out"), 1)
            with a.Else():
                with a.Fori(0, NG // 2) as gg:
                    for u in range(2):
                        gi = 2 * gg + u
                        a.wait_ge(S("grp_sum"), gi + 1)
                        a.activation(at[:, :, bass.ds(GW * gi, GW)], ps[:, u, 0:KEYS].rearrange("p (s d) -> p s d", d=GW),
                                     ACT.Copy).then_inc(S("grp_free"), 1)
            a.nop()
            barrier(a)
            for l in range(3):
                with a.Fori(0, NT // 2) as tt:
                    for u in range(2):
                        t = 2 * tt + u
                        a.wait_ge(S("g"), NT * l + t + 1)
                        a.activation(g_hi[:, bass.ds(t, 1), :], ps[:, u:u + 1, 0:D], ACT.Copy, scale=1.0 / WS).then_inc(S("g_hi"), 1)
                with a.Fori(0, NC) as c:
                    for f in range(2):
                        i = 2 * NC * l + 2 * c + f
                        a.wait_ge(S("agg"), NC * l + c + 1)
                        a.wait_ge(S("pre"), i + 1)
                        a.activation(tmp_p[:, f:f + 1], ps[:, bass.ds(4 + 2 * (c % 2) + f, 1), :], ACT.Identity,
                                     bias=cols[:, 96 + 2 * l + f:97 + 2 * l + f], scale=1.0 / WS).then_inc(S("own"), 1)
                    for f in range(2):
                        i = 2 * NC * l + 2 * c + f
                        a.wait_ge(S("pre"), i + 3)
                        a.activation(ht_hi[:, f, bass.ds(c * 512, 512)], tmp_t[:, f], ACT.Relu).then_inc(S("h_hi"), 1)
            barrier(a)

            a.wait_ge(S("stats"), 2)
            a.activation(std, mv[:, :, 1], ACT.Sqrt, bias=eps[:, 0:1]).then_inc(S("std"), 1)
            for t in range(NT):
                a.wait_ge(S("yT"), t + 1)
                if t >= 2:
                    a.wait_ge(S("logits"), t - 1)
                a.activation(yT[:, t % 2], ps[:, t % 2, 0:D].rearrange("p (k n) -> p k n", k=KD), ACT.Copy).then_inc(S("yT_in"), 1)
            a.wait_ge(S("stats"), 3)
            a.wait_ge(S("y"), NT)
            a.activation(std, mv[:, :, 1], ACT.Sqrt, bias=eps[:, 0:1]).then_inc(S("std"), 1)
            a.wait_ge(S("nmr"), 1)
            for t in range(NT):
                a.activation(xn2[:, t, :], xn2[:, t, :], ACT.Identity, bias=nmr[:, t:t + 1], scale=rstd[:, t:t + 1]).then_inc(S("xn2"), 1)
            a.wait_ge(S("diff"), 1)
            a.activation(wgt[:, 1], wgt[:, 1], ACT.Exp).then_inc(S("wexp"), 1)
            for i in range(2 * NE):
                e, w = divmod(i, 2)
                a.wait_ge(S(f"ew_in{e}"), 32)
                if i >= 2:
                    a.wait_ge(S("ew_lo"), i - 1)
                a.activation(w_e[e][2 * w].rearrange("p k n -> p (k n)"), ew_raw[i], ACT.Copy, scale=WS).then_inc(S("ew_hi"), 1)
            a.sem_inc(S("e_gelu"), 2)
            barrier(a)
            a.preload_act_table(ACT.Gelu)

            def gelu(b, u):
                e = a.value_load(blk_e[0:1, bass.ds(b, 1)], min_val=0, max_val=NE - 1)
                a.wait_ge(S("e_h"), b + 3)
                a.wait_ge(S("e_lo"), b + 1)
                for j in range(KH):
                    ins = a.activation(hf[:, u, j], ps[:, 2 * u + j // 4, (j % 4) * P:(j % 4 + 1) * P], ACT.Gelu,
                                       bias=cols[:, bass.ds(KH * e + j, 1)], scale=1.0 / WS)
                ins.then_inc(S("e_gelu"), 1)
                a.wait_ge(S("e_gelu"), b + 3)
                a.wait_ge(S("e_yp"), b + 1)
                a.activation(h_hi[:, u], hf[:, u], ACT.Copy).then_inc(S("e_hi"), 1)

            with a.Fori(0, NPAIR) as bb:
                gelu(2 * bb, 0)
                gelu(2 * bb + 1, 1)
            gelu(NB - 1, 0)
            barrier(a)

        @block.tensor
        def _(pe):
            def three(out_, w_hi, w_lo, x_hi, x_lo, first, last):
                pe.matmul(out_, w_hi, x_hi, start=first, stop=False)
                pe.matmul(out_, w_hi, x_lo, start=False, stop=False)
                return pe.matmul(out_, w_lo, x_hi, start=False, stop=last)

            pe.wait_ge(S("consts"), 1)
            pe.wait_ge(S("lt"), 1)
            for q, lo in enumerate((0, GB, 1, GB + 1)):
                for c in range(NS):
                    ins = pe.matmul(ps[0:GB, 0, q:q + 1], lt[:, c, lo:lo + GB], ones16[:, 0:1], start=c == 0, stop=c == NS - 1)
            ins.then_inc(S("counted"), 1)
            pe.wait_ge(S("excess"), 1)
            pe.matmul(ps[0:1, 1, 0:1], ones[0:GB, 0:1], excess[0:GB, 0:1], start=True, stop=False)
            pe.matmul(ps[0:1, 1, 0:1], ones[0:GB, 0:1], excess[0:GB, 1:2], start=False, stop=False)
            pe.matmul(ps[0:1, 1, 0:1], ones[:, 0:1], viol, start=False, stop=True).then_inc(S("badsum"), 1)
            pe.wait_ge(S("xn"), 1)
            for i in range(2 * NC):
                k, c = divmod(i, NC)
                if i >= 2:
                    pe.wait_ge(S("xt_lo"), i - 1)
                for q in range(4):
                    ins = pe.transpose(ps[:, 2 + i % 2, q * P:(q + 1) * P], xn[:, 4 * c + q, k * P:(k + 1) * P], ident)
                ins.then_inc(S("xt"), 1)
            pe.wait_ge(S("rows_in"), 16 * 9)
            pe.wait_ge(S("counted"), 1)
            pe.wait_ge(S("widx"), 1)
            pe.transpose(ps[:, 0, 0:P], stack, ident).then_inc(S("colsT"), 1)
            pe.wait_ge(S("wkvc"), 1)
            pe.wait_ge(S("bad"), 1)
            for G in range(KD):
                for k in range(KD):
                    ins = pe.transpose(ps[:, 1, G * D + k * P:G * D + (k + 1) * P], wq[:, k, G * P:(G + 1) * P], ident)
            ins.then_inc(S("wqT"), 1)
            pe.wait_ge(S("wqT_in"), 1)
            pe.wait_ge(S("xt_lo"), 2 * NC)
            pe.wait_ge(S("w_lo"), 1)
            for b in range(NT // 4 + 1):
                if b < NT // 4:
                    if b:
                        pe.wait_ge(S("kv_z"), b)
                    for t in range(4):
                        o = (4 * b + t) * P
                        for k in range(KD):
                            ins = three(ps[:, t, :], ht_hi[:, k, o:o + P], ht_lo[:, k, o:o + P], wkv_hi[:, k], wkv_lo[:, k], k == 0, k == KD - 1)
                    ins.then_inc(S("kv"), 1)
                if b:
                    pe.wait_ge(S("k_ready"), b)
                    for t in range(4):
                        n = P if 4 * (b - 1) + t < NT - 1 else LAST
                        first, last = b == 1 and t == 0, b == NT // 4 and t == 3
                        for G in range(KD):
                            kk = kv_n[0:n, t, G * P:(G + 1) * P]
                            pe.matmul(ps[:, 4 + G, 0:P], kk, kv_n[0:n, t, 256 + G * P:256 + (G + 1) * P], start=first, stop=last)
                            ins = pe.matmul(ps[:, 6 + G, 0:1], kk, ones[0:n, 0:1], start=first, stop=last)
                    ins.then_inc(S("kv_used"), 1)
            pe.wait_ge(S("kvm"), 1)
            for G in range(KD):
                ins = pe.matmul(ps[:, 2 + G, 0:D + 1], kvm[:, G], wqT[:, G], start=True, stop=True)
            ins.then_inc(S("mT"), 1)
            pe.wait_ge(S("mT_in"), 1)
            pe.wait_ge(S("w1_in"), 16)
            for k in range(KD):
                for G in range(KD):
                    pe.matmul(ps[:, 0, k * D:(k + 1) * D], mT[:, G, k * P:(k + 1) * P], w1[:, G], start=G == 0, stop=G == KD - 1)
            for j in range(KD):
                for G in range(KD):
                    ins = pe.matmul(ps[:, 1, j:j + 1], w1[:, G, j * P:(j + 1) * P], retb[:, G:G + 1], start=G == 0, stop=G == KD - 1)
            ins.then_inc(S("m1"), 1)
            pe.wait_ge(S("m1_lo"), 1)
            for i in range(2 * NC):
                c, f = divmod(i, 2)
                if i >= 4:
                    pe.wait_ge(S("h1f"), i - 3)
                for k in range(KD):
                    fs, cs = slice(f * P, (f + 1) * P), slice(c * 512, (c + 1) * 512)
                    ins = three(ps[:, 2 + i % 4, :], m1_hi[:, k, fs], m1_lo[:, k, fs], ht_hi[:, k, cs], ht_lo[:, k, cs], k == 0, k == KD - 1)
                ins.then_inc(S("h1"), 1)
            pe.wait_ge(S("h1_lo"), 2 * NC)
            for t in range(NT):
                if t >= 2:
                    pe.wait_ge(S("mix_acc"), t - 1)
                for k in range(KD):
                    n = slice(t * P, (t + 1) * P)
                    ins = three(ps[:, 6 + t % 2, 0:D], h1_hi[:, k, n], h1_lo[:, k, n], w2_hi[:, k], w2_lo[:, k], k == 0, k == KD - 1)
                ins.then_inc(S("mix_out"), 1)
            pe.wait_ge(S("keys"), 1)
            for b in range(2):
                for j in range(3):
                    o = j * NG + b * GB
                    pe.transpose(ps[:, 4, o:o + GB], kc[0:GB, b, j * P:(j + 1) * P], ident[0:GB, 0:GB])
                    ins = pe.transpose(ps[:, 5, o:o + GB], klo[0:GB, b, j * P:(j + 1) * P], ident[0:GB, 0:GB])
            ins.then_inc(S("keysT"), 1)
            barrier(pe)
            with pe.If(unsorted(pe) > 0):
                pe.wait_ge(S("any_zero"), 1)
                with pe.Fori(0, PASSES) as q:
                    pe.wait_ge(S("any_keys"), q + 1)
                    for b in range(2):
                        for j in range(3):
                            o = j * NG + b * GB
                            pe.transpose(ps[:, 4, o:o + GB], any_c[0:GB, b, j * P:(j + 1) * P], ident[0:GB, 0:GB])
                            ins = pe.transpose(ps[:, 5, o:o + GB], any_lo[0:GB, j * P:(j + 1) * P], ident[0:GB, 0:GB])
                    ins.then_inc(S("any_keysT"), 1)
                    with pe.Fori(0, NG) as gi:
                        pe.wait_ge(S("any_hot"), NG * q + gi + 1)
                        pe.matmul(ps[:, 0, 0:KEYS].rearrange("p (s d) -> p s d", d=GW), ident16, at[:, :, bass.ds(GW * gi, GW)], start=True, stop=False)
                        for j in range(3):
                            ins = pe.matmul(ps[:, 0, 0:KEYS], src_hot[:, 0, j, :], key_hot[:, 0, j, :], start=False, stop=j == 2)
                        ins.then_inc(S("any_sum"), 1)
            with pe.Else():
                with pe.Fori(0, NG // 2) as gg:
                    for u in range(2):
                        gi = 2 * gg + u
                        pe.wait_ge(S("hot"), gi + 1)
                        pe.wait_ge(S("grp_free"), gi + 1)
                        for j in range(3):
                            ins = pe.matmul(ps[:, u, 0:KEYS], src_hot[:, u, j, :], key_hot[:, u, j, :], start=j == 0, stop=j == 2)
                        ins.then_inc(S("grp_sum"), 1)
            pe.nop()
            barrier(pe)
            for c in range(NC):
                for s_ in range(NT):
                    ins = pe.matmul(ps[:, c, :], onesq, at[:, s_, c * 512:(c + 1) * 512], start=s_ == 0, stop=s_ == NT - 1)
                ins.then_inc(S("deg"), 1)
            pe.wait_ge(S("rcnt"), 1)
            for l in range(3):
                if l:
                    pe.wait_ge(S("h_lo"), 2 * NC * l + 4)
                with pe.Fori(0, NT // 2) as tt:
                    for u in range(2):
                        t = 2 * tt + u
                        pe.wait_ge(S("g_lo"), NT * l + t + 1)
                        n = bass.ds(t * P, P)
                        for k in range(KD):
                            wbh, wbl = (w[:, l, k].rearrange("p w d -> p (w d)") for w in (wbf_hi, wbf_lo))
                            ins = three(ps[:, u, :], ht_hi[:, k, n], ht_lo[:, k, n], wbh, wbl, k == 0, k == KD - 1)
                        ins.then_inc(S("g"), 1)
                pe.wait_ge(S("g_lo"), NT * (l + 1) + 2)
                with pe.Fori(0, NC) as c:
                    cs = bass.ds(c * 512, 512)
                    pe.wait_ge(S("h_lo"), 2 * (NC * l + c) + 2)
                    for f in range(2):
                        fs = slice(f * P, (f + 1) * P)
                        for k in range(KD):
                            three(ps[:, bass.ds(4 + 2 * (c % 2) + f, 1), :], wd_hi[:, l, k, fs], wd_lo[:, l, k, fs], ht_hi[:, k:k + 1, cs], ht_lo[:, k:k + 1, cs], k == 0, k == KD - 1)
                    for s_ in range(NT):
                        for f in range(2):
                            for part, g_ in enumerate((g_hi, g_lo)):
                                ins = pe.matmul(ps[:, bass.ds(2 * (c % 2) + f, 1), :], g_[:, s_, f * P:(f + 1) * P], at[:, s_:s_ + 1, cs],
                                                start=s_ == 0 and part == 0, stop=s_ == NT - 1 and part == 1)
                    ins.then_inc(S("agg"), 1)
            pe.wait_ge(S("h_lo"), 2 * NC * 3 + 4)
            for t in range(NT):
                pe.wait_ge(S("f3_acc"), t + 1)
                n = slice(t * P, (t + 1) * P)
                for k in range(KD):
                    ins = three(ps[:, t % 2, 0:D], ht_hi[:, k, n], ht_lo[:, k, n], wf3_hi[:, k], wf3_lo[:, k], k == 0, k == KD - 1)
                ins.then_inc(S("f3"), 1)
            barrier(pe)
            pe.wait_ge(S("wr_in"), 32)
            for t in range(NT + 1):
                if t < NT:
                    pe.wait_ge(S("y"), t + 1)
                    if t >= 2:
                        pe.wait_ge(S("yT_in"), t - 1)
                    for k in range(KD):
                        ins = pe.transpose(ps[:, t % 2, k * P:(k + 1) * P], xn2[:, t, k * P:(k + 1) * P], ident)
                    ins.then_inc(S("yT"), 1)
                if t:
                    pe.wait_ge(S("yT_in"), t)
                    for k in range(KD):
                        ins = pe.matmul(ps[:, 2, (t - 1) * NE:t * NE], yT[:, (t - 1) % 2, k], wr[:, k], start=k == 0, stop=k == KD - 1)
                    ins.then_inc(S("logits"), 1)
            pe.wait_ge(S("hot12"), 1)
            h12 = hot12.rearrange("p t e -> p (t e)")
            pe.matmul(ps[:, 3, 0:NT * NE], below, h12, start=True, stop=True)
            pe.matmul(ps[:, 4, 0:NT * NE], ones, h12, start=True, stop=True).then_inc(S("ranks"), 1)
            pe.sem_inc(S("e_turned"), 2)
            pe.sem_inc(S("e_h"), 2)
            pe.sem_inc(S("e_yp"), 2)
            barrier(pe)

            def turn(b, bb, u):
                pe.wait_ge(S(f"e_x{u}"), 16 * (bb + 1))
                pe.wait_ge(S("e_xe"), b + 1)
                for k in range(KD):
                    ins = pe.transpose(ps[:, 4 + u, k * P:(k + 1) * P], x_in[:, u, k * P:(k + 1) * P], ident)
                ins.then_inc(S("e_turned"), 1)

            def hidden(b, u):
                pe.wait_ge(S("e_w1"), b + 1)
                pe.wait_ge(S("e_xe"), b + 3)
                pe.wait_ge(S("e_gelu"), b + 1)
                for j in range(KH):
                    for k in range(KD):
                        js = slice(j * P, (j + 1) * P)
                        ins = three(ps[:, 2 * u + j // 4, (j % 4) * P:(j % 4 + 1) * P], w1_now[:, u, 0, k, js], w1_now[:, u, 1, k, js],
                                    xe_hi[:, u, k], xe_lo[:, u, k], k == 0, k == KD - 1)
                ins.then_inc(S("e_h"), 1)

            def outward(b, u):
                e = pe.value_load(blk_e[0:1, bass.ds(b, 1)], min_val=0, max_val=NE - 1)
                pe.wait_ge(S("e_lo"), b + 3)
                pe.wait_ge(S("e_out"), b + 1)
                for j in range(KH):
                    o = e * EWN + j * D
                    ins = three(ps[:, 6 + u, 0:D], h_hi[:, u, j], h_lo[:, u, j], mem[:, bass.ds(o + W2_HI, D)], mem[:, bass.ds(o + W2_LO, D)],
                                j == 0, j == KH - 1)
                ins.then_inc(S("e_yp"), 1)

            turn(0, 0, 0)
            turn(1, 0, 1)
            hidden(0, 0)
            with pe.Fori(0, NPAIR - 1) as bb:
                turn(2 * bb + 2, bb + 1, 0)
                hidden(2 * bb + 1, 1)
                outward(2 * bb, 0)
                turn(2 * bb + 3, bb + 1, 1)
                hidden(2 * bb + 2, 0)
                outward(2 * bb + 1, 1)
            turn(NB - 1, NPAIR, 0)
            hidden(NB - 2, 1)
            outward(NB - 3, 0)
            hidden(NB - 1, 0)
            outward(NB - 2, 1)
            outward(NB - 1, 0)
            barrier(pe)



def lay_out(inputs):
    arrays = {k: np.ascontiguousarray(v) for k, v in inputs.items() if k not in ("src", "dst")}
    src, dst = np.asarray(inputs["src"]), np.asarray(inputs["dst"])
    size = STEP * (NWIN - 1) + WIN
    src_p = np.concatenate([src, np.zeros(size - E_ALL, src.dtype)])
    dst_p = np.concatenate([dst, np.full(size - E_ALL, NOWHERE, dst.dtype)])
    arrays["srcw"] = np.stack([src_p[i:i + WIN] for i in range(0, STEP * NWIN, STEP)])
    arrays["dstw"] = np.stack([dst_p[i:i + WIN] for i in range(0, STEP * NWIN, STEP)])
    arrays["dsamp"] = np.ascontiguousarray(dst_p[:STEP * NWIN:STEP].reshape(P, NS))
    arrays["dpair"] = np.stack([dst_p[i:i + EC + 1] for i in range(0, EC * P, EC)])
    return arrays


def kernel(**inputs):
    import concourse.bacc as bacc
    from concourse.bass_utils import run_bass_kernel_spmd

    nc = bacc.Bacc("TRN2", target_bir_lowering=False, num_devices=1)
    arrays = lay_out(inputs)
    aps = {k: nc.dram_tensor(k, a.shape, mybir.dt.from_np(a.dtype), kind="ExternalInput").ap() for k, a in arrays.items()}
    out = nc.dram_tensor("out", (N, D), F32, kind="ExternalOutput").ap()
    build(nc, aps, out)
    r = run_bass_kernel_spmd(nc, [arrays], core_ids=[0])
    return r.results[0]["out"]
```

```python
import contextlib

import numpy as np

import concourse.bass as bass
from concourse import mybir

ALU = mybir.AluOpType
ACT = mybir.ActivationFunctionType
AX_X = mybir.AxisListType.X
F32, F16 = mybir.dt.float32, mybir.dt.float16
I32, U32 = mybir.dt.int32, mybir.dt.uint32

P = 128
N = 2500
D = 256
KD = D // P
NT = (N + P - 1) // P
NP = NT * P
LAST = N - (NT - 1) * P
NC = NP // 512
E_ALL = 42500
NOWHERE = 4095

GW = 16
NG = NP // GW
GB = NG // 2
STEP = 16
WIN = 3 * P
NWIN = 2688
NS = NWIN // P
EC = (E_ALL + P - 1) // P
KEYS = NT * GW
PASSES = (E_ALL + WIN - 1) // WIN
GC = 512 // GW
SETS = 4

HEADS = 8
HC = D // HEADS
NE = 8
H = 1024
KH = H // P
TOPK = 2
NB = (TOPK * N + NE * (P - 1)) // P
SLOTS = NB * P
EPS = 1e-5
WS = 64.0

AT_B = NT * NP * 2
HALF = KD * NP * 2


def split_memory(mem):
    def view(off, dims, dt):
        size = 4 if dt in (F32, I32, U32) else 2
        n = int(np.prod(dims))
        v = mem[:, off // 2:(off + n * size) // 2]
        if dt != F16:
            v = v.bitcast(dt)
        if len(dims) == 2:
            v = v.rearrange("p (a b) -> p a b", b=dims[1])
        elif len(dims) == 3:
            v = v.rearrange("p (a b c) -> p a b c", b=dims[1], c=dims[2])
        elif len(dims) == 4:
            v = v.rearrange("p (a b c d) -> p a b c d", b=dims[1], c=dims[2], d=dims[3])
        return v
    return view


def build(nc, I, out):
    ctx = contextlib.ExitStack()
    with ctx:
        ctx.enter_context(nc.allow_non_contiguous_dma(reason="small parameter rows"))
        TOP = 211968
        mem = ctx.enter_context(nc.sbuf_tensor("mem", [P, TOP // 2], F16))
        view = split_memory(mem)
        ps = ctx.enter_context(nc.psum_tensor("ps", [P, 8, 512], F32))

        names = {}

        def S(name):
            if name not in names:
                names[name] = ctx.enter_context(nc.semaphore(name))
            return names[name]

        xslots = nc.dram_tensor("xslots", (SLOTS, D), F32).ap()
        yslots = nc.dram_tensor("yslots", (SLOTS, D), F32).ap()

        off = 0
        at = view(0, [NC * NT, 512], F16)
        ht_hi = view(AT_B, [KD, NP], F16)
        ht_lo = view(AT_B + HALF, [KD, NP], F16)
        g_hi = view(AT_B + 2 * HALF, [NT, D], F16)
        g_lo = view(AT_B + 3 * HALF, [NT, D], F16)
        h1_hi = view(AT_B + 2 * HALF, [KD, NP], F16)
        h1_lo = view(AT_B + 3 * HALF, [KD, NP], F16)
        xn = view(AT_B + 2 * HALF, [NT, D], F32)
        ACC_B = AT_B + 4 * HALF
        acc = view(ACC_B, [NT, D], F32)
        WR_B = ACC_B + NT * D * 4
        wd_hi = view(WR_B, [3, KD, D], F16)
        wd_lo = view(WR_B + 3072, [3, KD, D], F16)
        wbf_hi = view(WR_B + 6144, [3, KD, 2, D], F16)
        wbf_lo = view(WR_B + 12288, [3, KD, 2, D], F16)
        wf3_hi = view(WR_B + 18432, [KD, D], F16)
        wf3_lo = view(WR_B + 19456, [KD, D], F16)
        w2_hi = view(WR_B + 20480, [KD, D], F16)
        w2_lo = view(WR_B + 21504, [KD, D], F16)
        m1_hi = view(WR_B + 22528, [KD, D], F16)
        m1_lo = view(WR_B + 23552, [KD, D], F16)
        RC_B = WR_B + 24576
        rcnt = view(RC_B, [NP], F32)
        has = view(RC_B + 10240, [NP], F16)
        src_hot = view(RC_B, [SETS // 2, P, 6], F16)
        key_hot = view(RC_B + SETS * 768, [SETS, 3, KEYS], F16)
        iota_key = view(RC_B + SETS * 2688, [KEYS], F16)
        iota_p = view(RC_B + SETS * 2688 + 640, [P, 6], F16)
        key_now = view(RC_B + SETS * 2688 + 640 + 1536, [3, SETS], F32)
        lo_now = view(RC_B + SETS * 2688 + 640 + 1536 + SETS * 12, [SETS // 2, 6], F16)
        assert SETS * 2688 + 640 + 1536 + SETS * 18 <= 15360
        C_B = RC_B + 15360
        cols_t = view(C_B + 2720 + 768, [6, NG], F32)
        key_t, lo_t = cols_t[:, 0:3], cols_t[:, 3:6]
        R_B0 = C_B + 2720
        ident = view(C_B, [P], F32)
        ones = view(C_B + 512, [P], F32)
        below = view(C_B + 1024, [P], F32)
        cols = view(C_B + 1536, [P], F32)
        ones16 = view(C_B + 2048, [2], F16)
        mv = view(C_B + 2112, [NT, 2], F32)
        rstd = view(C_B + 2304, [NT], F32)
        grp = view(C_B + 2400, [2], F32)
        cnts = view(C_B + 2416, [4], F32)
        excess = view(C_B + 2432, [2], F32)
        viol = view(C_B + 2440, [1], F32)
        widx = view(C_B + 2448, [2], U32)
        bad = view(C_B + 2456, [1], I32)
        eps = view(C_B + 2464, [1], F32)
        iota8 = view(C_B + 2496, [NE], F32)
        onesq = view(R_B0, [P], F16)
        any_s, any_d = view(AT_B + 2 * HALF, [WIN], I32), view(AT_B + 2 * HALF + 1536, [WIN], I32)
        any_k, any_lo = view(AT_B + 2 * HALF + 3072, [WIN], F32), view(AT_B + 2 * HALF + 4608, [WIN], F32)
        any_a, any_b, any_c = (view(AT_B + 2 * HALF + 6144 + 3072 * i, [2, WIN], F32) for i in range(3))
        any_i = view(AT_B + 2 * HALF + 15360, [WIN], I32)
        ident16 = view(AT_B + 2 * HALF + 17408, [P], F16)
        blockdiag = view(R_B0 + 256, [P], F32)
        onecol = view(C_B + 2528, [1], F32)
        b1p = view(C_B + 2536, [KD], F32)
        retb = view(C_B + 2544, [KD], F32)
        nmr = view(C_B + 2560, [NT], F32)
        std = view(C_B + 2640, [NT], F32)
        R_B = C_B + 2720 + 768
        tmp_t = view(R_B, [2, 512], F32)
        tmp_p = view(WR_B + 20480, [2, 512], F32)

        spot, end = [0], [0]

        def temp(dims, dt):
            v = view(spot[0], dims, dt)
            spot[0] += -(-int(np.prod(dims)) * (2 if dt == F16 else 4) // 32) * 32
            assert spot[0] <= end[0]
            return v

        CHUNK = NT * 512 * 2
        end[0] = 3 * CHUNK
        stg = temp([3, 6, D], F32)
        stg3 = temp([KD, D], F32)
        stgw2 = temp([KD, D], F32)
        wqkv = temp([KD, 3 * D], F32)
        wkvc = temp([KD, 512], F32)
        wq = temp([KD, D], F32)
        bkv = temp([512], F32)
        bout = temp([2, D], F32)
        msum = temp([KD, 16], F32)
        bsum = temp([16], F32)
        stack = temp([P], F32)
        samp_i = temp([NS], I32)
        samp = temp([NS], F32)
        lt = temp([NS, NG + 2], F16)
        bounds = temp([NG + 2], F16)
        pair = temp([EC + 1], I32)
        cmp = temp([EC], F32)
        win_s = temp([2, WIN], I32)
        win_d = temp([2, WIN], I32)
        spot[0], end[0] = 3 * CHUNK, 4 * CHUNK
        kv_z = temp([4, 512], F32)
        kv_n = temp([4, 514], F32)
        wkv_hi = temp([KD, 512], F16)
        spot[0], end[0] = 4 * CHUNK, 5 * CHUNK
        kv_sq = temp([4, 512], F32)
        h1f = view(4 * CHUNK, [2, 512], F32)
        kvt = view(4 * CHUNK + 4096, [KD, P], F32)
        mT = view(4 * CHUNK + 5120, [KD, D + 1], F32)
        wkv_lo = temp([KD, 512], F16)
        w1 = temp([KD, D], F32)
        wqT = temp([KD, D + 1], F32)
        bias_kv = temp([512], F32)
        gbkv = temp([4, HC], F32)
        kvm = temp([KD, P], F32)
        sk = temp([KD], F32)
        kst = temp([4, 16], F32)
        kst2 = temp([4, 16], F32)
        zero = temp([D], F32)
        ka, kb, kc, klo = (view(i * 3072, [2, WIN], F32) for i in range(4))
        ki = view(4 * 3072, [2, WIN], I32)
        st6 = view(R_B, [NT, 6], F32)

        EW = 16384
        w_e = [[view(EW * e, [KD, H], F16), view(EW * e + 4096, [KD, H], F16),
                view(EW * e + 8192, [KH, D], F16), view(EW * e + 12288, [KH, D], F16)] for e in range(NE)]
        W1_HI, W1_LO, W2_HI, W2_LO = (i * 2048 for i in range(4))
        EWN = EW // 2
        b2_all = view(NE * EW, [NE, D], F32)
        ew_raw = [view(8192 * i + 12288, [2048], F32) for i in range(2 * NE)]
        assert 8192 * (2 * NE - 1) + 12288 + 8192 <= ACC_B
        RAW_IN_AT = (AT_B - 12288) // 8192
        rt = [RC_B]

        def small(dims, dt=F32):
            v = view(rt[0], dims, dt)
            rt[0] += -(-int(np.prod(dims)) * 4 // 32) * 32
            return v

        logit, mx = small([NT, NE]), small([NT, NE])
        hot1, hot2, hot12 = small([NT, NE]), small([NT, NE]), small([NT, NE])
        top = small([NT, NE], U32)
        assert rt[0] <= RC_B + 12288
        rt[0] = R_B
        tot_a, tot_b, rank = small([NT, NE]), small([NT, NE]), small([NT, NE])
        topf = small([NT, 2])
        slot_f, slot = small([TOPK, NT]), small([TOPK, NT], U32)
        wgt = small([TOPK, NT])
        nblk, cum, cum2, base = small([NE]), small([NE]), small([NE]), small([NE])
        nblk_i = small([NE], I32)
        valid = small([1])
        blk = small([NB])
        blk_e = small([NB], I32)
        assert rt[0] <= TOP, rt[0]
        wr, br = view(R_B + 4096, [KD, NE], F32), view(R_B + 4096 + 64, [NE], F32)
        blk_ge = view(RC_B + 12288, [NB, NE], F32)
        xn2 = view(WR_B, [NT, D], F32)
        yT = view(RC_B + 12288, [2, KD, P], F32)
        xe = view(WR_B, [KD, P], F32)
        xe_hi, xe_lo = view(WR_B + 1024, [2, KD, P], F16), view(WR_B + 2048, [2, KD, P], F16)
        hf = view(WR_B + 3072, [2, KH, P], F32)
        h_hi, h_lo = view(WR_B + 11264, [2, KH, P], F16), view(WR_B + 15360, [2, KH, P], F16)
        x_in, y_out = view(WR_B + 19456, [2, D], F32), view(WR_B + 21504, [2, D], F32)
        w1_now = view(WR_B + 23552, [2, 2, KD, H], F16)
        assert WR_B + 23552 + 16384 <= C_B
        y1, y2 = view(0, [NT, D], F32), view(NT * D * 4, [NT, D], F32)

        PHASES1 = 3
        NPAIR = NB // 2
        BIAS_DMAS = 8
        X_PARTS = ((0, 6), (6, 13), (13, NT - 1))
        DEG_BANK = (0, 1, 4, 2, 3)
        X_BANK = (2, 3, 6, 7)
        G_BATCH, G_FOLD, G_H1, G_OUT = (8, 4, 4), (8, 4, 4), 4, 4
        OUT_BANK = (2, 3, 5)
        FOLD0 = sum(G_BATCH) * (NT // 4)
        H10 = FOLD0 + sum(G_FOLD)
        OUT0 = H10 + G_H1 * NC
        LAST0 = OUT0 + G_OUT * (NT // 2)
        assert H10 == 3 * GC and OUT0 % SETS == 0 and LAST0 < NG
        BANK = (2, 3, 0, 1)

        def barrier(e):
            NBAR_i[e] = NBAR_i.get(e, 0) + 1
            e.drain().then_inc(S("phase"), 1)
            e.wait_ge(S("phase"), 5 * NBAR_i[e])
        NBAR_i = {}

        def unsorted(e):
            return e.value_load(bad[0:1, 0:1], min_val=0, max_val=1 << 20)

        block = ctx.enter_context(nc.Block())

        HALF_LIST = [(wd_hi[:, l], wd_lo[:, l], stg[:, l, 0:2]) for l in range(3)]
        HALF_LIST += [(wbf_hi[:, l, :, w], wbf_lo[:, l, :, w], stg[:, l, 2 + 2 * w:4 + 2 * w]) for l in range(3) for w in range(2)]
        HALF_LIST += [(wf3_hi, wf3_lo, stg3), (w2_hi, w2_lo, stgw2), (wkv_hi, wkv_lo, wkvc)]
        NSPLIT = len(HALF_LIST)

        def heads(v, first, n=8):
            return v.rearrange("p (h c) -> p h c", c=HC)

        def bc(v, dims):
            return v.to_broadcast(dims)

        @block.sync
        def _(sp):
            x = I["x"]
            sp.dma_start(samp_i, I["dsamp"]).then_inc(S("samp_in"), 16)
            sp.dma_start(pair, I["dpair"]).then_inc(S("pair_in"), 16)
            for q, (t0, t1) in enumerate(X_PARTS):
                sp.dma_start(acc[:, t0:t1, :], x[t0 * P:t1 * P, :].rearrange("(t p) d -> p t d", p=P)).then_inc(S(f"x_in{q}"), 16)
            sp.wait_ge(S("pad0"), 1)
            sp.dma_start(acc[0:LAST, NT - 1, :], x[(NT - 1) * P:N, :]).then_inc(S(f"x_in{len(X_PARTS) - 1}"), 16)
            sp.dma_start(wqkv, I["L0_mix_w_qkv"].rearrange("(r p) d -> p r d", p=P)).then_inc(S("wqkv_in"), 16)
            sp.dma_start(w1, I["L0_mix_w1"].rearrange("(r p) d -> p r d", p=P)).then_inc(S("w1_in"), 16)
            for l in range(3):
                sp.dma_start(stg[:, l, 0:4, :], I[f"L0_gnn_W{l}"].rearrange("(r p) d -> p r d", p=P)).then_inc(S("w_in"), 16)
                sp.dma_start(stg[:, l, 4:6, :], I["L0_gnn_Wf"][l * D:(l + 1) * D, :].rearrange("(r p) d -> p r d", p=P)).then_inc(S("w_in"), 16)
            sp.dma_start(stg3, I["L0_gnn_Wf"][3 * D:4 * D, :].rearrange("(r p) d -> p r d", p=P)).then_inc(S("w_in"), 16)
            sp.dma_start(stgw2, I["L0_mix_w2"].rearrange("(r p) d -> p r d", p=P)).then_inc(S("w_in"), 16)
            sp.wait_ge(S("consts"), 1)
            sp.wait_ge(S("wkvc"), 1)
            sp.dma_start(xslots.rearrange("(b p) d -> p b d", p=P), zero.rearrange("p (b d) -> p b d", b=1).to_broadcast([P, NB, D])).then_inc(S("slots_zero"), 16)
            sp.wait_ge(S("slots_zero"), 16)
            barrier(sp)
            with sp.If(unsorted(sp) > 0):
                with sp.Fori(0, PASSES) as q:
                    sp.wait_ge(S("any_read"), q + 1)
                    for tab, dst in ((I["srcw"], any_s), (I["dstw"], any_d)):
                        sp.dma_start(dst[0:GB], tab[bass.ds(q * (WIN // STEP), 1), :].to_broadcast([GB, WIN])).then_inc(S("any_in"), 16)
            sp.nop()
            barrier(sp)
            sp.dma_start(wr, I["L0_ffn_Wr"].rearrange("(k p) e -> p k e", p=P)).then_inc(S("wr_in"), 16)
            sp.dma_start(br, I["L0_ffn_br"].partition_broadcast(P)).then_inc(S("wr_in"), 16)
            sp.wait_ge(S("agg"), 3 * NC)
            for i in range(2 * NE):
                e, w = divmod(i, 2)
                if i == RAW_IN_AT:
                    sp.wait_ge(S("f3"), NT)
                src = (I["L0_ffn_W1"], I["L0_ffn_W2"])[w][e].rearrange("(k p) n -> p k n", p=P)
                sp.dma_start(ew_raw[i].rearrange("p (k n) -> p k n", k=(KD, KH)[w]), src).then_inc(S(f"ew_in{e}"), 16)
            barrier(sp)
            sp.wait_ge(S("ew_lo"), 2 * NE)
            sp.dma_start(b2_all, I["L0_ffn_b2"].rearrange("e d -> (e d)").partition_broadcast(P)).then_inc(S("b2_in"), 16)
            barrier(sp)

            def load(b, u):
                sp.wait_ge(S("e_turned"), b + 1)
                sp.dma_start(x_in[:, u], xslots[bass.ds(b * P, P), :]).then_inc(S(f"e_x{u}"), 16)

            load(0, 0)
            load(1, 1)
            with sp.Fori(0, NPAIR - 1) as bb:
                for u in range(2):
                    load(2 * bb + 2 + u, u)
            load(NB - 1, 0)
            barrier(sp)
            for t in range(NT):
                n = P if t < NT - 1 else LAST
                sp.wait_ge(S("final"), t + 1)
                sp.dma_start(out[t * P:t * P + n, :], acc[0:n, t, :]).then_inc(S("out"), 16)
            sp.wait_ge(S("out"), 16 * NT)

        @block.gpsimd
        def _(pool):
            pool.memset(ident, 0.0)
            pool.memset(below, 1.0)
            pool.memset(ones, 1.0)
            pool.memset(ones16, 1.0)
            pool.memset(onesq, 1.0)
            pool.memset(kv_n[:, :, D + P:D + P + 1], 1.0)
            pool.memset(kv_n[:, :, D + 2 * P + 1:D + 2 * P + 2], 1.0)
            pool.memset(blockdiag, 1.0 / N)
            pool.memset(zero, 0.0)
            pool.memset(stack, 0.0)
            pool.memset(eps, EPS).then_inc(S("fill"), 1)
            pool.iota(bounds, [[GW, NG + 2]], base=0, channel_multiplier=0, allow_small_or_imprecise_dtypes=True)
            pool.iota(iota_key, [[1, KEYS]], base=1, channel_multiplier=0, allow_small_or_imprecise_dtypes=True)
            pool.iota(iota_p, [[1, P], [0, 6]], base=0, channel_multiplier=0, allow_small_or_imprecise_dtypes=True)
            pool.iota(iota8, [[1, NE]], base=0, channel_multiplier=0, allow_small_or_imprecise_dtypes=True)
            pool.iota(grp, [[-GW * GB, 2]], base=0, channel_multiplier=-GW, allow_small_or_imprecise_dtypes=True)
            pool.wait_ge(S("fill"), 1)
            pool.affine_select(out=ident, in_=ident, compare_op=ALU.not_equal, fill=1.0, base=0,
                               pattern=[[-1, P]], channel_multiplier=1)
            bd = blockdiag.rearrange("p (a c) -> p a c", c=HC)
            pool.affine_select(out=bd, in_=bd, compare_op=ALU.is_ge, fill=0.0, base=0,
                               pattern=[[-HC, 4], [0, HC]], channel_multiplier=1).then_inc(S("fill"), 1)
            pool.wait_ge(S("fill"), 2)
            pool.affine_select(out=bd, in_=bd, compare_op=ALU.is_ge, fill=0.0, base=HC - 1,
                               pattern=[[HC, 4], [0, HC]], channel_multiplier=-1)
            pool.affine_select(out=below, in_=below, compare_op=ALU.is_gt, fill=0.0, base=0,
                               pattern=[[1, P]], channel_multiplier=-1).then_inc(S("consts"), 1)
            pool.wait_ge(S("widx"), 1)
            for b in range(2):
                for tab, dst in ((I["srcw"], win_s), (I["dstw"], win_d)):
                    pool.indirect_dma_start(out=dst[0:GB, b, :], out_offset=None, in_=tab,
                                            in_offset=bass.IndirectOffsetOnAxis(ap=widx[0:GB, b:b + 1], axis=0)).then_inc(S("win_in"), 16)
            pool.wait_ge(S("w_in"), 128)
            for l in range(3):
                pool.tensor_tensor(stg[:, l, 0:2], stg[:, l, 0:2], stg[:, l, 2:4], ALU.subtract).then_inc(S("wd"), 1)
            pool.wait_ge(S("xn"), 1)
            pool.tensor_tensor(acc, acc, xn, ALU.add).then_inc(S("acc"), 1)
            pool.wait_ge(S("bias_in"), 16 * BIAS_DMAS)
            pool.tensor_tensor(bout[:, 0], bout[:, 0], bout[:, 1], ALU.add).then_inc(S("acc"), 1)
            pool.wait_ge(S("acc"), 2)
            pool.tensor_tensor(acc, acc, bout[:, 0:1, :].to_broadcast([P, NT, D]), ALU.add).then_inc(S("acc"), 1)
            for b in range(NT // 4):
                pool.wait_ge(S("kn"), b + 1)
                for t in range(4):
                    k3 = kv_n[:, t, 0:256].rearrange("p (h c) -> p h c", c=HC)
                    ins = pool.tensor_tensor(k3, k3, gbkv[:, 0:1, :].to_broadcast([P, HEADS, HC]), ALU.mult)
                ins.then_inc(S("kg"), 1)
                pool.wait_ge(S("kg"), b + 1)
                for t in range(4):
                    k3 = kv_n[:, t, 0:256].rearrange("p (h c) -> p h c", c=HC)
                    ins = pool.tensor_tensor(k3, k3, gbkv[:, 1:2, :].to_broadcast([P, HEADS, HC]), ALU.add)
                ins.then_inc(S("k_ready"), 1)
            barrier(pool)
            barrier(pool)
            with pool.Fori(0, 3) as l:
                for c in range(NC):
                    for f in range(2):
                        pool.wait_ge(S("own"), 2 * NC * l + 2 * c + f + 1)
                        pool.tensor_tensor(tmp_p[:, f], tmp_p[:, f], has[:, c * 512:(c + 1) * 512], ALU.mult).then_inc(S("own_has"), 1)
            barrier(pool)
            pool.iota(blk, [[1, NB]], base=0, channel_multiplier=0, allow_small_or_imprecise_dtypes=True)
            pool.iota(valid, [[0, 1]], base=0, channel_multiplier=1, allow_small_or_imprecise_dtypes=True).then_inc(S("blk"), 1)
            pool.wait_ge(S("slots"), 1)
            pool.wait_ge(S("slots_zero"), 16)
            for t in range(NT):
                n = P if t < NT - 1 else LAST
                pool.wait_ge(S("xn2"), t + 1)
                for q in range(TOPK):
                    pool.indirect_dma_start(out=xslots, out_offset=bass.IndirectOffsetOnAxis(ap=slot[0:n, q, t:t + 1], axis=0),
                                            in_=xn2[0:n, t, :], in_offset=None).then_inc(S("scattered"), 16)
            pool.wait_ge(S("scattered"), 16 * NT * TOPK)
            barrier(pool)

            def store(b, u):
                pool.wait_ge(S("e_out"), b + 3)
                pool.dma_start(yslots[bass.ds(b * P, P), :], y_out[:, u]).then_inc(S(f"e_y{u}"), 16)

            with pool.Fori(0, NPAIR) as bb:
                for u in range(2):
                    store(2 * bb + u, u)
            store(NB - 1, 0)
            pool.wait_ge(S("e_y0"), 16 * (NPAIR + 1))
            pool.wait_ge(S("e_y1"), 16 * NPAIR)
            barrier(pool)
            for t in range(NT):
                n = P if t < NT - 1 else LAST
                for q, y_ in enumerate((y1, y2)):
                    pool.indirect_dma_start(out=y_[0:n, t, :], out_offset=None, in_=yslots,
                                            in_offset=bass.IndirectOffsetOnAxis(ap=slot[0:n, q, t:t + 1], axis=0)).then_inc(S(f"y_in{t // 2}"), 16)

        @block.vector
        def _(v):
            steps = [0]

            def step(ins):
                steps[0] += 1
                ins.then_inc(S("v_step"), 1)
                v.wait_ge(S("v_step"), steps[0])

            v.memset(acc[:, NT - 1, :], 0.0).then_inc(S("pad0"), 1)
            v.wait_ge(S("samp_in"), 16)
            step(v.tensor_copy(samp, samp_i))
            v.wait_ge(S("consts"), 1)
            for c in range(NS):
                ins = v.tensor_scalar(lt[:, c, :], bounds, samp[:, c:c + 1], None, ALU.is_gt)
            ins.then_inc(S("lt"), 1)
            v.wait_ge(S("pair_in"), 16)
            step(v.tensor_tensor(cmp, pair[:, 0:EC], pair[:, 1:EC + 1], ALU.is_gt))
            step(v.tensor_reduce(viol, cmp, AX_X, ALU.add))
            v.wait_ge(S("counted"), 1)
            step(v.tensor_copy(cnts[0:GB, :], ps[0:GB, 0, 0:4]))
            step(v.tensor_scalar(cnts[0:GB, 0:2], cnts[0:GB, 0:2], -1.0, 0.0, ALU.add, ALU.max))
            v.tensor_copy(widx[0:GB, :], cnts[0:GB, 0:2]).then_inc(S("widx"), 1)
            step(v.tensor_tensor(excess[0:GB, :], cnts[0:GB, 2:4], cnts[0:GB, 0:2], ALU.subtract))
            v.tensor_scalar(excess[0:GB, :], excess[0:GB, :], float(WIN // STEP), None, ALU.is_gt).then_inc(S("excess"), 1)
            v.wait_ge(S("badsum"), 1)
            v.tensor_copy(bad[0:1, :], ps[0:1, 1, 0:1]).then_inc(S("bad"), 1)

            for q, (t0, t1) in enumerate(X_PARTS):
                last = q == len(X_PARTS) - 1
                v.wait_ge(S(f"x_in{q}"), 32 if last else 16)
                for t in range(t0, t1 + last):
                    ins = v.bn_stats(st6[:, t, :], acc[:, t, :])
            step(ins)
            for t in range(NT):
                ins = v.bn_aggr(mv[:, t, :], st6[:, t, :])
            ins.then_inc(S("stats"), 1)
            v.wait_ge(S("std"), 1)
            step(v.reciprocal(rstd, std))
            for t in range(NT):
                ins = v.tensor_scalar(xn[:, t, :], acc[:, t, :], mv[:, t, 0:1], rstd[:, t:t + 1], ALU.subtract, ALU.mult)
            ins.then_inc(S("xn"), 1)
            for i, (hi, lo, raw) in enumerate(HALF_LIST[:-1]):
                v.wait_ge(S("w_hi"), i + 1)
                ins = v.scalar_tensor_tensor(lo, raw, WS, hi, ALU.mult, ALU.subtract)
            ins.then_inc(S("w_lo"), 1)
            for i in range(2 * NC):
                k, c = divmod(i, NC)
                v.wait_ge(S("xt_hi"), i + 1)
                v.tensor_tensor(ht_lo[:, k, c * 512:(c + 1) * 512], ps[:, X_BANK[i % 4], :],
                                ht_hi[:, k, c * 512:(c + 1) * 512], ALU.subtract).then_inc(S("xt_lo"), 1)
            v.wait_ge(S("w_lo"), 1)
            v.wait_ge(S("win_in"), 64)
            g = slice(0, GB)
            v.tensor_scalar(ki[g], win_s[g], 7, 4, ALU.logical_shift_right, ALU.logical_shift_left)
            for b in range(2):
                v.tensor_scalar(ka[g, b], win_d[g, b], grp[g, b:b + 1], None, ALU.add)
            step(v.tensor_scalar(win_s[g], win_s[g], 127, None, ALU.bitwise_and))
            v.tensor_scalar(kb[g], ka[g], 0.0, None, ALU.is_ge)
            v.tensor_copy(klo[g], win_s[g])
            step(v.tensor_tensor(kc[g], ki[g], ka[g], ALU.add))
            step(v.scalar_tensor_tensor(ka[g], ka[g], float(GW), kb[g], ALU.is_lt, ALU.mult))
            v.scalar_tensor_tensor(kc[g], kc[g], 1.0, ka[g], ALU.add, ALU.mult).then_inc(S("keys"), 1)
            v.wait_ge(S("wqkv_in"), 16)
            v.wait_ge(S("bias_in"), 16 * BIAS_DMAS)
            for k in range(KD):
                v.tensor_reduce(msum[:, k].rearrange("p (s h) -> p h s", s=2),
                                wqkv[:, k].rearrange("p (h s c) -> p h s c", s=3, c=HC)[:, :, 1:3, :], AX_X, ALU.add)
            step(v.tensor_reduce(bsum, bkv.rearrange("p (s c) -> p s c", c=HC), AX_X, ALU.add))
            v.tensor_scalar(msum, msum, 1.0 / HC, None, ALU.mult)
            step(v.tensor_scalar(bsum, bsum, 1.0 / HC, None, ALU.mult))
            for k in range(KD):
                for s_ in range(2):
                    v.tensor_tensor(wkvc[:, k, s_ * 256:(s_ + 1) * 256].rearrange("p (h c) -> p h c", c=HC),
                                    wqkv[:, k].rearrange("p (h s c) -> p h s c", s=3, c=HC)[:, :, 1 + s_, :],
                                    msum[:, k, 8 * s_:8 * s_ + 8].rearrange("p (h o) -> p h o", o=1).to_broadcast([P, HEADS, HC]), ALU.subtract)
                v.tensor_copy(heads(wq[:, k], 0), wqkv[:, k].rearrange("p (h s c) -> p h s c", s=3, c=HC)[:, :, 0, :])
            v.tensor_tensor(bias_kv.rearrange("p (s c) -> p s c", c=HC), bkv.rearrange("p (s c) -> p s c", c=HC),
                            bsum.rearrange("p (s o) -> p s o", o=1).to_broadcast([P, 16, HC]), ALU.subtract).then_inc(S("wkvc"), 1)
            hi, lo, raw = HALF_LIST[-1]
            v.wait_ge(S("w_hi"), NSPLIT)
            v.scalar_tensor_tensor(lo, raw, WS, hi, ALU.mult, ALU.subtract).then_inc(S("w_lo"), 1)
            v.wait_ge(S("colsT"), 1)
            step(v.tensor_copy(cols, ps[:, 0, 0:P]))
            v.wait_ge(S("wqT"), 1)
            for G in range(KD):
                v.tensor_copy(wqT[:, G, 0:D], ps[:, 1, G * D:(G + 1) * D])
                ins = v.tensor_copy(wqT[:, G, D:D + 1], cols[:, 104 + G:105 + G])
            ins.then_inc(S("wqT_in"), 1)
            v.wait_ge(S("keysT"), 1)
            v.tensor_copy(key_t, ps[:, 4, 0:3 * NG].rearrange("p (j g) -> p j g", j=3))
            v.tensor_copy(lo_t, ps[:, 5, 0:3 * NG].rearrange("p (j g) -> p j g", j=3)).then_inc(S("keycols"), 1)
            v.wait_ge(S("keycols"), 1)

            def hots(g0, n):
                with v.Fori(0, n // SETS) as k:
                    v.wait_ge(S("hot"), SETS * k + g0 + 1)
                    cols = bass.ds(SETS * k + g0, SETS)
                    v.tensor_copy(key_now, key_t[:, :, cols])
                    v.tensor_copy(lo_now.rearrange("p a (u j) -> p j (a u)", j=3), lo_t[:, :, cols]).then_inc(S("cols_now"), 1)
                    v.wait_ge(S("cols_now"), k + (g0 // SETS + 1))
                    for u in range(SETS):
                        if u % 2 == 0:
                            v.wait_ge(S("grp_sum"), SETS * k + (g0 + u + 2))
                            v.tensor_tensor(src_hot[:, u // 2], iota_p, lo_now[:, u // 2:u // 2 + 1, :].to_broadcast([P, P, 6]), ALU.is_equal)
                        for j in range(3):
                            ins = v.tensor_scalar(key_hot[:, u, j, :], iota_key, key_now[:, j, u:u + 1], None, ALU.is_equal)
                        ins.then_inc(S("hot"), 1)

            for b in range(NT // 4):
                g0 = sum(G_BATCH) * b
                v.wait_ge(S("kv"), b + 1)
                if b:
                    v.wait_ge(S("kn"), b)
                for t in range(4):
                    ins = v.scalar_tensor_tensor(kv_z[:, t], ps[:, t, :], 1.0 / WS, bias_kv, ALU.mult, ALU.add)
                ins.then_inc(S("kv_z"), 1)
                hots(g0, G_BATCH[0])
                v.wait_ge(S("kv_sq"), b + 1)
                v.tensor_reduce(kst, kv_sq.rearrange("p t (s c) -> p (t s) c", c=HC), AX_X, ALU.add).then_inc(S("kv_var"), 1)
                hots(g0 + G_BATCH[0], G_BATCH[1])
                v.wait_ge(S("kv_std"), b + 1)
                step(v.reciprocal(kst2, kst))
                if b:
                    v.wait_ge(S("kv_used"), b)
                for z0, n0, w in ((0, 0, D), (D, D, P), (D + P, D + P + 1, P)):
                    ins = v.tensor_tensor(kv_n[:, :, n0:n0 + w].rearrange("p t (s c) -> p t s c", c=HC), kv_z[:, :, z0:z0 + w].rearrange("p t (s c) -> p t s c", c=HC),
                                          kst2[:, :, z0 // HC:(z0 + w) // HC].rearrange("p t (s o) -> p t s o", o=1).to_broadcast([P, 4, w // HC, HC]), ALU.mult)
                ins.then_inc(S("kn"), 1)
                hots(g0 + sum(G_BATCH[:2]), G_BATCH[2])
            hots(FOLD0, G_FOLD[0])
            v.wait_ge(S("kv_used"), NT // 4)
            for G in range(KD):
                v.tensor_copy(sk[:, G:G + 1], ps[:, 4 + G, P:P + 1])
                ins = v.tensor_tensor(kvt[:, G].rearrange("p (a c) -> p a c", c=HC), ps[:, 4 + G, 0:P].rearrange("p (a c) -> p a c", c=HC),
                                      gbkv[:, 2:3, :].to_broadcast([P, 4, HC]), ALU.mult)
            step(ins)
            for G in range(KD):
                ins = v.scalar_tensor_tensor(kvt[:, G].rearrange("p (a c) -> p a c", c=HC), gbkv[:, 3:4, :].to_broadcast([P, 4, HC]),
                                             sk[:, G:G + 1], kvt[:, G].rearrange("p (a c) -> p a c", c=HC), ALU.mult, ALU.add)
            step(ins)
            v.tensor_tensor(kvm, kvt, blockdiag.rearrange("p (o c) -> p o c", o=1).to_broadcast([P, KD, P]), ALU.mult).then_inc(S("kvm"), 1)
            hots(FOLD0 + G_FOLD[0], G_FOLD[1])
            v.wait_ge(S("mT"), 1)
            for G in range(KD):
                v.tensor_copy(retb[:, G:G + 1], ps[:, 2 + G, D:D + 1])
                ins = v.tensor_copy(mT[:, G, :], ps[:, 2 + G, 0:D + 1])
            step(ins)
            for G in range(KD):
                ins = v.tensor_tensor(mT[:, G, G * P:(G + 1) * P], mT[:, G, G * P:(G + 1) * P], ident, ALU.add)
            ins.then_inc(S("mT_in"), 1)
            hots(FOLD0 + sum(G_FOLD[:2]), G_FOLD[2])
            v.wait_ge(S("m1_hi"), 1)
            v.scalar_tensor_tensor(m1_lo, ps[:, 0, :].rearrange("p (k d) -> p k d", k=KD), WS, m1_hi, ALU.mult, ALU.subtract)
            v.tensor_tensor(b1p, ps[:, 1, 0:KD], cols[:, 102:104], ALU.add).then_inc(S("m1_lo"), 1)
            for i in range(2 * NC):
                c, f = divmod(i, 2)
                if f == 0:
                    hots(H10 + G_H1 * c, G_H1)
                v.wait_ge(S("h1_hi"), i + 1)
                v.tensor_tensor(h1_lo[:, f, c * 512:(c + 1) * 512], h1f[:, f], h1_hi[:, f, c * 512:(c + 1) * 512], ALU.subtract).then_inc(S("h1_lo"), 1)
            v.wait_ge(S("acc"), 3)
            for t in range(NT):
                if t % 2 == 0:
                    hots(OUT0 + G_OUT * (t // 2), G_OUT)
                v.wait_ge(S("mix_out"), t + 1)
                v.scalar_tensor_tensor(acc[:, t], ps[:, OUT_BANK[t % 3], 0:D], 1.0 / WS, acc[:, t], ALU.mult, ALU.add).then_inc(S("mix_acc"), 1)
            hots(LAST0, NG - LAST0)
            barrier(v)
            with v.If(unsorted(v) > 0):
                v.memset(at, 0.0)
                v.tensor_copy(ident16, ident).then_inc(S("any_zero"), 1)
                v.sem_inc(S("any_read"), 1)
                v.sem_inc(S("any_out"), 1)
                with v.Fori(0, PASSES) as q:
                    v.wait_ge(S("any_in"), 32 * (q + 1))
                    v.wait_ge(S("any_out"), NG * q + 1)
                    v.tensor_scalar(any_i[g], any_s[g], 7, 4, ALU.logical_shift_right, ALU.logical_shift_left)
                    for b in range(2):
                        v.tensor_scalar(any_a[g, b], any_d[g], grp[g, b:b + 1], None, ALU.add)
                    v.tensor_scalar(any_s[g], any_s[g], 127, None, ALU.bitwise_and).then_inc(S("any_step"), 1)
                    v.wait_ge(S("any_step"), 4 * q + 1)
                    v.tensor_copy(any_k[g], any_i[g])
                    v.tensor_copy(any_lo[g], any_s[g]).then_inc(S("any_read"), 1)
                    v.tensor_scalar(any_b[g], any_a[g], 0.0, None, ALU.is_ge).then_inc(S("any_step"), 1)
                    v.wait_ge(S("any_step"), 4 * q + 2)
                    v.tensor_tensor(any_c[g], any_a[g], any_k[g].rearrange("p (o w) -> p o w", o=1).to_broadcast([GB, 2, WIN]), ALU.add).then_inc(S("any_step"), 1)
                    v.wait_ge(S("any_step"), 4 * q + 3)
                    v.scalar_tensor_tensor(any_a[g], any_a[g], float(GW), any_b[g], ALU.is_lt, ALU.mult).then_inc(S("any_step"), 1)
                    v.wait_ge(S("any_step"), 4 * q + 4)
                    v.scalar_tensor_tensor(any_c[g], any_c[g], 1.0, any_a[g], ALU.add, ALU.mult).then_inc(S("any_keys"), 1)
                    v.wait_ge(S("any_keysT"), q + 1)
                    v.tensor_copy(key_t, ps[:, 4, 0:3 * NG].rearrange("p (j g) -> p j g", j=3))
                    v.tensor_copy(lo_t, ps[:, 5, 0:3 * NG].rearrange("p (j g) -> p j g", j=3)).then_inc(S("any_cols"), 1)
                    with v.Fori(0, NG) as gi:
                        v.wait_ge(S("any_cols"), q + 1)
                        v.wait_ge(S("any_out"), NG * q + gi + 1)
                        for j in range(3):
                            v.tensor_scalar(src_hot[:, 0, :, j], iota_p[:, :, 0], lo_t[:, j, bass.ds(gi, 1)], None, ALU.is_equal)
                            ins = v.tensor_scalar(key_hot[:, 0, j, :], iota_key, key_t[:, j, bass.ds(gi, 1)], None, ALU.is_equal)
                        ins.then_inc(S("any_hot"), 1)
            v.nop()
            v.sem_inc(S("g_lo"), 4)
            v.sem_inc(S("f3_acc"), 4)
            v.sem_inc(S("h_lo"), 4)
            v.sem_inc(S("pre"), 2)
            barrier(v)
            for c in (3, 4, 0, 1, 2):
                v.tensor_scalar(has[:, c * 512:(c + 1) * 512], ps[:, DEG_BANK[c], :], 1.0, None, ALU.min)
                v.tensor_scalar(rcnt[:, c * 512:(c + 1) * 512], ps[:, DEG_BANK[c], :], 1.0, None, ALU.max).then_inc(S("rcnt"), 1)
            for l in range(3):
                with v.Fori(0, NC) as c:
                    for u in range(4):
                        t = 4 * c + u
                        v.wait_ge(S("g_hi"), NT * l + t + 1)
                        v.scalar_tensor_tensor(g_lo[:, bass.ds(t, 1), :], ps[:, BANK[u]:BANK[u] + 1, 0:D], 1.0 / WS, g_hi[:, bass.ds(t, 1), :], ALU.mult, ALU.subtract)
                        v.scalar_tensor_tensor(acc[:, bass.ds(t, 1), :], ps[:, BANK[u]:BANK[u] + 1, D:2 * D], 1.0 / WS, acc[:, bass.ds(t, 1), :], ALU.mult, ALU.add).then_inc(S("g_lo"), 1)
                if l == 0:
                    v.wait_ge(S("rcnt"), NC)
                    v.reciprocal(rcnt, rcnt).then_inc(S("rcnt"), 1)
                    v.wait_ge(S("rcnt"), NC + 1)
                with v.Fori(0, NC) as c:
                    v.wait_ge(S("agg"), NC * l + c + 1)
                    for f in range(2):
                        i = 2 * NC * l + 2 * c + f
                        v.wait_ge(S("h_lo"), i + 3)
                        v.tensor_tensor(tmp_t[:, f:f + 1], ps[:, bass.ds(2 * (c % 2) + f, 1), :],
                                        rcnt.rearrange("p (o n) -> p o n", o=1)[:, :, bass.ds(c * 512, 512)], ALU.mult).then_inc(S("mean"), 1)
                    for f in range(2):
                        i = 2 * NC * l + 2 * c + f
                        v.wait_ge(S("mean"), i + 1)
                        v.wait_ge(S("own_has"), i + 1)
                        v.tensor_tensor(tmp_t[:, f], tmp_t[:, f], tmp_p[:, f], ALU.add).then_inc(S("pre"), 1)
                    for f in range(2):
                        i = 2 * NC * l + 2 * c + f
                        v.wait_ge(S("h_hi"), i + 1)
                        v.scalar_tensor_tensor(ht_lo[:, f, bass.ds(c * 512, 512)], tmp_t[:, f], 0.0,
                                               ht_hi[:, f, bass.ds(c * 512, 512)], ALU.max, ALU.subtract).then_inc(S("h_lo"), 1)
            for t in range(NT + 2):
                if t < NT:
                    v.wait_ge(S("f3"), t + 1)
                    v.scalar_tensor_tensor(acc[:, t], ps[:, BANK[t % 4], 0:D], 1.0 / WS, acc[:, t], ALU.mult, ALU.add).then_inc(S("f3_acc"), 1)
                if 1 <= t <= NT:
                    v.wait_ge(S("f3_acc"), t + 4)
                    v.bn_stats(st6[:, t - 1, :], acc[:, t - 1, :]).then_inc(S("bn1"), 1)
                if t >= 2:
                    v.wait_ge(S("bn1"), t - 1)
                    ins = v.bn_aggr(mv[:, t - 2, :], st6[:, t - 2, :])
            ins.then_inc(S("stats"), 1)
            barrier(v)

            v.wait_ge(S("std"), 2)
            step(v.reciprocal(rstd, std))
            for t in range(NT):
                v.tensor_scalar(xn2[:, t, :], acc[:, t, :], mv[:, t, 0:1], rstd[:, t:t + 1], ALU.subtract, ALU.mult).then_inc(S("y"), 1)
            for t in range(NT):
                v.wait_ge(S("y"), t + 1)
                v.bn_stats(st6[:, t, :], xn2[:, t, :]).then_inc(S("bn2"), 1)
            v.wait_ge(S("bn2"), NT)
            v.wait_ge(S("y"), NT)
            for t in range(NT):
                ins = v.bn_aggr(mv[:, t, :], st6[:, t, :])
            ins.then_inc(S("stats"), 1)
            v.wait_ge(S("std"), 3)
            step(v.reciprocal(rstd, std))
            v.scalar_tensor_tensor(nmr, mv[:, :, 0], -1.0, rstd, ALU.mult, ALU.mult).then_inc(S("nmr"), 1)
            v.wait_ge(S("logits"), NT)
            v.wait_ge(S("wr_in"), 32)
            step(v.tensor_tensor(logit, ps[:, 2, 0:NT * NE].rearrange("p (t e) -> p t e", e=NE),
                                 br.rearrange("p (o e) -> p o e", o=1).to_broadcast([P, NT, NE]), ALU.add))
            for t in range(NT):
                ins = v.max(mx[:, t, :], logit[:, t, :])
            step(ins)
            for t in range(NT):
                ins = v.max_index(top[:, t, :], mx[:, t, :], logit[:, t, :])
            step(ins)
            v.tensor_copy(topf, top[:, :, 0:2])
            v.wait_ge(S("blk"), 1)
            v.tensor_scalar(valid, valid, float(LAST), None, ALU.is_lt)
            step(v.tensor_tensor(wgt[:, 1], mx[:, :, 1], mx[:, :, 0], ALU.subtract))
            for q, hot in enumerate((hot1, hot2)):
                ins = v.tensor_tensor(hot, iota8.rearrange("p (o e) -> p o e", o=1).to_broadcast([P, NT, NE]),
                                      topf[:, :, q:q + 1].to_broadcast([P, NT, NE]), ALU.is_equal)
            ins.then_inc(S("diff"), 1)
            v.wait_ge(S("diff"), 1)
            step(v.tensor_tensor(hot12, hot1, hot2, ALU.add))
            v.tensor_scalar(hot12[:, NT - 1], hot12[:, NT - 1], valid, None, ALU.mult).then_inc(S("hot12"), 1)
            v.wait_ge(S("ranks"), 1)
            totals = ps[:, 4, 0:NT * NE].rearrange("p (t e) -> p t e", e=NE)
            step(v.tensor_copy(tot_a, totals))
            src, dst = tot_a, tot_b
            s_ = 1
            while s_ < NT:
                v.tensor_tensor(dst[:, s_:NT], src[:, s_:NT], src[:, 0:NT - s_], ALU.add)
                step(v.tensor_copy(dst[:, 0:s_], src[:, 0:s_]))
                src, dst = dst, src
                s_ *= 2
            v.tensor_tensor(rank, src, totals, ALU.subtract)
            step(v.tensor_scalar(nblk_i, src[:, NT - 1], float(P - 1), None, ALU.add))
            step(v.tensor_tensor(rank, rank, ps[:, 3, 0:NT * NE].rearrange("p (t e) -> p t e", e=NE), ALU.add))
            step(v.tensor_scalar(nblk_i, nblk_i, 7, None, ALU.logical_shift_right))
            step(v.tensor_copy(nblk, nblk_i))
            step(v.tensor_copy(cum, nblk))
            cs, cd = cum, cum2
            for s_ in (1, 2, 4):
                v.tensor_tensor(cd[:, s_:NE], cs[:, s_:NE], cs[:, 0:NE - s_], ALU.add)
                step(v.tensor_copy(cd[:, 0:s_], cs[:, 0:s_]))
                cs, cd = cd, cs
            step(v.tensor_tensor(base, cs, nblk, ALU.subtract))
            step(v.tensor_scalar(base, base, float(P), None, ALU.mult))
            step(v.tensor_tensor(rank, rank, base.rearrange("p (o e) -> p o e", o=1).to_broadcast([P, NT, NE]), ALU.add))
            v.tensor_tensor(hot1, hot1, rank, ALU.mult)
            step(v.tensor_tensor(hot2, hot2, rank, ALU.mult))
            v.tensor_reduce(slot_f[:, 0], hot1, AX_X, ALU.add)
            step(v.tensor_reduce(slot_f[:, 1], hot2, AX_X, ALU.add))
            v.tensor_copy(slot, slot_f).then_inc(S("slots"), 1)
            step(v.tensor_tensor(blk_ge, blk.rearrange("p (b o) -> p b o", o=1).to_broadcast([P, NB, NE]),
                                 cs.rearrange("p (o e) -> p o e", o=1).to_broadcast([P, NB, NE]), ALU.is_ge))
            step(v.tensor_reduce(blk, blk_ge, AX_X, ALU.add))
            v.tensor_scalar(blk_e, blk, float(NE - 1), None, ALU.min).then_inc(S("blk_e"), 1)
            v.wait_ge(S("blk_e"), 1)
            v.wait_ge(S("wexp"), 1)
            step(v.tensor_scalar(wgt[:, 0], wgt[:, 1], 1.0, None, ALU.add))
            step(v.reciprocal(wgt[:, 0], wgt[:, 0]))
            step(v.tensor_tensor(wgt[:, 1], wgt[:, 1], wgt[:, 0], ALU.mult))
            for i in range(2 * NE):
                e, w = divmod(i, 2)
                v.wait_ge(S("ew_hi"), i + 1)
                if i:
                    v.wait_ge(S("ew_lo"), i)
                v.scalar_tensor_tensor(w_e[e][2 * w + 1].rearrange("p k n -> p (k n)"), ew_raw[i], WS,
                                       w_e[e][2 * w].rearrange("p k n -> p (k n)"), ALU.mult, ALU.subtract).then_inc(S("ew_lo"), 1)
            v.sem_inc(S("e_xe"), 2)
            v.sem_inc(S("e_lo"), 2)
            v.sem_inc(S("e_out"), 2)
            barrier(v)

            def widen(b, u):
                e = v.value_load(blk_e[0:1, bass.ds(b, 1)], min_val=0, max_val=NE - 1)
                v.wait_ge(S("e_turned"), b + 3)
                v.wait_ge(S("e_h"), b + 1)
                v.wait_ge(S("e_xe"), b + 2)
                for k in range(KD):
                    gcol, bcol = cols[:, bass.ds(64 + KD * e + k, 1)], cols[:, bass.ds(80 + KD * e + k, 1)]
                    ins = v.tensor_scalar(xe[:, k], ps[:, 4 + u, k * P:(k + 1) * P], gcol, bcol, ALU.mult, ALU.add)
                ins.then_inc(S("e_xf"), 1)
                v.wait_ge(S("e_xf"), b + 1)
                v.tensor_copy(xe_hi[:, u], xe).then_inc(S("e_xw"), 1)
                v.wait_ge(S("e_xw"), b + 1)
                v.tensor_tensor(xe_lo[:, u], xe, xe_hi[:, u], ALU.subtract).then_inc(S("e_xe"), 1)

            def fetch(b, u):
                e = v.value_load(blk_e[0:1, bass.ds(b, 1)], min_val=0, max_val=NE - 1)
                v.wait_ge(S("e_h"), b + 1)
                v.tensor_copy(w1_now[:, u].rearrange("p s k h -> p (s k h)"), mem[:, bass.ds(e * EWN + W1_HI, 2 * KD * H)]).then_inc(S("e_w1"), 1)

            def low(b, u):
                v.wait_ge(S("e_hi"), b + 1)
                v.tensor_tensor(h_lo[:, u], hf[:, u], h_hi[:, u], ALU.subtract).then_inc(S("e_lo"), 1)

            def result(b, bb, u):
                e = v.value_load(blk_e[0:1, bass.ds(b, 1)], min_val=0, max_val=NE - 1)
                v.wait_ge(S("e_yp"), b + 3)
                if bb is not None:
                    v.wait_ge(S(f"e_y{u}"), 16 * bb)
                v.scalar_tensor_tensor(y_out[:, u:u + 1], ps[:, 6 + u:7 + u, 0:D], 1.0 / WS, b2_all[:, bass.ds(e, 1), :], ALU.mult, ALU.add).then_inc(S("e_out"), 1)

            v.wait_ge(S("b2_in"), 16)
            widen(0, 0)
            fetch(0, 0)
            widen(1, 1)
            fetch(1, 1)
            low(0, 0)

            def two_blocks(bb, stores):
                fetch(2 * bb + 2, 0)
                widen(2 * bb + 2, 0)
                low(2 * bb + 1, 1)
                result(2 * bb, stores, 0)
                fetch(2 * bb + 3, 1)
                widen(2 * bb + 3, 1)
                low(2 * bb + 2, 0)
                result(2 * bb + 1, stores, 1)

            two_blocks(0, None)
            with v.Fori(1, NPAIR - 1) as bb:
                two_blocks(bb, bb)
            widen(NB - 1, 0)
            fetch(NB - 1, 0)
            low(NB - 2, 1)
            result(NB - 3, NPAIR - 1, 0)
            low(NB - 1, 0)
            result(NB - 2, NPAIR - 1, 1)
            result(NB - 1, NPAIR, 0)
            barrier(v)
            for t in range(NT):
                n = P if t < NT - 1 else LAST
                v.wait_ge(S(f"y_in{t // 2}"), 32 * TOPK)
                step(v.scalar_tensor_tensor(acc[0:n, t], y1[0:n, t], wgt[0:n, 0, t:t + 1], acc[0:n, t], ALU.mult, ALU.add))
                v.scalar_tensor_tensor(acc[0:n, t], y2[0:n, t], wgt[0:n, 1, t:t + 1], acc[0:n, t], ALU.mult, ALU.add).then_inc(S("final"), 1)

        @block.scalar
        def _(a):
            a.wait_ge(S("consts"), 1)
            rows = [(I["L0_ffn_b1"].rearrange("e (j p) -> (e j) p", p=P), 0, NE * KH),
                    (I["L0_ffn_ln_g"].rearrange("e (j p) -> (e j) p", p=P), 64, NE * KD),
                    (I["L0_ffn_ln_b"].rearrange("e (j p) -> (e j) p", p=P), 80, NE * KD),
                    (I["L0_gnn_b0"].rearrange("(j p) -> j p", p=P), 96, KD), (I["L0_gnn_b1"].rearrange("(j p) -> j p", p=P), 98, KD),
                    (I["L0_gnn_b2"].rearrange("(j p) -> j p", p=P), 100, KD), (I["L0_mix_b1"].rearrange("(j p) -> j p", p=P), 102, KD)]
            for src, r, n in rows:
                a.dma_start(stack[r:r + n, :], src).then_inc(S("rows_in"), 16)
            bq = I["L0_mix_b_qkv"].rearrange("(h s c) -> s h c", s=3, c=HC)
            for G in range(KD):
                a.dma_start(stack[104 + G:105 + G, :].rearrange("o (h c) -> o h c", c=HC), bq[0:1, 4 * G:4 * G + 4, :]).then_inc(S("rows_in"), 16)
            for s_ in range(2):
                a.dma_start(bkv[:, s_ * 256:(s_ + 1) * 256].rearrange("p (h c) -> p h c", c=HC), bq[1 + s_:2 + s_, :, :].to_broadcast([P, HEADS, HC])).then_inc(S("bias_in"), 16)
            for i, n in enumerate(("kln_g", "kln_b", "vln_g", "vln_b")):
                a.dma_start(gbkv[:, i], I[f"L0_mix_{n}"].partition_broadcast(P)).then_inc(S("bias_in"), 16)
            a.dma_start(bout[:, 0], I["L0_gnn_bf"].partition_broadcast(P)).then_inc(S("bias_in"), 16)
            a.dma_start(bout[:, 1], I["L0_mix_b2"].partition_broadcast(P)).then_inc(S("bias_in"), 16)

            a.wait_ge(S("stats"), 1)
            a.activation(std, mv[:, :, 1], ACT.Sqrt, bias=eps[:, 0:1]).then_inc(S("std"), 1)
            a.wait_ge(S("w_in"), 128)
            for i, (hi, lo, raw) in enumerate(HALF_LIST[:-1]):
                if i < 3:
                    a.wait_ge(S("wd"), i + 1)
                a.activation(hi, raw, ACT.Copy, scale=WS).then_inc(S("w_hi"), 1)
            for i in range(2 * NC):
                k, c = divmod(i, NC)
                a.wait_ge(S("xt"), i + 1)
                a.activation(ht_hi[:, k, c * 512:(c + 1) * 512], ps[:, X_BANK[i % 4], :], ACT.Copy).then_inc(S("xt_hi"), 1)
            a.wait_ge(S("wkvc"), 1)
            a.activation(HALF_LIST[-1][0], HALF_LIST[-1][2], ACT.Copy, scale=WS).then_inc(S("w_hi"), 1)

            def counts(g0, n):
                c = g0 // GC
                with a.Fori(0, n // SETS) as k:
                    for u in range(SETS):
                        a.wait_ge(S("grp_sum"), SETS * k + (g0 + u + 1 + SETS))
                        a.activation(at[:, c * NT:(c + 1) * NT, bass.ds(GW * SETS * k + GW * (g0 + u - c * GC), GW)],
                                     ps[:, 6 + u % 2, 0:KEYS].rearrange("p (s d) -> p s d", d=GW), ACT.Copy).then_inc(S("grp_free"), 1)

            for b in range(NT // 4):
                g0 = sum(G_BATCH) * b
                a.wait_ge(S("kv_z"), b + 1)
                if b:
                    a.wait_ge(S("kv_var"), b)
                a.activation(kv_sq, kv_z, ACT.Square).then_inc(S("kv_sq"), 1)
                if b == 0:
                    a.wait_ge(S("keycols"), 1)
                    a.wait_ge(S("w_lo"), 2)
                    a.wait_ge(S("wqT"), 1)
                    a.wait_ge(S("acc"), 3)
                counts(g0, G_BATCH[0])
                a.wait_ge(S("kv_var"), b + 1)
                a.activation(kst, kst, ACT.Sqrt, bias=eps[:, 0:1], scale=1.0 / HC).then_inc(S("kv_std"), 1)
                counts(g0 + G_BATCH[0], G_BATCH[1])
                counts(g0 + sum(G_BATCH[:2]), G_BATCH[2])
            counts(FOLD0, G_FOLD[0])
            counts(FOLD0 + G_FOLD[0], G_FOLD[1])
            a.wait_ge(S("m1"), 1)
            a.activation(m1_hi, ps[:, 0, :].rearrange("p (k d) -> p k d", k=KD), ACT.Copy, scale=WS).then_inc(S("m1_hi"), 1)
            counts(FOLD0 + sum(G_FOLD[:2]), G_FOLD[2])
            a.wait_ge(S("m1_lo"), 1)
            a.wait_ge(S("kv_used"), NT // 4)
            for i in range(2 * NC):
                c, f = divmod(i, 2)
                a.wait_ge(S("h1"), i + 1)
                if i >= 2:
                    a.wait_ge(S("h1_lo"), i - 1)
                a.activation(h1f[:, f], ps[:, 2 + i % 4, :], ACT.Gelu, bias=b1p[:, f:f + 1], scale=1.0 / WS).then_inc(S("h1f"), 1)
                a.wait_ge(S("h1f"), i + 1)
                a.activation(h1_hi[:, f, c * 512:(c + 1) * 512], h1f[:, f], ACT.Copy).then_inc(S("h1_hi"), 1)
                if f == 1:
                    counts(H10 + G_H1 * c, G_H1)
            a.wait_ge(S("h1_lo"), 2 * NC)
            a.wait_ge(S("slots_zero"), 16)
            for i in range(NT // 2):
                counts(OUT0 + G_OUT * i, G_OUT)
            counts(LAST0, NG - LAST0)
            barrier(a)
            with a.If(unsorted(a) > 0):
                with a.Fori(0, PASSES) as q:
                    for c in range(NC):
                        with a.Fori(0, GC) as gi:
                            a.wait_ge(S("any_sum"), NG * q + GC * c + gi + 1)
                            a.activation(at[:, c * NT:(c + 1) * NT, bass.ds(GW * gi, GW)], ps[:, 0, 0:KEYS].rearrange("p (s d) -> p s d", d=GW),
                                         ACT.Copy).then_inc(S("any_out"), 1)
            a.nop()
            barrier(a)
            for l in range(3):
                with a.Fori(0, NC) as c:
                    for u in range(4):
                        t = 4 * c + u
                        a.wait_ge(S("g"), NT * l + t + 1)
                        a.activation(g_hi[:, bass.ds(t, 1), :], ps[:, BANK[u]:BANK[u] + 1, 0:D], ACT.Copy, scale=1.0 / WS).then_inc(S("g_hi"), 1)
                with a.Fori(0, NC) as c:
                    for f in range(2):
                        i = 2 * NC * l + 2 * c + f
                        a.wait_ge(S("own_sum"), NC * l + c + 1)
                        a.wait_ge(S("pre"), i + 1)
                        a.activation(tmp_p[:, f:f + 1], ps[:, bass.ds(4 + 2 * (c % 2) + f, 1), :], ACT.Identity,
                                     bias=cols[:, 96 + 2 * l + f:97 + 2 * l + f], scale=1.0 / WS).then_inc(S("own"), 1)
                    for f in range(2):
                        i = 2 * NC * l + 2 * c + f
                        a.wait_ge(S("pre"), i + 3)
                        a.activation(ht_hi[:, f, bass.ds(c * 512, 512)], tmp_t[:, f], ACT.Relu).then_inc(S("h_hi"), 1)
            barrier(a)

            a.wait_ge(S("stats"), 2)
            a.activation(std, mv[:, :, 1], ACT.Sqrt, bias=eps[:, 0:1]).then_inc(S("std"), 1)
            for t in range(NT):
                a.wait_ge(S("yT"), t + 1)
                if t >= 2:
                    a.wait_ge(S("logits"), t - 1)
                a.activation(yT[:, t % 2], ps[:, t % 2, 0:D].rearrange("p (k n) -> p k n", k=KD), ACT.Copy).then_inc(S("yT_in"), 1)
            a.wait_ge(S("stats"), 3)
            a.wait_ge(S("y"), NT)
            a.activation(std, mv[:, :, 1], ACT.Sqrt, bias=eps[:, 0:1]).then_inc(S("std"), 1)
            a.wait_ge(S("nmr"), 1)
            for t in range(NT):
                a.activation(xn2[:, t, :], xn2[:, t, :], ACT.Identity, bias=nmr[:, t:t + 1], scale=rstd[:, t:t + 1]).then_inc(S("xn2"), 1)
            a.wait_ge(S("diff"), 1)
            a.activation(wgt[:, 1], wgt[:, 1], ACT.Exp).then_inc(S("wexp"), 1)
            for i in range(2 * NE):
                e, w = divmod(i, 2)
                a.wait_ge(S(f"ew_in{e}"), 32)
                if i >= 2:
                    a.wait_ge(S("ew_lo"), i - 1)
                a.activation(w_e[e][2 * w].rearrange("p k n -> p (k n)"), ew_raw[i], ACT.Copy, scale=WS).then_inc(S("ew_hi"), 1)
            a.sem_inc(S("e_gelu"), 2)
            barrier(a)
            a.preload_act_table(ACT.Gelu)

            def gelu(b, u):
                e = a.value_load(blk_e[0:1, bass.ds(b, 1)], min_val=0, max_val=NE - 1)
                a.wait_ge(S("e_h"), b + 3)
                a.wait_ge(S("e_lo"), b + 1)
                for j in range(KH):
                    ins = a.activation(hf[:, u, j], ps[:, 2 * u + j // 4, (j % 4) * P:(j % 4 + 1) * P], ACT.Gelu,
                                       bias=cols[:, bass.ds(KH * e + j, 1)], scale=1.0 / WS)
                ins.then_inc(S("e_gelu"), 1)
                a.wait_ge(S("e_gelu"), b + 3)
                a.wait_ge(S("e_yp"), b + 1)
                a.activation(h_hi[:, u], hf[:, u], ACT.Copy).then_inc(S("e_hi"), 1)

            with a.Fori(0, NPAIR) as bb:
                gelu(2 * bb, 0)
                gelu(2 * bb + 1, 1)
            gelu(NB - 1, 0)
            barrier(a)

        @block.tensor
        def _(pe):
            def three(out_, w_hi, w_lo, x_hi, x_lo, first, last):
                pe.matmul(out_, w_hi, x_hi, start=first, stop=False)
                pe.matmul(out_, w_hi, x_lo, start=False, stop=False)
                return pe.matmul(out_, w_lo, x_hi, start=False, stop=last)

            pe.sem_inc(S("grp_sum"), SETS)
            pe.sem_inc(S("grp_free"), 2)
            pe.sem_inc(S("hot"), 1)
            pe.wait_ge(S("consts"), 1)
            pe.wait_ge(S("lt"), 1)
            for q, lo in enumerate((0, GB, 1, GB + 1)):
                for c in range(NS):
                    ins = pe.matmul(ps[0:GB, 0, q:q + 1], lt[:, c, lo:lo + GB], ones16[:, 0:1], start=c == 0, stop=c == NS - 1)
            ins.then_inc(S("counted"), 1)
            pe.wait_ge(S("excess"), 1)
            pe.matmul(ps[0:1, 1, 0:1], ones[0:GB, 0:1], excess[0:GB, 0:1], start=True, stop=False)
            pe.matmul(ps[0:1, 1, 0:1], ones[0:GB, 0:1], excess[0:GB, 1:2], start=False, stop=False)
            pe.matmul(ps[0:1, 1, 0:1], ones[:, 0:1], viol, start=False, stop=True).then_inc(S("badsum"), 1)
            pe.wait_ge(S("xn"), 1)
            for i in range(2 * NC):
                k, c = divmod(i, NC)
                if i >= 4:
                    pe.wait_ge(S("xt_lo"), i - 3)
                for q in range(4):
                    ins = pe.transpose(ps[:, X_BANK[i % 4], q * P:(q + 1) * P], xn[:, 4 * c + q, k * P:(k + 1) * P], ident)
                ins.then_inc(S("xt"), 1)
            pe.wait_ge(S("rows_in"), 16 * 9)
            pe.wait_ge(S("counted"), 1)
            pe.wait_ge(S("widx"), 1)
            pe.transpose(ps[:, 0, 0:P], stack, ident).then_inc(S("colsT"), 1)
            pe.wait_ge(S("wkvc"), 1)
            pe.wait_ge(S("bad"), 1)
            for G in range(KD):
                for k in range(KD):
                    ins = pe.transpose(ps[:, 1, G * D + k * P:G * D + (k + 1) * P], wq[:, k, G * P:(G + 1) * P], ident)
            ins.then_inc(S("wqT"), 1)
            pe.wait_ge(S("keys"), 1)
            for b in range(2):
                for j in range(3):
                    o = j * NG + b * GB
                    pe.transpose(ps[:, 4, o:o + GB], kc[0:GB, b, j * P:(j + 1) * P], ident[0:GB, 0:GB])
                    ins = pe.transpose(ps[:, 5, o:o + GB], klo[0:GB, b, j * P:(j + 1) * P], ident[0:GB, 0:GB])
            ins.then_inc(S("keysT"), 1)

            def sums(g0, n):
                with pe.Fori(0, n // SETS) as k:
                    for u in range(SETS):
                        pe.wait_ge(S("hot"), SETS * k + (g0 + u + 2))
                        pe.wait_ge(S("grp_free"), SETS * k + (g0 + u + 1))
                        for j in range(3):
                            ins = pe.matmul(ps[:, 6 + u % 2, 0:KEYS], src_hot[:, u // 2, :, 3 * (u % 2) + j], key_hot[:, u, j, :], start=j == 0, stop=j == 2)
                        ins.then_inc(S("grp_sum"), 1)

            def degrees(c):
                pe.wait_ge(S("grp_free"), GC * (c + 1) + 2)
                for s_ in range(NT):
                    pe.matmul(ps[:, DEG_BANK[c], :], onesq, at[:, c * NT + s_, :], start=s_ == 0, stop=s_ == NT - 1)

            pe.wait_ge(S("wqT_in"), 1)
            pe.wait_ge(S("xt_lo"), 2 * NC)
            pe.wait_ge(S("w_lo"), 2)
            def keys_values(b):
                if b:
                    pe.wait_ge(S("kv_z"), b)
                for t in range(4):
                    o = (4 * b + t) * P
                    for k in range(KD):
                        ins = three(ps[:, t, :], ht_hi[:, k, o:o + P], ht_lo[:, k, o:o + P], wkv_hi[:, k], wkv_lo[:, k], k == 0, k == KD - 1)
                ins.then_inc(S("kv"), 1)

            keys_values(0)
            for b in range(NT // 4 + 1):
                if b < NT // 4:
                    g0 = sum(G_BATCH) * b
                    sums(g0, G_BATCH[0])
                else:
                    sums(FOLD0, G_FOLD[0])
                if b:
                    pe.wait_ge(S("k_ready"), b)
                    pe.wait_ge(S("keycols"), 1)
                    for t in range(4):
                        n = P if 4 * (b - 1) + t < NT - 1 else LAST
                        first, last = b == 1 and t == 0, b == NT // 4 and t == 3
                        for G in range(KD):
                            ins = pe.matmul(ps[:, 4 + G, 0:P + 1], kv_n[0:n, t, G * P:(G + 1) * P], kv_n[0:n, t, D + G * (P + 1):D + (G + 1) * (P + 1)], start=first, stop=last)
                    ins.then_inc(S("kv_used"), 1)
                if b < NT // 4:
                    sums(g0 + G_BATCH[0], G_BATCH[1])
                    if b + 1 < NT // 4:
                        keys_values(b + 1)
                    sums(g0 + sum(G_BATCH[:2]), G_BATCH[2])
            pe.wait_ge(S("kvm"), 1)
            for G in range(KD):
                ins = pe.matmul(ps[:, 2 + G, 0:D + 1], kvm[:, G], wqT[:, G], start=True, stop=True)
            ins.then_inc(S("mT"), 1)
            sums(FOLD0 + G_FOLD[0], G_FOLD[1])
            pe.wait_ge(S("mT_in"), 1)
            pe.wait_ge(S("w1_in"), 16)
            for k in range(KD):
                for G in range(KD):
                    pe.matmul(ps[:, 0, k * D:(k + 1) * D], mT[:, G, k * P:(k + 1) * P], w1[:, G], start=G == 0, stop=G == KD - 1)
            for j in range(KD):
                for G in range(KD):
                    ins = pe.matmul(ps[:, 1, j:j + 1], w1[:, G, j * P:(j + 1) * P], retb[:, G:G + 1], start=G == 0, stop=G == KD - 1)
            ins.then_inc(S("m1"), 1)
            sums(FOLD0 + sum(G_FOLD[:2]), G_FOLD[2])
            pe.wait_ge(S("m1_lo"), 1)
            for i in range(2 * NC):
                c, f = divmod(i, 2)
                if i >= 4:
                    pe.wait_ge(S("h1f"), i - 3)
                for k in range(KD):
                    fs, cs = slice(f * P, (f + 1) * P), slice(c * 512, (c + 1) * 512)
                    ins = three(ps[:, 2 + i % 4, :], m1_hi[:, k, fs], m1_lo[:, k, fs], ht_hi[:, k, cs], ht_lo[:, k, cs], k == 0, k == KD - 1)
                ins.then_inc(S("h1"), 1)
                if f == 1:
                    sums(H10 + G_H1 * c, G_H1)
                if i in (3, 7):
                    degrees(i // 4)
            pe.wait_ge(S("h1_lo"), 2 * NC)
            for t in range(NT):
                if t >= 3:
                    pe.wait_ge(S("mix_acc"), t - 2)
                for k in range(KD):
                    n = slice(t * P, (t + 1) * P)
                    ins = three(ps[:, OUT_BANK[t % 3], 0:D], h1_hi[:, k, n], h1_lo[:, k, n], w2_hi[:, k], w2_lo[:, k], k == 0, k == KD - 1)
                ins.then_inc(S("mix_out"), 1)
                if t % 2:
                    sums(OUT0 + G_OUT * (t // 2), G_OUT)
                if t == 11:
                    degrees(2)
            pe.wait_ge(S("mix_acc"), NT)
            sums(LAST0, NG - LAST0)
            degrees(3)
            degrees(4)
            barrier(pe)
            with pe.If(unsorted(pe) > 0):
                pe.wait_ge(S("any_zero"), 1)
                with pe.Fori(0, PASSES) as q:
                    pe.wait_ge(S("any_keys"), q + 1)
                    for b in range(2):
                        for j in range(3):
                            o = j * NG + b * GB
                            pe.transpose(ps[:, 4, o:o + GB], any_c[0:GB, b, j * P:(j + 1) * P], ident[0:GB, 0:GB])
                            ins = pe.transpose(ps[:, 5, o:o + GB], any_lo[0:GB, j * P:(j + 1) * P], ident[0:GB, 0:GB])
                    ins.then_inc(S("any_keysT"), 1)
                    for c in range(NC):
                        with pe.Fori(0, GC) as gi:
                            pe.wait_ge(S("any_hot"), NG * q + GC * c + gi + 1)
                            pe.matmul(ps[:, 0, 0:KEYS].rearrange("p (s d) -> p s d", d=GW), ident16, at[:, c * NT:(c + 1) * NT, bass.ds(GW * gi, GW)], start=True, stop=False)
                            for j in range(3):
                                ins = pe.matmul(ps[:, 0, 0:KEYS], src_hot[:, 0, :, j], key_hot[:, 0, j, :], start=False, stop=j == 2)
                            ins.then_inc(S("any_sum"), 1)
                pe.wait_ge(S("any_out"), NG * PASSES + 1)
                for c in range(NC):
                    degrees(c)
            pe.nop()
            barrier(pe)
            for l in range(3):
                with pe.Fori(0, NC) as c:
                    if l:
                        pe.wait_ge(S("h_lo"), 2 * NC * (l - 1) + 2 * c + 6)
                        pe.wait_ge(S("mean"), 2 * NC * l - 2)
                    for u in range(4):
                        t = 4 * c + u
                        if l == 0:
                            pe.wait_ge(S("rcnt"), u + 1)
                        if l and u == 2:
                            pe.wait_ge(S("mean"), 2 * NC * l)
                        pe.wait_ge(S("g_lo"), NT * l + t + 1)
                        n = bass.ds(t * P, P)
                        for k in range(KD):
                            wbh, wbl = (w[:, l, k].rearrange("p w d -> p (w d)") for w in (wbf_hi, wbf_lo))
                            ins = three(ps[:, BANK[u], :], ht_hi[:, k, n], ht_lo[:, k, n], wbh, wbl, k == 0, k == KD - 1)
                        ins.then_inc(S("g"), 1)
                with pe.Fori(0, NC) as c:
                    cs = bass.ds(c * 512, 512)
                    pe.wait_ge(S("h_lo"), 2 * (NC * l + c) + 2)
                    for f in range(2):
                        fs = slice(f * P, (f + 1) * P)
                        for k in range(KD):
                            ins = three(ps[:, bass.ds(4 + 2 * (c % 2) + f, 1), :], wd_hi[:, l, k, fs], wd_lo[:, l, k, fs], ht_hi[:, k:k + 1, cs], ht_lo[:, k:k + 1, cs], k == 0, k == KD - 1)
                    ins.then_inc(S("own_sum"), 1)
                    pe.wait_ge(S("g_lo"), NT * (l + 1) + 4)
                    for s_ in range(NT):
                        for f in range(2):
                            for part, g_ in enumerate((g_hi, g_lo)):
                                ins = pe.matmul(ps[:, bass.ds(2 * (c % 2) + f, 1), :], g_[:, s_, f * P:(f + 1) * P], at[:, bass.ds(c * NT + s_, 1), :],
                                                start=s_ == 0 and part == 0, stop=s_ == NT - 1 and part == 1)
                    ins.then_inc(S("agg"), 1)
            for t in range(NT):
                if t % 4 == 0:
                    pe.wait_ge(S("h_lo"), 2 * NC * 2 + 2 * (t // 4) + 6)
                if t % 4 == 0:
                    pe.wait_ge(S("mean"), 2 * NC * 3 - 2)
                if t % 4 == 2:
                    pe.wait_ge(S("mean"), 2 * NC * 3)
                pe.wait_ge(S("f3_acc"), t + 1)
                n = slice(t * P, (t + 1) * P)
                for k in range(KD):
                    ins = three(ps[:, BANK[t % 4], 0:D], ht_hi[:, k, n], ht_lo[:, k, n], wf3_hi[:, k], wf3_lo[:, k], k == 0, k == KD - 1)
                ins.then_inc(S("f3"), 1)
            barrier(pe)
            pe.wait_ge(S("wr_in"), 32)
            for t in range(NT + 1):
                if t < NT:
                    pe.wait_ge(S("y"), t + 1)
                    if t >= 2:
                        pe.wait_ge(S("yT_in"), t - 1)
                    for k in range(KD):
                        ins = pe.transpose(ps[:, t % 2, k * P:(k + 1) * P], xn2[:, t, k * P:(k + 1) * P], ident)
                    ins.then_inc(S("yT"), 1)
                if t:
                    pe.wait_ge(S("yT_in"), t)
                    for k in range(KD):
                        ins = pe.matmul(ps[:, 2, (t - 1) * NE:t * NE], yT[:, (t - 1) % 2, k], wr[:, k], start=k == 0, stop=k == KD - 1)
                    ins.then_inc(S("logits"), 1)
            pe.wait_ge(S("hot12"), 1)
            h12 = hot12.rearrange("p t e -> p (t e)")
            pe.matmul(ps[:, 3, 0:NT * NE], below, h12, start=True, stop=True)
            pe.matmul(ps[:, 4, 0:NT * NE], ones, h12, start=True, stop=True).then_inc(S("ranks"), 1)
            pe.sem_inc(S("e_turned"), 2)
            pe.sem_inc(S("e_h"), 2)
            pe.sem_inc(S("e_yp"), 2)
            barrier(pe)

            def turn(b, bb, u):
                pe.wait_ge(S(f"e_x{u}"), 16 * (bb + 1))
                pe.wait_ge(S("e_xe"), b + 1)
                for k in range(KD):
                    ins = pe.transpose(ps[:, 4 + u, k * P:(k + 1) * P], x_in[:, u, k * P:(k + 1) * P], ident)
                ins.then_inc(S("e_turned"), 1)

            def hidden(b, u):
                pe.wait_ge(S("e_w1"), b + 1)
                pe.wait_ge(S("e_xe"), b + 3)
                pe.wait_ge(S("e_gelu"), b + 1)
                for j in range(KH):
                    for k in range(KD):
                        js = slice(j * P, (j + 1) * P)
                        ins = three(ps[:, 2 * u + j // 4, (j % 4) * P:(j % 4 + 1) * P], w1_now[:, u, 0, k, js], w1_now[:, u, 1, k, js],
                                    xe_hi[:, u, k], xe_lo[:, u, k], k == 0, k == KD - 1)
                ins.then_inc(S("e_h"), 1)

            def outward(b, u):
                e = pe.value_load(blk_e[0:1, bass.ds(b, 1)], min_val=0, max_val=NE - 1)
                pe.wait_ge(S("e_lo"), b + 3)
                pe.wait_ge(S("e_out"), b + 1)
                for j in range(KH):
                    o = e * EWN + j * D
                    ins = three(ps[:, 6 + u, 0:D], h_hi[:, u, j], h_lo[:, u, j], mem[:, bass.ds(o + W2_HI, D)], mem[:, bass.ds(o + W2_LO, D)],
                                j == 0, j == KH - 1)
                ins.then_inc(S("e_yp"), 1)

            turn(0, 0, 0)
            turn(1, 0, 1)
            hidden(0, 0)
            with pe.Fori(0, NPAIR - 1) as bb:
                turn(2 * bb + 2, bb + 1, 0)
                hidden(2 * bb + 1, 1)
                outward(2 * bb, 0)
                turn(2 * bb + 3, bb + 1, 1)
                hidden(2 * bb + 2, 0)
                outward(2 * bb + 1, 1)
            turn(NB - 1, NPAIR, 0)
            hidden(NB - 2, 1)
            outward(NB - 3, 0)
            hidden(NB - 1, 0)
            outward(NB - 2, 1)
            outward(NB - 1, 0)
            barrier(pe)



def lay_out(inputs):
    arrays = {k: np.ascontiguousarray(v) for k, v in inputs.items() if k not in ("src", "dst")}
    src, dst = np.asarray(inputs["src"]), np.asarray(inputs["dst"])
    size = STEP * (NWIN - 1) + WIN
    src_p = np.concatenate([src, np.zeros(size - E_ALL, src.dtype)])
    dst_p = np.concatenate([dst, np.full(size - E_ALL, NOWHERE, dst.dtype)])
    arrays["srcw"] = np.stack([src_p[i:i + WIN] for i in range(0, STEP * NWIN, STEP)])
    arrays["dstw"] = np.stack([dst_p[i:i + WIN] for i in range(0, STEP * NWIN, STEP)])
    arrays["dsamp"] = np.ascontiguousarray(dst_p[:STEP * NWIN:STEP].reshape(P, NS))
    arrays["dpair"] = np.stack([dst_p[i:i + EC + 1] for i in range(0, EC * P, EC)])
    return arrays


def kernel(**inputs):
    import concourse.bacc as bacc
    from concourse.bass_utils import run_bass_kernel_spmd

    nc = bacc.Bacc("TRN2", target_bir_lowering=False, num_devices=1)
    arrays = lay_out(inputs)
    aps = {k: nc.dram_tensor(k, a.shape, mybir.dt.from_np(a.dtype), kind="ExternalInput").ap() for k, a in arrays.items()}
    out = nc.dram_tensor("out", (N, D), F32, kind="ExternalOutput").ap()
    build(nc, aps, out)
    r = run_bass_kernel_spmd(nc, [arrays], core_ids=[0])
    return r.results[0]["out"]
```

```python
import contextlib

import numpy as np

import concourse.bass as bass
from concourse import mybir

ALU = mybir.AluOpType
ACT = mybir.ActivationFunctionType
AX_X = mybir.AxisListType.X
F32, F16 = mybir.dt.float32, mybir.dt.float16
I32, U32 = mybir.dt.int32, mybir.dt.uint32

P = 128
N = 2500
D = 256
KD = D // P
NT = (N + P - 1) // P
NP = NT * P
LAST = N - (NT - 1) * P
NC = NP // 512
LASTC = N - (NC - 1) * 512
E_ALL = 42500
NOWHERE = 4095

GW = 16
NG = NP // GW
GB = NG // 2
STEP = 16
WIN = 3 * P
NWIN = 2688
NS = NWIN // P
EC = (E_ALL + P - 1) // P
KEYS = NT * GW
PASSES = (E_ALL + WIN - 1) // WIN
GC = 512 // GW
SETS = 4

HEADS = 8
HC = D // HEADS
NE = 8
H = 1024
KH = H // P
TOPK = 2
NB = (TOPK * N + NE * (P - 1)) // P
SLOTS = NB * P
NB_MAIN = 44
EPS = 1e-5
WS = 64.0

AT_B = NT * NP * 2
HALF = KD * NP * 2


def split_memory(mem):
    def view(off, dims, dt):
        size = 4 if dt in (F32, I32, U32) else 2
        n = int(np.prod(dims))
        v = mem[:, off // 2:(off + n * size) // 2]
        if dt != F16:
            v = v.bitcast(dt)
        if len(dims) == 2:
            v = v.rearrange("p (a b) -> p a b", b=dims[1])
        elif len(dims) == 3:
            v = v.rearrange("p (a b c) -> p a b c", b=dims[1], c=dims[2])
        elif len(dims) == 4:
            v = v.rearrange("p (a b c d) -> p a b c d", b=dims[1], c=dims[2], d=dims[3])
        return v
    return view


def build(nc, I, out):
    ctx = contextlib.ExitStack()
    with ctx:
        ctx.enter_context(nc.allow_non_contiguous_dma(reason="small parameter rows"))
        TOP = 211968
        mem = ctx.enter_context(nc.sbuf_tensor("mem", [P, TOP // 2], F16))
        view = split_memory(mem)
        ps = ctx.enter_context(nc.psum_tensor("ps", [P, 8, 512], F32))

        names = {}

        def S(name):
            if name not in names:
                names[name] = ctx.enter_context(nc.semaphore(name))
            return names[name]

        xrows = nc.dram_tensor("xrows", (NP, D), F32).ap()
        yrows = nc.dram_tensor("yrows", (TOPK * NP + SLOTS, D), F32).ap()

        off = 0
        at = view(0, [NC * NT, 512], F16)
        ht_hi = view(AT_B, [KD, NP], F16)
        ht_lo = view(AT_B + HALF, [KD, NP], F16)
        g_hi = view(AT_B + 2 * HALF, [NT, D], F16)
        g_lo = view(AT_B + 3 * HALF, [NT, D], F16)
        h1_hi = view(AT_B + 2 * HALF, [KD, NP], F16)
        h1_lo = view(AT_B + 3 * HALF, [KD, NP], F16)
        xn = view(AT_B + 2 * HALF, [NT, D], F32)
        ACC_B = AT_B + 4 * HALF
        acc = view(ACC_B, [NT, D], F32)
        WR_B = ACC_B + NT * D * 4
        wd_hi = view(WR_B, [3, KD, D], F16)
        wd_lo = view(WR_B + 3072, [3, KD, D], F16)
        wbf_hi = view(WR_B + 6144, [3, KD, 2, D], F16)
        wbf_lo = view(WR_B + 12288, [3, KD, 2, D], F16)
        wf3_hi = view(WR_B + 18432, [KD, D], F16)
        wf3_lo = view(WR_B + 19456, [KD, D], F16)
        w2_hi = view(WR_B + 20480, [KD, D], F16)
        w2_lo = view(WR_B + 21504, [KD, D], F16)
        m1_hi = view(WR_B + 22528, [KD, D], F16)
        m1_lo = view(WR_B + 23552, [KD, D], F16)
        RC_B = WR_B + 24576
        rcnt = view(RC_B, [NP], F32)
        has = view(RC_B + 10240, [NP], F16)
        src_hot = view(RC_B, [SETS // 2, P, 6], F16)
        key_hot = view(RC_B + SETS * 768, [SETS, 3, KEYS], F16)
        iota_key = view(RC_B + SETS * 2688, [KEYS], F16)
        iota_p = view(RC_B + SETS * 2688 + 640, [P, 6], F16)
        key_now = view(RC_B + SETS * 2688 + 640 + 1536, [3, SETS], F32)
        lo_now = view(RC_B + SETS * 2688 + 640 + 1536 + SETS * 12, [SETS // 2, 6], F16)
        assert SETS * 2688 + 640 + 1536 + SETS * 18 <= 15360
        C_B = RC_B + 15360
        cols_t = view(C_B + 2720 + 768, [6, NG], F32)
        key_t, lo_t = cols_t[:, 0:3], cols_t[:, 3:6]
        R_B0 = C_B + 2720
        ident = view(C_B, [P], F32)
        ones = view(C_B + 512, [P], F32)
        below = view(C_B + 1024, [P], F32)
        cols = view(C_B + 1536, [P], F32)
        ones16 = view(C_B + 2048, [2], F16)
        mv = view(C_B + 2112, [NT, 2], F32)
        rstd = view(C_B + 2304, [NT], F32)
        grp = view(C_B + 2400, [2], F32)
        cnts = view(C_B + 2416, [4], F32)
        excess = view(C_B + 2432, [2], F32)
        viol = view(C_B + 2440, [1], F32)
        widx = view(C_B + 2448, [2], U32)
        bad = view(C_B + 2456, [1], I32)
        eps = view(C_B + 2464, [1], F32)
        iota8 = view(C_B + 2496, [NE], F32)
        onesq = view(R_B0, [P], F16)
        any_s, any_d = view(AT_B + 2 * HALF, [WIN], I32), view(AT_B + 2 * HALF + 1536, [WIN], I32)
        any_k, any_lo = view(AT_B + 2 * HALF + 3072, [WIN], F32), view(AT_B + 2 * HALF + 4608, [WIN], F32)
        any_a, any_b, any_c = (view(AT_B + 2 * HALF + 6144 + 3072 * i, [2, WIN], F32) for i in range(3))
        any_i = view(AT_B + 2 * HALF + 15360, [WIN], I32)
        ident16 = view(AT_B + 2 * HALF + 17408, [P], F16)
        blockdiag = view(R_B0 + 256, [P], F32)
        onecol = view(C_B + 2528, [1], F32)
        b1p = view(C_B + 2536, [KD], F32)
        retb = view(C_B + 2544, [KD], F32)
        nmr = view(C_B + 2560, [NT], F32)
        std = view(C_B + 2640, [NT], F32)
        R_B = C_B + 2720 + 768
        tmp_t = view(R_B, [2, 512], F32)
        tmp_p = view(WR_B + 20480, [2, 512], F32)

        spot, end = [0], [0]

        def temp(dims, dt):
            v = view(spot[0], dims, dt)
            spot[0] += -(-int(np.prod(dims)) * (2 if dt == F16 else 4) // 32) * 32
            assert spot[0] <= end[0]
            return v

        CHUNK = NT * 512 * 2
        end[0] = 3 * CHUNK
        stg = temp([3, 6, D], F32)
        stg3 = temp([KD, D], F32)
        stgw2 = temp([KD, D], F32)
        wqkv = temp([KD, 3 * D], F32)
        wkvc = temp([KD, 512], F32)
        wq = temp([KD, D], F32)
        bkv = temp([512], F32)
        bout = temp([2, D], F32)
        msum = temp([KD, 16], F32)
        bsum = temp([16], F32)
        stack = temp([P], F32)
        samp_i = temp([NS], I32)
        samp = temp([NS], F32)
        lt = temp([NS, NG + 2], F16)
        bounds = temp([NG + 2], F16)
        pair = temp([EC + 1], I32)
        cmp = temp([EC], F32)
        win_s = temp([2, WIN], I32)
        win_d = temp([2, WIN], I32)
        spot[0], end[0] = 3 * CHUNK, 4 * CHUNK
        kv_z = temp([4, 512], F32)
        kv_n = temp([4, 514], F32)
        wkv_hi = temp([KD, 512], F16)
        spot[0], end[0] = 4 * CHUNK, 5 * CHUNK
        kv_sq = temp([4, 512], F32)
        h1f = view(4 * CHUNK, [2, 512], F32)
        kvt = view(4 * CHUNK + 4096, [KD, P], F32)
        mT = view(4 * CHUNK + 5120, [KD, D + 1], F32)
        wkv_lo = temp([KD, 512], F16)
        w1 = temp([KD, D], F32)
        wqT = temp([KD, D + 1], F32)
        bias_kv = temp([512], F32)
        gbkv = temp([4, HC], F32)
        kvm = temp([KD, P], F32)
        sk = temp([KD], F32)
        kst = temp([4, 16], F32)
        kst2 = temp([4, 16], F32)
        ka, kb, kc, klo = (view(i * 3072, [2, WIN], F32) for i in range(4))
        ki = view(4 * 3072, [2, WIN], I32)
        st6 = view(R_B, [NT, 6], F32)

        EW = 16384
        w_e = [[view(EW * e, [KD, H], F16), view(EW * e + 4096, [KD, H], F16),
                view(EW * e + 8192, [KH, D], F16), view(EW * e + 12288, [KH, D], F16)] for e in range(NE)]
        W1_HI, W1_LO, W2_HI, W2_LO = (i * 2048 for i in range(4))
        EWN = EW // 2
        b2_all = view(NE * EW, [NE, D], F32)
        ew_raw = [view(8192 * i + 12288, [2048], F32) for i in range(2 * NE)]
        assert 8192 * (2 * NE - 1) + 12288 + 8192 <= ACC_B
        RAW_IN_AT = (AT_B - 12288) // 8192
        rt = [RC_B]

        def small(dims, dt=F32):
            v = view(rt[0], dims, dt)
            rt[0] += -(-int(np.prod(dims)) * 4 // 32) * 32
            return v

        logit, mx = small([NT, NE]), small([NT, NE])
        hot1, hot2, hot12 = small([NT, NE]), small([NT, NE]), small([NT, NE])
        top = small([NT, NE], U32)
        iota_pos, iota_blk, y_free, node = small([P]), small([NB]), small([NB]), small([TOPK, NT])
        TQ = 4 * TOPK
        place_hot = [view(WR_B + 20480, [TQ, P], F32), small([TQ, P])]
        blk_hot = [small([TQ, NB]), small([TQ, NB])]
        slot_i, place_f, slot_blk = small([TOPK, NT], I32), small([TOPK, NT]), small([TOPK, NT])
        found, second, unused = small([NB]), small([NB]), small([NB])
        assert rt[0] <= RC_B + 13824
        rt[0] = R_B
        tot_a, tot_b, rank = small([NT, NE]), small([NT, NE]), small([NT, NE])
        topf = small([NT, 2])
        slot_f, slot = small([TOPK, NT]), small([TOPK, NT], I32)
        wgt = small([TOPK, NT])
        nblk, cum, cum2, base = small([NE]), small([NE]), small([NE]), small([NE])
        nblk_i = small([NE], I32)
        valid = small([1])
        blk = small([NB])
        blk_e = small([NB], I32)
        blk_n = small([1], I32)
        x_row, y_row = small([NB], U32), small([NB], U32)
        assert rt[0] <= R_B + 4096, rt[0]
        assert NB_MAIN % 2 == 0
        wr, br = view(R_B + 4096, [KD, NE], F32), view(R_B + 4096 + 64, [NE], F32)
        blk_ge = view(RC_B + 13824, [NB, NE], F32)
        xn2 = view(WR_B, [NT, D], F32)
        yT = view(WR_B + 20480, [2, 2 * KD, P], F32)
        xe = view(WR_B, [KD, P], F32)
        xe_hi, xe_lo = view(WR_B + 1024, [2, KD, P], F16), view(WR_B + 2048, [2, KD, P], F16)
        hf = view(WR_B + 3072, [2, KH, P], F32)
        h_hi, h_lo = view(WR_B + 11264, [2, KH, P], F16), view(WR_B + 15360, [2, KH, P], F16)
        x_in, y_out = view(WR_B + 19456, [2, D], F32), view(WR_B + 21504, [2, D], F32)
        w1_now = view(WR_B + 23552, [2, 2, KD, H], F16)
        assert WR_B + 23552 + 16384 <= C_B
        y1, y2 = view(0, [NT, D], F32), view(NT * D * 4, [NT, D], F32)

        PHASES1 = 3
        NPAIR = NB_MAIN // 2
        BIAS_DMAS = 8
        Y_DVE = 8
        STD_AT = 3
        SPLIT_AFTER = ((), (), (0, 1), (2, 3, 4, 5))
        IN_LAYER = sum(len(p) for p in SPLIT_AFTER)
        BESIDE = min(NC, 2 * NE - IN_LAYER - 5)
        EARLY = 5
        X_PARTS = ((0, 6), (6, 13), (13, NT - 1))
        DEG_BANK = (0, 1, 4, 2, 3)
        X_BANK = (2, 3, 6, 7)
        G_BATCH, G_FOLD, G_H1, G_OUT = (8, 4, 4), (8, 4, 4), 4, 4
        OUT_BANK = (2, 3, 5)
        FOLD0 = sum(G_BATCH) * (NT // 4)
        H10 = FOLD0 + sum(G_FOLD)
        OUT0 = H10 + G_H1 * NC
        LAST0 = OUT0 + G_OUT * (NT // 2)
        assert H10 == 3 * GC and OUT0 % SETS == 0 and LAST0 < NG
        BANK = (2, 3, 0, 1)

        def barrier(e):
            NBAR_i[e] = NBAR_i.get(e, 0) + 1
            e.drain().then_inc(S("phase"), 1)
            e.wait_ge(S("phase"), 5 * NBAR_i[e])
        NBAR_i = {}

        def unsorted(e):
            return e.value_load(bad[0:1, 0:1], min_val=0, max_val=1 << 20)

        def blocks(e):
            return e.value_load(blk_n[0:1, 0:1], min_val=0, max_val=NB)

        block = ctx.enter_context(nc.Block())

        HALF_LIST = [(wd_hi[:, l], wd_lo[:, l], stg[:, l, 0:2]) for l in range(3)]
        HALF_LIST += [(wbf_hi[:, l, :, w], wbf_lo[:, l, :, w], stg[:, l, 2 + 2 * w:4 + 2 * w]) for l in range(3) for w in range(2)]
        HALF_LIST += [(wf3_hi, wf3_lo, stg3), (w2_hi, w2_lo, stgw2), (wkv_hi, wkv_lo, wkvc)]
        NSPLIT = len(HALF_LIST)

        def heads(v, first, n=8):
            return v.rearrange("p (h c) -> p h c", c=HC)

        def bc(v, dims):
            return v.to_broadcast(dims)

        @block.sync
        def _(sp):
            x = I["x"]
            sp.dma_start(samp_i, I["dsamp"]).then_inc(S("samp_in"), 16)
            sp.dma_start(pair, I["dpair"]).then_inc(S("pair_in"), 16)
            for q, (t0, t1) in enumerate(X_PARTS):
                sp.dma_start(acc[:, t0:t1, :], x[t0 * P:t1 * P, :].rearrange("(t p) d -> p t d", p=P)).then_inc(S(f"x_in{q}"), 16)
            sp.wait_ge(S("pad0"), 1)
            sp.dma_start(acc[0:LAST, NT - 1, :], x[(NT - 1) * P:N, :]).then_inc(S(f"x_in{len(X_PARTS) - 1}"), 16)
            sp.dma_start(wqkv, I["L0_mix_w_qkv"].rearrange("(r p) d -> p r d", p=P)).then_inc(S("wqkv_in"), 16)
            sp.dma_start(w1, I["L0_mix_w1"].rearrange("(r p) d -> p r d", p=P)).then_inc(S("w1_in"), 16)
            for l in range(3):
                sp.dma_start(stg[:, l, 0:4, :], I[f"L0_gnn_W{l}"].rearrange("(r p) d -> p r d", p=P)).then_inc(S("w_in"), 16)
                sp.dma_start(stg[:, l, 4:6, :], I["L0_gnn_Wf"][l * D:(l + 1) * D, :].rearrange("(r p) d -> p r d", p=P)).then_inc(S("w_in"), 16)
            sp.dma_start(stg3, I["L0_gnn_Wf"][3 * D:4 * D, :].rearrange("(r p) d -> p r d", p=P)).then_inc(S("w_in"), 16)
            sp.dma_start(stgw2, I["L0_mix_w2"].rearrange("(r p) d -> p r d", p=P)).then_inc(S("w_in"), 16)
            barrier(sp)
            with sp.If(unsorted(sp) > 0):
                with sp.Fori(0, PASSES) as q:
                    sp.wait_ge(S("any_read"), q + 1)
                    for tab, dst in ((I["srcw"], any_s), (I["dstw"], any_d)):
                        sp.dma_start(dst[0:GB], tab[bass.ds(q * (WIN // STEP), 1), :].to_broadcast([GB, WIN])).then_inc(S("any_in"), 16)
            sp.nop()
            barrier(sp)
            sp.dma_start(wr, I["L0_ffn_Wr"].rearrange("(k p) e -> p k e", p=P)).then_inc(S("wr_in"), 16)
            sp.dma_start(br, I["L0_ffn_br"].partition_broadcast(P)).then_inc(S("wr_in"), 16)
            for i in range(2 * NE):
                e, w = divmod(i, 2)
                if i < RAW_IN_AT:
                    sp.wait_ge(S("agg"), 2 * NC + -(-(8192 * i + 12288 + 8192) // (AT_B // NC)))
                if i == RAW_IN_AT:
                    sp.wait_ge(S("f3"), NT)
                src = (I["L0_ffn_W1"], I["L0_ffn_W2"])[w][e].rearrange("(k p) n -> p k n", p=P)
                sp.dma_start(ew_raw[i].rearrange("p (k n) -> p k n", k=(KD, KH)[w]), src).then_inc(S(f"ew_in{e}"), 16)
            barrier(sp)
            for q in range(NC):
                sp.wait_ge(S("xn2"), 4 * (q + 1))
                sp.dma_start(xrows[q * 512:(q + 1) * 512, :].rearrange("(t p) d -> p t d", p=P), xn2[:, 4 * q:4 * q + 4, :]).then_inc(S("xrows"), 16)
            sp.wait_ge(S("ew_lo"), 2 * NE)
            sp.dma_start(b2_all, I["L0_ffn_b2"].rearrange("e d -> (e d)").partition_broadcast(P)).then_inc(S("b2_in"), 16)
            barrier(sp)

            barrier(sp)
            for c in range(NC):
                for q, y_ in enumerate((y1, y2)):
                    rows = min(512, N - c * 512)
                    full = rows // P
                    r0 = q * NP + c * 512
                    sp.dma_start(y_[:, 4 * c:4 * c + full, :], yrows[r0:r0 + full * P, :].rearrange("(t p) d -> p t d", p=P)).then_inc(S(f"y_in{c}"), 16)
                    if rows % P:
                        sp.dma_start(y_[0:LAST, NT - 1, :], yrows[r0 + full * P:r0 + rows, :]).then_inc(S(f"y_in{c}"), 16)
            for c in range(NC):
                sp.wait_ge(S("final"), 4 * (c + 1))
                if c < NC - 1:
                    sp.dma_start(out[c * 512:(c + 1) * 512, :].rearrange("(t p) d -> p t d", p=P), acc[:, 4 * c:4 * c + 4, :]).then_inc(S("out"), 16)
            sp.dma_start(out[4 * (NC - 1) * P:(NT - 1) * P, :].rearrange("(t p) d -> p t d", p=P), acc[:, 4 * (NC - 1):NT - 1, :]).then_inc(S("out"), 16)
            sp.dma_start(out[(NT - 1) * P:N, :], acc[0:LAST, NT - 1, :]).then_inc(S("out"), 16)
            sp.wait_ge(S("out"), 16 * (NC + 1))

        @block.gpsimd
        def _(pool):
            pool.memset(ident, 0.0)
            pool.memset(below, 1.0)
            pool.memset(ones, 1.0)
            pool.memset(ones16, 1.0)
            pool.memset(onesq, 1.0)
            pool.memset(kv_n[:, :, D + P:D + P + 1], 1.0)
            pool.memset(kv_n[:, :, D + 2 * P + 1:D + 2 * P + 2], 1.0)
            pool.memset(blockdiag, 1.0 / N)
            pool.memset(stack, 0.0)
            pool.memset(eps, EPS).then_inc(S("fill"), 1)
            pool.iota(bounds, [[GW, NG + 2]], base=0, channel_multiplier=0, allow_small_or_imprecise_dtypes=True)
            pool.iota(iota_key, [[1, KEYS]], base=1, channel_multiplier=0, allow_small_or_imprecise_dtypes=True)
            pool.iota(iota_p, [[1, P], [0, 6]], base=0, channel_multiplier=0, allow_small_or_imprecise_dtypes=True)
            pool.iota(iota8, [[1, NE]], base=0, channel_multiplier=0, allow_small_or_imprecise_dtypes=True)
            pool.iota(grp, [[-GW * GB, 2]], base=0, channel_multiplier=-GW, allow_small_or_imprecise_dtypes=True)
            pool.wait_ge(S("fill"), 1)
            pool.affine_select(out=ident, in_=ident, compare_op=ALU.not_equal, fill=1.0, base=0,
                               pattern=[[-1, P]], channel_multiplier=1)
            bd = blockdiag.rearrange("p (a c) -> p a c", c=HC)
            pool.affine_select(out=bd, in_=bd, compare_op=ALU.is_ge, fill=0.0, base=0,
                               pattern=[[-HC, 4], [0, HC]], channel_multiplier=1).then_inc(S("fill"), 1)
            pool.wait_ge(S("fill"), 2)
            pool.affine_select(out=bd, in_=bd, compare_op=ALU.is_ge, fill=0.0, base=HC - 1,
                               pattern=[[HC, 4], [0, HC]], channel_multiplier=-1)
            pool.affine_select(out=below, in_=below, compare_op=ALU.is_gt, fill=0.0, base=0,
                               pattern=[[1, P]], channel_multiplier=-1).then_inc(S("consts"), 1)
            pool.wait_ge(S("widx"), 1)
            for b in range(2):
                for tab, dst in ((I["srcw"], win_s), (I["dstw"], win_d)):
                    pool.indirect_dma_start(out=dst[0:GB, b, :], out_offset=None, in_=tab,
                                            in_offset=bass.IndirectOffsetOnAxis(ap=widx[0:GB, b:b + 1], axis=0)).then_inc(S("win_in"), 16)
            pool.wait_ge(S("w_in"), 128)
            for l in range(3):
                pool.tensor_tensor(stg[:, l, 0:2], stg[:, l, 0:2], stg[:, l, 2:4], ALU.subtract).then_inc(S("wd"), 1)
            pool.wait_ge(S("xn"), 1)
            pool.tensor_tensor(acc, acc, xn, ALU.add).then_inc(S("acc"), 1)
            pool.wait_ge(S("bias_in"), 16 * BIAS_DMAS)
            pool.tensor_tensor(bout[:, 0], bout[:, 0], bout[:, 1], ALU.add).then_inc(S("acc"), 1)
            pool.wait_ge(S("acc"), 2)
            pool.tensor_tensor(acc, acc, bout[:, 0:1, :].to_broadcast([P, NT, D]), ALU.add).then_inc(S("acc"), 1)
            for b in range(NT // 4):
                pool.wait_ge(S("kn"), b + 1)
                for t in range(4):
                    k3 = kv_n[:, t, 0:256].rearrange("p (h c) -> p h c", c=HC)
                    ins = pool.tensor_tensor(k3, k3, gbkv[:, 0:1, :].to_broadcast([P, HEADS, HC]), ALU.mult)
                ins.then_inc(S("kg"), 1)
                pool.wait_ge(S("kg"), b + 1)
                for t in range(4):
                    k3 = kv_n[:, t, 0:256].rearrange("p (h c) -> p h c", c=HC)
                    ins = pool.tensor_tensor(k3, k3, gbkv[:, 1:2, :].to_broadcast([P, HEADS, HC]), ALU.add)
                ins.then_inc(S("k_ready"), 1)
            barrier(pool)
            barrier(pool)
            with pool.Fori(0, 3) as l:
                for c in range(NC):
                    for f in range(2):
                        n = 512 if c < NC - 1 else LASTC
                        pool.wait_ge(S("own"), 2 * NC * l + 2 * c + f + 1)
                        pool.tensor_tensor(tmp_p[:, f, 0:n], tmp_p[:, f, 0:n], has[:, c * 512:c * 512 + n], ALU.mult).then_inc(S("own_has"), 1)
            barrier(pool)
            pool.iota(blk, [[1, NB]], base=0, channel_multiplier=0, allow_small_or_imprecise_dtypes=True)
            pool.iota(iota_pos, [[1, P]], base=0, channel_multiplier=0, allow_small_or_imprecise_dtypes=True)
            pool.iota(iota_blk, [[1, NB]], base=0, channel_multiplier=0, allow_small_or_imprecise_dtypes=True)
            pool.iota(y_free, [[P, NB]], base=TOPK * NP + 1, channel_multiplier=1, allow_small_or_imprecise_dtypes=True)
            pool.iota(node, [[NP, TOPK], [P, NT]], base=1, channel_multiplier=1, allow_small_or_imprecise_dtypes=True)
            pool.iota(valid, [[0, 1]], base=0, channel_multiplier=1, allow_small_or_imprecise_dtypes=True).then_inc(S("blk"), 1)

            def gather(b):
                pool.wait_ge(S("e_turned"), b + 1)
                pool.indirect_dma_start(out=x_in[:, b % 2], out_offset=None, in_=xrows,
                                        in_offset=bass.IndirectOffsetOnAxis(ap=x_row[:, b:b + 1], axis=0)).then_inc(S(f"e_x{b % 2}"), 16)

            def scatter(b):
                pool.wait_ge(S("e_out"), b + 3)
                pool.indirect_dma_start(out=yrows, out_offset=bass.IndirectOffsetOnAxis(ap=y_row[:, b:b + 1], axis=0),
                                        in_=y_out[:, b % 2], in_offset=None).then_inc(S(f"e_y{b % 2}"), 16)

            pool.wait_ge(S("xrows"), 16 * NC)
            pool.wait_ge(S("rows_known"), 1)
            pool.wait_ge(S("found"), NC)
            gather(0)
            gather(1)
            barrier(pool)
            gather(2)
            gather(3)
            for b in range(NB_MAIN):
                if b + 4 < NB_MAIN:
                    gather(b + 4)
                scatter(b)
            for u in range(2):
                pool.wait_ge(S(f"e_y{u}"), 16 * NPAIR)
            with pool.If(blocks(pool) > NB_MAIN):
                for b in range(NB_MAIN, NB):
                    gather(b)
                    scatter(b)
                pool.wait_ge(S("e_y0"), 16 * ((NB + 1) // 2))
                pool.wait_ge(S("e_y1"), 16 * (NB // 2))
            pool.nop()
            barrier(pool)

        @block.vector
        def _(v):
            steps = [0]

            def step(ins):
                steps[0] += 1
                ins.then_inc(S("v_step"), 1)
                v.wait_ge(S("v_step"), steps[0])

            v.memset(acc[:, NT - 1, :], 0.0).then_inc(S("pad0"), 1)
            v.wait_ge(S("samp_in"), 16)
            step(v.tensor_copy(samp, samp_i))
            v.wait_ge(S("consts"), 1)
            for c in range(NS):
                ins = v.tensor_scalar(lt[:, c, :], bounds, samp[:, c:c + 1], None, ALU.is_gt)
            ins.then_inc(S("lt"), 1)
            v.wait_ge(S("pair_in"), 16)
            step(v.tensor_tensor(cmp, pair[:, 0:EC], pair[:, 1:EC + 1], ALU.is_gt))
            step(v.tensor_reduce(viol, cmp, AX_X, ALU.add))
            v.wait_ge(S("counted"), 1)
            step(v.tensor_copy(cnts[0:GB, :], ps[0:GB, 0, 0:4]))
            step(v.tensor_scalar(cnts[0:GB, 0:2], cnts[0:GB, 0:2], -1.0, 0.0, ALU.add, ALU.max))
            v.tensor_copy(widx[0:GB, :], cnts[0:GB, 0:2]).then_inc(S("widx"), 1)
            step(v.tensor_tensor(excess[0:GB, :], cnts[0:GB, 2:4], cnts[0:GB, 0:2], ALU.subtract))
            v.tensor_scalar(excess[0:GB, :], excess[0:GB, :], float(WIN // STEP), None, ALU.is_gt).then_inc(S("excess"), 1)
            v.wait_ge(S("badsum"), 1)
            v.tensor_copy(bad[0:1, :], ps[0:1, 1, 0:1]).then_inc(S("bad"), 1)

            for q, (t0, t1) in enumerate(X_PARTS):
                last = q == len(X_PARTS) - 1
                v.wait_ge(S(f"x_in{q}"), 32 if last else 16)
                for t in range(t0, t1 + last):
                    ins = v.bn_stats(st6[:, t, :], acc[:, t, :])
            step(ins)
            for t in range(NT):
                ins = v.bn_aggr(mv[:, t, :], st6[:, t, :])
            ins.then_inc(S("stats"), 1)
            v.wait_ge(S("std"), 1)
            step(v.reciprocal(rstd, std))
            for t in range(NT):
                ins = v.tensor_scalar(xn[:, t, :], acc[:, t, :], mv[:, t, 0:1], rstd[:, t:t + 1], ALU.subtract, ALU.mult)
            ins.then_inc(S("xn"), 1)
            for i, (hi, lo, raw) in enumerate(HALF_LIST[:-1]):
                v.wait_ge(S("w_hi"), i + 1)
                ins = v.scalar_tensor_tensor(lo, raw, WS, hi, ALU.mult, ALU.subtract)
            ins.then_inc(S("w_lo"), 1)
            for i in range(2 * NC):
                k, c = divmod(i, NC)
                v.wait_ge(S("xt_hi"), i + 1)
                v.tensor_tensor(ht_lo[:, k, c * 512:(c + 1) * 512], ps[:, X_BANK[i % 4], :],
                                ht_hi[:, k, c * 512:(c + 1) * 512], ALU.subtract).then_inc(S("xt_lo"), 1)
            v.wait_ge(S("w_lo"), 1)
            v.wait_ge(S("win_in"), 64)
            g = slice(0, GB)
            v.tensor_scalar(ki[g], win_s[g], 7, 4, ALU.logical_shift_right, ALU.logical_shift_left)
            for b in range(2):
                v.tensor_scalar(ka[g, b], win_d[g, b], grp[g, b:b + 1], None, ALU.add)
            step(v.tensor_scalar(win_s[g], win_s[g], 127, None, ALU.bitwise_and))
            v.tensor_scalar(kb[g], ka[g], 0.0, None, ALU.is_ge)
            v.tensor_copy(klo[g], win_s[g])
            step(v.tensor_tensor(kc[g], ki[g], ka[g], ALU.add))
            step(v.scalar_tensor_tensor(ka[g], ka[g], float(GW), kb[g], ALU.is_lt, ALU.mult))
            v.scalar_tensor_tensor(kc[g], kc[g], 1.0, ka[g], ALU.add, ALU.mult).then_inc(S("keys"), 1)
            v.wait_ge(S("wqkv_in"), 16)
            v.wait_ge(S("bias_in"), 16 * BIAS_DMAS)
            for k in range(KD):
                v.tensor_reduce(msum[:, k].rearrange("p (s h) -> p h s", s=2),
                                wqkv[:, k].rearrange("p (h s c) -> p h s c", s=3, c=HC)[:, :, 1:3, :], AX_X, ALU.add)
            step(v.tensor_reduce(bsum, bkv.rearrange("p (s c) -> p s c", c=HC), AX_X, ALU.add))
            v.tensor_scalar(msum, msum, 1.0 / HC, None, ALU.mult)
            step(v.tensor_scalar(bsum, bsum, 1.0 / HC, None, ALU.mult))
            for k in range(KD):
                for s_ in range(2):
                    v.tensor_tensor(wkvc[:, k, s_ * 256:(s_ + 1) * 256].rearrange("p (h c) -> p h c", c=HC),
                                    wqkv[:, k].rearrange("p (h s c) -> p h s c", s=3, c=HC)[:, :, 1 + s_, :],
                                    msum[:, k, 8 * s_:8 * s_ + 8].rearrange("p (h o) -> p h o", o=1).to_broadcast([P, HEADS, HC]), ALU.subtract)
                v.tensor_copy(heads(wq[:, k], 0), wqkv[:, k].rearrange("p (h s c) -> p h s c", s=3, c=HC)[:, :, 0, :])
            v.tensor_tensor(bias_kv.rearrange("p (s c) -> p s c", c=HC), bkv.rearrange("p (s c) -> p s c", c=HC),
                            bsum.rearrange("p (s o) -> p s o", o=1).to_broadcast([P, 16, HC]), ALU.subtract).then_inc(S("wkvc"), 1)
            hi, lo, raw = HALF_LIST[-1]
            v.wait_ge(S("w_hi"), NSPLIT)
            v.scalar_tensor_tensor(lo, raw, WS, hi, ALU.mult, ALU.subtract).then_inc(S("w_lo"), 1)
            v.wait_ge(S("colsT"), 1)
            step(v.tensor_copy(cols, ps[:, 0, 0:P]))
            v.wait_ge(S("wqT"), 1)
            for G in range(KD):
                v.tensor_copy(wqT[:, G, 0:D], ps[:, 1, G * D:(G + 1) * D])
                ins = v.tensor_copy(wqT[:, G, D:D + 1], cols[:, 104 + G:105 + G])
            ins.then_inc(S("wqT_in"), 1)
            v.wait_ge(S("keysT"), 1)
            v.tensor_copy(key_t, ps[:, 4, 0:3 * NG].rearrange("p (j g) -> p j g", j=3))
            v.tensor_copy(lo_t, ps[:, 5, 0:3 * NG].rearrange("p (j g) -> p j g", j=3)).then_inc(S("keycols"), 1)
            v.wait_ge(S("keycols"), 1)

            def hots(g0, n):
                with v.Fori(0, n // SETS) as k:
                    v.wait_ge(S("hot"), SETS * k + g0 + 1)
                    cols = bass.ds(SETS * k + g0, SETS)
                    v.tensor_copy(key_now, key_t[:, :, cols])
                    v.tensor_copy(lo_now.rearrange("p a (u j) -> p j (a u)", j=3), lo_t[:, :, cols]).then_inc(S("cols_now"), 1)
                    v.wait_ge(S("cols_now"), k + (g0 // SETS + 1))
                    for u in range(SETS):
                        if u % 2 == 0:
                            v.wait_ge(S("grp_sum"), SETS * k + (g0 + u + 2))
                            v.tensor_tensor(src_hot[:, u // 2], iota_p, lo_now[:, u // 2:u // 2 + 1, :].to_broadcast([P, P, 6]), ALU.is_equal)
                        for j in range(3):
                            ins = v.tensor_scalar(key_hot[:, u, j, :], iota_key, key_now[:, j, u:u + 1], None, ALU.is_equal)
                        ins.then_inc(S("hot"), 1)

            for b in range(NT // 4):
                g0 = sum(G_BATCH) * b
                v.wait_ge(S("kv"), b + 1)
                if b:
                    v.wait_ge(S("kn"), b)
                for t in range(4):
                    ins = v.scalar_tensor_tensor(kv_z[:, t], ps[:, t, :], 1.0 / WS, bias_kv, ALU.mult, ALU.add)
                ins.then_inc(S("kv_z"), 1)
                hots(g0, G_BATCH[0])
                v.wait_ge(S("kv_sq"), b + 1)
                v.tensor_reduce(kst, kv_sq.rearrange("p t (s c) -> p (t s) c", c=HC), AX_X, ALU.add).then_inc(S("kv_var"), 1)
                hots(g0 + G_BATCH[0], G_BATCH[1])
                v.wait_ge(S("kv_std"), b + 1)
                step(v.reciprocal(kst2, kst))
                if b:
                    v.wait_ge(S("kv_used"), b)
                for z0, n0, w in ((0, 0, D), (D, D, P), (D + P, D + P + 1, P)):
                    ins = v.tensor_tensor(kv_n[:, :, n0:n0 + w].rearrange("p t (s c) -> p t s c", c=HC), kv_z[:, :, z0:z0 + w].rearrange("p t (s c) -> p t s c", c=HC),
                                          kst2[:, :, z0 // HC:(z0 + w) // HC].rearrange("p t (s o) -> p t s o", o=1).to_broadcast([P, 4, w // HC, HC]), ALU.mult)
                ins.then_inc(S("kn"), 1)
                hots(g0 + sum(G_BATCH[:2]), G_BATCH[2])
            hots(FOLD0, G_FOLD[0])
            v.wait_ge(S("kv_used"), NT // 4)
            for G in range(KD):
                v.tensor_copy(sk[:, G:G + 1], ps[:, 4 + G, P:P + 1])
                ins = v.tensor_tensor(kvt[:, G].rearrange("p (a c) -> p a c", c=HC), ps[:, 4 + G, 0:P].rearrange("p (a c) -> p a c", c=HC),
                                      gbkv[:, 2:3, :].to_broadcast([P, 4, HC]), ALU.mult)
            step(ins)
            for G in range(KD):
                ins = v.scalar_tensor_tensor(kvt[:, G].rearrange("p (a c) -> p a c", c=HC), gbkv[:, 3:4, :].to_broadcast([P, 4, HC]),
                                             sk[:, G:G + 1], kvt[:, G].rearrange("p (a c) -> p a c", c=HC), ALU.mult, ALU.add)
            step(ins)
            v.tensor_tensor(kvm, kvt, blockdiag.rearrange("p (o c) -> p o c", o=1).to_broadcast([P, KD, P]), ALU.mult).then_inc(S("kvm"), 1)
            hots(FOLD0 + G_FOLD[0], G_FOLD[1])
            v.wait_ge(S("mT"), 1)
            for G in range(KD):
                v.tensor_copy(retb[:, G:G + 1], ps[:, 2 + G, D:D + 1])
                ins = v.tensor_copy(mT[:, G, :], ps[:, 2 + G, 0:D + 1])
            step(ins)
            for G in range(KD):
                ins = v.tensor_tensor(mT[:, G, G * P:(G + 1) * P], mT[:, G, G * P:(G + 1) * P], ident, ALU.add)
            ins.then_inc(S("mT_in"), 1)
            hots(FOLD0 + sum(G_FOLD[:2]), G_FOLD[2])
            v.wait_ge(S("m1_hi"), 1)
            v.scalar_tensor_tensor(m1_lo, ps[:, 0, :].rearrange("p (k d) -> p k d", k=KD), WS, m1_hi, ALU.mult, ALU.subtract)
            v.tensor_tensor(b1p, ps[:, 1, 0:KD], cols[:, 102:104], ALU.add).then_inc(S("m1_lo"), 1)
            for i in range(2 * NC):
                c, f = divmod(i, 2)
                if f == 0:
                    hots(H10 + G_H1 * c, G_H1)
                v.wait_ge(S("h1_hi"), i + 1)
                v.tensor_tensor(h1_lo[:, f, c * 512:(c + 1) * 512], h1f[:, f], h1_hi[:, f, c * 512:(c + 1) * 512], ALU.subtract).then_inc(S("h1_lo"), 1)
            v.wait_ge(S("acc"), 3)
            for t in range(NT):
                if t % 2 == 0:
                    hots(OUT0 + G_OUT * (t // 2), G_OUT)
                v.wait_ge(S("mix_out"), t + 1)
                v.scalar_tensor_tensor(acc[:, t], ps[:, OUT_BANK[t % 3], 0:D], 1.0 / WS, acc[:, t], ALU.mult, ALU.add).then_inc(S("mix_acc"), 1)
            hots(LAST0, NG - LAST0)
            barrier(v)
            with v.If(unsorted(v) > 0):
                v.memset(at, 0.0)
                v.tensor_copy(ident16, ident).then_inc(S("any_zero"), 1)
                v.sem_inc(S("any_read"), 1)
                v.sem_inc(S("any_out"), 1)
                with v.Fori(0, PASSES) as q:
                    v.wait_ge(S("any_in"), 32 * (q + 1))
                    v.wait_ge(S("any_out"), NG * q + 1)
                    v.tensor_scalar(any_i[g], any_s[g], 7, 4, ALU.logical_shift_right, ALU.logical_shift_left)
                    for b in range(2):
                        v.tensor_scalar(any_a[g, b], any_d[g], grp[g, b:b + 1], None, ALU.add)
                    v.tensor_scalar(any_s[g], any_s[g], 127, None, ALU.bitwise_and).then_inc(S("any_step"), 1)
                    v.wait_ge(S("any_step"), 4 * q + 1)
                    v.tensor_copy(any_k[g], any_i[g])
                    v.tensor_copy(any_lo[g], any_s[g]).then_inc(S("any_read"), 1)
                    v.tensor_scalar(any_b[g], any_a[g], 0.0, None, ALU.is_ge).then_inc(S("any_step"), 1)
                    v.wait_ge(S("any_step"), 4 * q + 2)
                    v.tensor_tensor(any_c[g], any_a[g], any_k[g].rearrange("p (o w) -> p o w", o=1).to_broadcast([GB, 2, WIN]), ALU.add).then_inc(S("any_step"), 1)
                    v.wait_ge(S("any_step"), 4 * q + 3)
                    v.scalar_tensor_tensor(any_a[g], any_a[g], float(GW), any_b[g], ALU.is_lt, ALU.mult).then_inc(S("any_step"), 1)
                    v.wait_ge(S("any_step"), 4 * q + 4)
                    v.scalar_tensor_tensor(any_c[g], any_c[g], 1.0, any_a[g], ALU.add, ALU.mult).then_inc(S("any_keys"), 1)
                    v.wait_ge(S("any_keysT"), q + 1)
                    v.tensor_copy(key_t, ps[:, 4, 0:3 * NG].rearrange("p (j g) -> p j g", j=3))
                    v.tensor_copy(lo_t, ps[:, 5, 0:3 * NG].rearrange("p (j g) -> p j g", j=3)).then_inc(S("any_cols"), 1)
                    with v.Fori(0, NG) as gi:
                        v.wait_ge(S("any_cols"), q + 1)
                        v.wait_ge(S("any_out"), NG * q + gi + 1)
                        for j in range(3):
                            v.tensor_scalar(src_hot[:, 0, :, j], iota_p[:, :, 0], lo_t[:, j, bass.ds(gi, 1)], None, ALU.is_equal)
                            ins = v.tensor_scalar(key_hot[:, 0, j, :], iota_key, key_t[:, j, bass.ds(gi, 1)], None, ALU.is_equal)
                        ins.then_inc(S("any_hot"), 1)
            v.nop()
            v.sem_inc(S("g_lo"), 4)
            v.sem_inc(S("f3_acc"), 4)
            v.sem_inc(S("h_lo"), 4)
            v.sem_inc(S("pre"), 2)
            barrier(v)
            def low_weights(i):
                e, w = divmod(i, 2)
                v.wait_ge(S("ew_hi"), i + 1)
                if i:
                    v.wait_ge(S("ew_lo"), i)
                v.scalar_tensor_tensor(w_e[e][2 * w + 1].rearrange("p k n -> p (k n)"), ew_raw[i], WS,
                                       w_e[e][2 * w].rearrange("p k n -> p (k n)"), ALU.mult, ALU.subtract).then_inc(S("ew_lo"), 1)

            for c in (3, 4, 0, 1, 2):
                v.tensor_scalar(has[:, c * 512:(c + 1) * 512], ps[:, DEG_BANK[c], :], 1.0, None, ALU.min)
                v.tensor_scalar(rcnt[:, c * 512:(c + 1) * 512], ps[:, DEG_BANK[c], :], 1.0, None, ALU.max).then_inc(S("rcnt"), 1)
            for l in range(3):
                with v.Fori(0, NC) as c:
                    for u in range(4):
                        t = 4 * c + u
                        v.wait_ge(S("g_hi"), NT * l + t + 1)
                        v.scalar_tensor_tensor(g_lo[:, bass.ds(t, 1), :], ps[:, BANK[u]:BANK[u] + 1, 0:D], 1.0 / WS, g_hi[:, bass.ds(t, 1), :], ALU.mult, ALU.subtract)
                        v.scalar_tensor_tensor(acc[:, bass.ds(t, 1), :], ps[:, BANK[u]:BANK[u] + 1, D:2 * D], 1.0 / WS, acc[:, bass.ds(t, 1), :], ALU.mult, ALU.add).then_inc(S("g_lo"), 1)
                if l == 0:
                    v.wait_ge(S("rcnt"), NC)
                    v.reciprocal(rcnt, rcnt).then_inc(S("rcnt"), 1)
                    v.wait_ge(S("rcnt"), NC + 1)
                def new_h(c, n):
                    v.wait_ge(S("agg"), NC * l + c + 1)
                    for f in range(2):
                        i = 2 * NC * l + 2 * c + f
                        v.wait_ge(S("h_lo"), i + 3)
                        v.tensor_tensor(tmp_t[:, f:f + 1, 0:n], ps[:, bass.ds(2 * (c % 2) + f, 1), 0:n],
                                        rcnt.rearrange("p (o n) -> p o n", o=1)[:, :, bass.ds(c * 512, n)], ALU.mult).then_inc(S("mean"), 1)
                    for f in range(2):
                        i = 2 * NC * l + 2 * c + f
                        v.wait_ge(S("mean"), i + 1)
                        v.wait_ge(S("own_has"), i + 1)
                        v.tensor_tensor(tmp_t[:, f, 0:n], tmp_t[:, f, 0:n], tmp_p[:, f, 0:n], ALU.add).then_inc(S("pre"), 1)
                    for f in range(2):
                        i = 2 * NC * l + 2 * c + f
                        v.wait_ge(S("h_hi"), i + 1)
                        v.scalar_tensor_tensor(ht_lo[:, f, bass.ds(c * 512, n)], tmp_t[:, f, 0:n], 0.0,
                                               ht_hi[:, f, bass.ds(c * 512, n)], ALU.max, ALU.subtract).then_inc(S("h_lo"), 1)

                if l < 2:
                    with v.Fori(0, NC - 1) as c:
                        new_h(c, 512)
                else:
                    for c in range(NC - 1):
                        new_h(c, 512)
                        for i in SPLIT_AFTER[c]:
                            low_weights(i)
                new_h(NC - 1, LASTC)
            for t in range(NT + 2):
                if t < NT:
                    v.wait_ge(S("f3"), t + 1)
                    v.scalar_tensor_tensor(acc[:, t], ps[:, BANK[t % 4], 0:D], 1.0 / WS, acc[:, t], ALU.mult, ALU.add).then_inc(S("f3_acc"), 1)
                if 1 <= t <= NT:
                    v.wait_ge(S("f3_acc"), t + 4)
                    v.bn_stats(st6[:, t - 1, :], acc[:, t - 1, :]).then_inc(S("bn1"), 1)
                if t >= 2:
                    v.wait_ge(S("bn1"), t - 1)
                    ins = v.bn_aggr(mv[:, t - 2, :], st6[:, t - 2, :])
            ins.then_inc(S("stats"), 1)
            barrier(v)

            v.wait_ge(S("std"), 2)
            step(v.reciprocal(rstd, std))
            v.scalar_tensor_tensor(nmr, mv[:, :, 0], -1.0, rstd, ALU.mult, ALU.mult).then_inc(S("nmr"), 1)
            for t in range(Y_DVE):
                v.tensor_scalar(xn2[:, t, :], acc[:, t, :], mv[:, t, 0:1], rstd[:, t:t + 1], ALU.subtract, ALU.mult).then_inc(S("y_first"), 1)
            for t in range(NT):
                if t < Y_DVE:
                    v.wait_ge(S("y_first"), t + 1)
                else:
                    v.wait_ge(S("y"), t + 1 - Y_DVE)
                v.bn_stats(st6[:, t, :], xn2[:, t, :]).then_inc(S("bn2"), 1)
            v.wait_ge(S("bn2"), NT)
            for t in range(NT):
                ins = v.bn_aggr(mv[:, t, :], st6[:, t, :])
            ins.then_inc(S("stats"), 1)
            v.wait_ge(S("std"), 3)
            step(v.reciprocal(rstd, std))
            v.scalar_tensor_tensor(nmr, mv[:, :, 0], -1.0, rstd, ALU.mult, ALU.mult).then_inc(S("nmr"), 1)
            for i in range(IN_LAYER, IN_LAYER + EARLY):
                low_weights(i)
            v.wait_ge(S("logits"), NT // 2)
            v.wait_ge(S("wr_in"), 32)
            step(v.tensor_tensor(logit, ps[:, 2, 0:NT * NE].rearrange("p (t e) -> p t e", e=NE),
                                 br.rearrange("p (o e) -> p o e", o=1).to_broadcast([P, NT, NE]), ALU.add))
            for t in range(NT):
                ins = v.max(mx[:, t, :], logit[:, t, :])
            step(ins)
            for t in range(NT):
                ins = v.max_index(top[:, t, :], mx[:, t, :], logit[:, t, :])
            step(ins)
            v.tensor_copy(topf, top[:, :, 0:2])
            v.wait_ge(S("blk"), 1)
            v.tensor_scalar(valid, valid, float(LAST), None, ALU.is_lt)
            step(v.tensor_tensor(wgt[:, 1], mx[:, :, 1], mx[:, :, 0], ALU.subtract))
            for q, hot in enumerate((hot1, hot2)):
                ins = v.tensor_tensor(hot, iota8.rearrange("p (o e) -> p o e", o=1).to_broadcast([P, NT, NE]),
                                      topf[:, :, q:q + 1].to_broadcast([P, NT, NE]), ALU.is_equal)
            ins.then_inc(S("diff"), 1)
            v.wait_ge(S("diff"), 1)
            step(v.tensor_tensor(hot12, hot1, hot2, ALU.add))
            v.tensor_scalar(hot12[:, NT - 1], hot12[:, NT - 1], valid, None, ALU.mult).then_inc(S("hot12"), 1)
            v.wait_ge(S("ranks"), 1)
            totals = ps[:, 4, 0:NT * NE].rearrange("p (t e) -> p t e", e=NE)
            step(v.tensor_copy(tot_a, totals))
            src, dst = tot_a, tot_b
            s_ = 1
            while s_ < NT:
                v.tensor_tensor(dst[:, s_:NT], src[:, s_:NT], src[:, 0:NT - s_], ALU.add)
                step(v.tensor_copy(dst[:, 0:s_], src[:, 0:s_]))
                src, dst = dst, src
                s_ *= 2
            v.tensor_tensor(rank, src, totals, ALU.subtract)
            step(v.tensor_scalar(nblk_i, src[:, NT - 1], float(P - 1), None, ALU.add))
            step(v.tensor_tensor(rank, rank, ps[:, 3, 0:NT * NE].rearrange("p (t e) -> p t e", e=NE), ALU.add))
            step(v.tensor_scalar(nblk_i, nblk_i, 7, None, ALU.logical_shift_right))
            step(v.tensor_copy(nblk, nblk_i))
            step(v.tensor_copy(cum, nblk))
            cs, cd = cum, cum2
            for s_ in (1, 2, 4):
                v.tensor_tensor(cd[:, s_:NE], cs[:, s_:NE], cs[:, 0:NE - s_], ALU.add)
                step(v.tensor_copy(cd[:, 0:s_], cs[:, 0:s_]))
                cs, cd = cd, cs
            step(v.tensor_tensor(base, cs, nblk, ALU.subtract))
            step(v.tensor_scalar(base, base, float(P), None, ALU.mult))
            step(v.tensor_tensor(rank, rank, base.rearrange("p (o e) -> p o e", o=1).to_broadcast([P, NT, NE]), ALU.add))
            v.tensor_tensor(hot1, hot1, rank, ALU.mult)
            step(v.tensor_tensor(hot2, hot2, rank, ALU.mult))
            v.tensor_reduce(slot_f[:, 0], hot1, AX_X, ALU.add)
            step(v.tensor_reduce(slot_f[:, 1], hot2, AX_X, ALU.add))
            step(v.tensor_copy(slot_i, slot_f))
            v.tensor_scalar(slot, slot_i, 7, None, ALU.logical_shift_right)
            step(v.tensor_scalar(slot_i, slot_i, P - 1, None, ALU.bitwise_and))
            v.tensor_copy(slot_blk, slot)
            step(v.tensor_copy(place_f, slot_i))
            for c in range(NC):
                hot_p = place_hot[c % 2].rearrange("p (q t) n -> p q t n", q=TOPK)
                hot_b = blk_hot[c % 2].rearrange("p (q t) n -> p q t n", q=TOPK)

                def spread(col, n):
                    return col[:, :, 4 * c:4 * c + 4].rearrange("p q (t o) -> p q t o", o=1).to_broadcast([P, TOPK, 4, n])

                def along(row, n):
                    return row.rearrange("p (q t n) -> p q t n", q=1, t=1).to_broadcast([P, TOPK, 4, n])

                if c >= 2:
                    v.wait_ge(S("found"), c - 1)
                step(v.tensor_tensor(hot_b, along(iota_blk, NB), spread(slot_blk, NB), ALU.is_equal))
                v.tensor_tensor(hot_p, along(iota_pos, P), spread(place_f, P), ALU.is_equal)
                v.tensor_tensor(hot_b, hot_b, spread(node, NB), ALU.mult).then_inc(S("place"), 1)
                if c < BESIDE:
                    low_weights(IN_LAYER + EARLY + c)
            step(v.tensor_tensor(blk_ge, blk.rearrange("p (b o) -> p b o", o=1).to_broadcast([P, NB, NE]),
                                 cs.rearrange("p (o e) -> p o e", o=1).to_broadcast([P, NB, NE]), ALU.is_ge))
            step(v.tensor_reduce(blk, blk_ge, AX_X, ALU.add))
            v.tensor_scalar(blk_e, blk, float(NE - 1), None, ALU.min)
            v.tensor_copy(blk_n, cs[:, NE - 1:NE]).then_inc(S("blk_e"), 1)
            v.wait_ge(S("found"), NC)
            step(v.tensor_copy(found, ps[:, 5, 0:NB]))
            v.tensor_scalar(second, found, NP + 0.5, -float(NP), ALU.is_gt, ALU.mult)
            step(v.tensor_scalar(unused, found, 0.5, None, ALU.is_lt))
            step(v.tensor_tensor(unused, unused, y_free, ALU.mult))
            step(v.tensor_tensor(second, second, found, ALU.add))
            v.scalar_tensor_tensor(y_row, found, -1.0, unused, ALU.add, ALU.add)
            v.tensor_scalar(x_row, second, -1.0, 0.0, ALU.add, ALU.max).then_inc(S("rows_known"), 1)
            v.wait_ge(S("blk_e"), 1)
            v.wait_ge(S("wexp"), 1)
            step(v.tensor_scalar(wgt[:, 0], wgt[:, 1], 1.0, None, ALU.add))
            step(v.reciprocal(wgt[:, 0], wgt[:, 0]))
            step(v.tensor_tensor(wgt[:, 1], wgt[:, 1], wgt[:, 0], ALU.mult))
            for i in range(IN_LAYER + EARLY + BESIDE, 2 * NE):
                low_weights(i)
            v.sem_inc(S("e_xe"), 2)
            v.sem_inc(S("e_lo"), 2)
            v.sem_inc(S("e_out"), 2)
            barrier(v)

            def widen(b, u):
                e = v.value_load(blk_e[0:1, bass.ds(b, 1)], min_val=0, max_val=NE - 1)
                v.wait_ge(S("e_turned"), b + 3)
                v.wait_ge(S("e_h"), b + 1)
                v.wait_ge(S("e_xe"), b + 2)
                for k in range(KD):
                    gcol, bcol = cols[:, bass.ds(64 + KD * e + k, 1)], cols[:, bass.ds(80 + KD * e + k, 1)]
                    ins = v.tensor_scalar(xe[:, k], ps[:, 4 + u, k * P:(k + 1) * P], gcol, bcol, ALU.mult, ALU.add)
                ins.then_inc(S("e_xf"), 1)
                v.wait_ge(S("e_xf"), b + 1)
                v.tensor_copy(xe_hi[:, u], xe).then_inc(S("e_xw"), 1)
                v.wait_ge(S("e_xw"), b + 1)
                v.tensor_tensor(xe_lo[:, u], xe, xe_hi[:, u], ALU.subtract).then_inc(S("e_xe"), 1)

            def fetch(b, u):
                e = v.value_load(blk_e[0:1, bass.ds(b, 1)], min_val=0, max_val=NE - 1)
                v.wait_ge(S("e_h"), b + 1)
                v.tensor_copy(w1_now[:, u].rearrange("p s k h -> p (s k h)"), mem[:, bass.ds(e * EWN + W1_HI, 2 * KD * H)]).then_inc(S("e_w1"), 1)

            def low(b, u):
                v.wait_ge(S("e_hi"), b + 1)
                v.tensor_tensor(h_lo[:, u], hf[:, u], h_hi[:, u], ALU.subtract).then_inc(S("e_lo"), 1)

            def result(b, bb, u):
                e = v.value_load(blk_e[0:1, bass.ds(b, 1)], min_val=0, max_val=NE - 1)
                v.wait_ge(S("e_yp"), b + 3)
                if bb is not None:
                    v.wait_ge(S(f"e_y{u}"), 16 * bb)
                v.scalar_tensor_tensor(y_out[:, u:u + 1], ps[:, 6 + u:7 + u, 0:D], 1.0 / WS, b2_all[:, bass.ds(e, 1), :], ALU.mult, ALU.add).then_inc(S("e_out"), 1)

            v.wait_ge(S("b2_in"), 16)
            widen(0, 0)
            fetch(0, 0)
            widen(1, 1)
            fetch(1, 1)
            low(0, 0)

            def two_blocks(bb, stores):
                fetch(2 * bb + 2, 0)
                widen(2 * bb + 2, 0)
                low(2 * bb + 1, 1)
                result(2 * bb, stores, 0)
                fetch(2 * bb + 3, 1)
                widen(2 * bb + 3, 1)
                low(2 * bb + 2, 0)
                result(2 * bb + 1, stores, 1)

            two_blocks(0, None)
            with v.Fori(1, NPAIR - 1) as bb:
                two_blocks(bb, bb)
            low(NB_MAIN - 1, 1)
            result(NB_MAIN - 2, NPAIR - 1, 0)
            result(NB_MAIN - 1, NPAIR - 1, 1)
            with v.If(blocks(v) > NB_MAIN):
                for b in range(NB_MAIN, NB):
                    fetch(b, b % 2)
                    widen(b, b % 2)
                    low(b, b % 2)
                    result(b, b // 2, b % 2)
            v.nop()
            barrier(v)
            for t in range(NT):
                n = P if t < NT - 1 else LAST
                if t % 4 == 0:
                    v.wait_ge(S(f"y_in{t // 4}"), 16 * TOPK * (1 if t < NT - 4 else 2))
                step(v.scalar_tensor_tensor(acc[0:n, t], y1[0:n, t], wgt[0:n, 0, t:t + 1], acc[0:n, t], ALU.mult, ALU.add))
                v.scalar_tensor_tensor(acc[0:n, t], y2[0:n, t], wgt[0:n, 1, t:t + 1], acc[0:n, t], ALU.mult, ALU.add).then_inc(S("final"), 1)

        @block.scalar
        def _(a):
            a.wait_ge(S("consts"), 1)
            rows = [(I["L0_ffn_b1"].rearrange("e (j p) -> (e j) p", p=P), 0, NE * KH),
                    (I["L0_ffn_ln_g"].rearrange("e (j p) -> (e j) p", p=P), 64, NE * KD),
                    (I["L0_ffn_ln_b"].rearrange("e (j p) -> (e j) p", p=P), 80, NE * KD),
                    (I["L0_gnn_b0"].rearrange("(j p) -> j p", p=P), 96, KD), (I["L0_gnn_b1"].rearrange("(j p) -> j p", p=P), 98, KD),
                    (I["L0_gnn_b2"].rearrange("(j p) -> j p", p=P), 100, KD), (I["L0_mix_b1"].rearrange("(j p) -> j p", p=P), 102, KD)]
            for src, r, n in rows:
                a.dma_start(stack[r:r + n, :], src).then_inc(S("rows_in"), 16)
            bq = I["L0_mix_b_qkv"].rearrange("(h s c) -> s h c", s=3, c=HC)
            for G in range(KD):
                a.dma_start(stack[104 + G:105 + G, :].rearrange("o (h c) -> o h c", c=HC), bq[0:1, 4 * G:4 * G + 4, :]).then_inc(S("rows_in"), 16)
            for s_ in range(2):
                a.dma_start(bkv[:, s_ * 256:(s_ + 1) * 256].rearrange("p (h c) -> p h c", c=HC), bq[1 + s_:2 + s_, :, :].to_broadcast([P, HEADS, HC])).then_inc(S("bias_in"), 16)
            for i, n in enumerate(("kln_g", "kln_b", "vln_g", "vln_b")):
                a.dma_start(gbkv[:, i], I[f"L0_mix_{n}"].partition_broadcast(P)).then_inc(S("bias_in"), 16)
            a.dma_start(bout[:, 0], I["L0_gnn_bf"].partition_broadcast(P)).then_inc(S("bias_in"), 16)
            a.dma_start(bout[:, 1], I["L0_mix_b2"].partition_broadcast(P)).then_inc(S("bias_in"), 16)

            a.wait_ge(S("stats"), 1)
            a.activation(std, mv[:, :, 1], ACT.Sqrt, bias=eps[:, 0:1]).then_inc(S("std"), 1)
            a.wait_ge(S("w_in"), 128)
            for i, (hi, lo, raw) in enumerate(HALF_LIST[:-1]):
                if i < 3:
                    a.wait_ge(S("wd"), i + 1)
                a.activation(hi, raw, ACT.Copy, scale=WS).then_inc(S("w_hi"), 1)
            for i in range(2 * NC):
                k, c = divmod(i, NC)
                a.wait_ge(S("xt"), i + 1)
                a.activation(ht_hi[:, k, c * 512:(c + 1) * 512], ps[:, X_BANK[i % 4], :], ACT.Copy).then_inc(S("xt_hi"), 1)
            a.wait_ge(S("wkvc"), 1)
            a.activation(HALF_LIST[-1][0], HALF_LIST[-1][2], ACT.Copy, scale=WS).then_inc(S("w_hi"), 1)

            def counts(g0, n):
                c = g0 // GC
                with a.Fori(0, n // SETS) as k:
                    for u in range(SETS):
                        a.wait_ge(S("grp_sum"), SETS * k + (g0 + u + 1 + SETS))
                        a.activation(at[:, c * NT:(c + 1) * NT, bass.ds(GW * SETS * k + GW * (g0 + u - c * GC), GW)],
                                     ps[:, 6 + u % 2, 0:KEYS].rearrange("p (s d) -> p s d", d=GW), ACT.Copy).then_inc(S("grp_free"), 1)

            for b in range(NT // 4):
                g0 = sum(G_BATCH) * b
                a.wait_ge(S("kv_z"), b + 1)
                if b:
                    a.wait_ge(S("kv_var"), b)
                a.activation(kv_sq, kv_z, ACT.Square).then_inc(S("kv_sq"), 1)
                if b == 0:
                    a.wait_ge(S("keycols"), 1)
                    a.wait_ge(S("w_lo"), 2)
                    a.wait_ge(S("wqT"), 1)
                    a.wait_ge(S("acc"), 3)
                counts(g0, G_BATCH[0])
                a.wait_ge(S("kv_var"), b + 1)
                a.activation(kst, kst, ACT.Sqrt, bias=eps[:, 0:1], scale=1.0 / HC).then_inc(S("kv_std"), 1)
                counts(g0 + G_BATCH[0], G_BATCH[1])
                counts(g0 + sum(G_BATCH[:2]), G_BATCH[2])
            counts(FOLD0, G_FOLD[0])
            counts(FOLD0 + G_FOLD[0], G_FOLD[1])
            a.wait_ge(S("m1"), 1)
            a.activation(m1_hi, ps[:, 0, :].rearrange("p (k d) -> p k d", k=KD), ACT.Copy, scale=WS).then_inc(S("m1_hi"), 1)
            counts(FOLD0 + sum(G_FOLD[:2]), G_FOLD[2])
            a.wait_ge(S("m1_lo"), 1)
            a.wait_ge(S("kv_used"), NT // 4)
            for i in range(2 * NC):
                c, f = divmod(i, 2)
                a.wait_ge(S("h1"), i + 1)
                if i >= 2:
                    a.wait_ge(S("h1_lo"), i - 1)
                a.activation(h1f[:, f], ps[:, 2 + i % 4, :], ACT.Gelu, bias=b1p[:, f:f + 1], scale=1.0 / WS).then_inc(S("h1f"), 1)
                a.wait_ge(S("h1f"), i + 1)
                a.activation(h1_hi[:, f, c * 512:(c + 1) * 512], h1f[:, f], ACT.Copy).then_inc(S("h1_hi"), 1)
                if f == 1:
                    counts(H10 + G_H1 * c, G_H1)
            a.wait_ge(S("h1_lo"), 2 * NC)
            for i in range(NT // 2):
                counts(OUT0 + G_OUT * i, G_OUT)
            counts(LAST0, NG - LAST0)
            barrier(a)
            with a.If(unsorted(a) > 0):
                with a.Fori(0, PASSES) as q:
                    for c in range(NC):
                        with a.Fori(0, GC) as gi:
                            a.wait_ge(S("any_sum"), NG * q + GC * c + gi + 1)
                            a.activation(at[:, c * NT:(c + 1) * NT, bass.ds(GW * gi, GW)], ps[:, 0, 0:KEYS].rearrange("p (s d) -> p s d", d=GW),
                                         ACT.Copy).then_inc(S("any_out"), 1)
            a.nop()
            barrier(a)

            def high_weights(i):
                e, w = divmod(i, 2)
                a.wait_ge(S(f"ew_in{e}"), 32)
                if i >= 2:
                    a.wait_ge(S("ew_lo"), i - 1)
                a.activation(w_e[e][2 * w].rearrange("p k n -> p (k n)"), ew_raw[i], ACT.Copy, scale=WS).then_inc(S("ew_hi"), 1)

            for l in range(3):
                with a.Fori(0, NC) as c:
                    for u in range(4):
                        t = 4 * c + u
                        a.wait_ge(S("g"), NT * l + t + 1)
                        a.activation(g_hi[:, bass.ds(t, 1), :], ps[:, BANK[u]:BANK[u] + 1, 0:D], ACT.Copy, scale=1.0 / WS).then_inc(S("g_hi"), 1)
                def new_h(c, n):
                    for f in range(2):
                        i = 2 * NC * l + 2 * c + f
                        a.wait_ge(S("own_sum"), NC * l + c + 1)
                        a.wait_ge(S("pre"), i + 1)
                        a.activation(tmp_p[:, f:f + 1, 0:n], ps[:, bass.ds(4 + 2 * (c % 2) + f, 1), 0:n], ACT.Identity,
                                     bias=cols[:, 96 + 2 * l + f:97 + 2 * l + f], scale=1.0 / WS).then_inc(S("own"), 1)
                    for f in range(2):
                        i = 2 * NC * l + 2 * c + f
                        a.wait_ge(S("pre"), i + 3)
                        a.activation(ht_hi[:, f, bass.ds(c * 512, n)], tmp_t[:, f, 0:n], ACT.Relu).then_inc(S("h_hi"), 1)

                if l < 2:
                    with a.Fori(0, NC - 1) as c:
                        new_h(c, 512)
                else:
                    for c in range(NC - 1):
                        new_h(c, 512)
                        for i in SPLIT_AFTER[c]:
                            high_weights(i)
                new_h(NC - 1, LASTC)
            barrier(a)

            a.wait_ge(S("stats"), 2)
            a.activation(std, mv[:, :, 1], ACT.Sqrt, bias=eps[:, 0:1]).then_inc(S("std"), 1)
            a.wait_ge(S("nmr"), 1)
            for t in range(Y_DVE, NT):
                a.activation(xn2[:, t, :], acc[:, t, :], ACT.Identity, bias=nmr[:, t:t + 1], scale=rstd[:, t:t + 1]).then_inc(S("y"), 1)

            for h in range(NT // 2):
                if h == STD_AT:
                    a.wait_ge(S("stats"), 3)
                    a.activation(std, mv[:, :, 1], ACT.Sqrt, bias=eps[:, 0:1]).then_inc(S("std"), 1)
                elif 1 <= h <= EARLY + 1:
                    high_weights(IN_LAYER + (h - 1 if h < STD_AT else h - 2))
                a.wait_ge(S("yT"), h + 1)
                if h >= 2:
                    a.wait_ge(S("logits"), h - 1)
                a.activation(yT[:, h % 2], ps[:, h % 2, :].rearrange("p (k n) -> p k n", n=P), ACT.Copy).then_inc(S("yT_in"), 1)
            a.wait_ge(S("nmr"), 2)
            for t in range(NT):
                a.activation(xn2[:, t, :], xn2[:, t, :], ACT.Identity, bias=nmr[:, t:t + 1], scale=rstd[:, t:t + 1]).then_inc(S("xn2"), 1)
            a.wait_ge(S("diff"), 1)
            a.activation(wgt[:, 1], wgt[:, 1], ACT.Exp).then_inc(S("wexp"), 1)
            for i in range(IN_LAYER + EARLY, 2 * NE):
                high_weights(i)
            a.sem_inc(S("e_gelu"), 2)
            barrier(a)
            a.preload_act_table(ACT.Gelu)

            def gelu(b, u):
                e = a.value_load(blk_e[0:1, bass.ds(b, 1)], min_val=0, max_val=NE - 1)
                a.wait_ge(S("e_h"), b + 3)
                a.wait_ge(S("e_lo"), b + 1)
                for j in range(KH):
                    ins = a.activation(hf[:, u, j], ps[:, 2 * u + j // 4, (j % 4) * P:(j % 4 + 1) * P], ACT.Gelu,
                                       bias=cols[:, bass.ds(KH * e + j, 1)], scale=1.0 / WS)
                ins.then_inc(S("e_gelu"), 1)
                a.wait_ge(S("e_gelu"), b + 3)
                a.wait_ge(S("e_yp"), b + 1)
                a.activation(h_hi[:, u], hf[:, u], ACT.Copy).then_inc(S("e_hi"), 1)

            with a.Fori(0, NPAIR) as bb:
                gelu(2 * bb, 0)
                gelu(2 * bb + 1, 1)
            with a.If(blocks(a) > NB_MAIN):
                for b in range(NB_MAIN, NB):
                    gelu(b, b % 2)
            a.nop()
            barrier(a)

        @block.tensor
        def _(pe):
            def three(out_, w_hi, w_lo, x_hi, x_lo, first, last):
                pe.matmul(out_, w_hi, x_hi, start=first, stop=False)
                pe.matmul(out_, w_hi, x_lo, start=False, stop=False)
                return pe.matmul(out_, w_lo, x_hi, start=False, stop=last)

            pe.sem_inc(S("grp_sum"), SETS)
            pe.sem_inc(S("grp_free"), 2)
            pe.sem_inc(S("hot"), 1)
            pe.wait_ge(S("consts"), 1)
            pe.wait_ge(S("lt"), 1)
            for q, lo in enumerate((0, GB, 1, GB + 1)):
                for c in range(NS):
                    ins = pe.matmul(ps[0:GB, 0, q:q + 1], lt[:, c, lo:lo + GB], ones16[:, 0:1], start=c == 0, stop=c == NS - 1)
            ins.then_inc(S("counted"), 1)
            pe.wait_ge(S("excess"), 1)
            pe.matmul(ps[0:1, 1, 0:1], ones[0:GB, 0:1], excess[0:GB, 0:1], start=True, stop=False)
            pe.matmul(ps[0:1, 1, 0:1], ones[0:GB, 0:1], excess[0:GB, 1:2], start=False, stop=False)
            pe.matmul(ps[0:1, 1, 0:1], ones[:, 0:1], viol, start=False, stop=True).then_inc(S("badsum"), 1)
            pe.wait_ge(S("xn"), 1)
            for i in range(2 * NC):
                k, c = divmod(i, NC)
                if i >= 4:
                    pe.wait_ge(S("xt_lo"), i - 3)
                for q in range(4):
                    ins = pe.transpose(ps[:, X_BANK[i % 4], q * P:(q + 1) * P], xn[:, 4 * c + q, k * P:(k + 1) * P], ident)
                ins.then_inc(S("xt"), 1)
            pe.wait_ge(S("rows_in"), 16 * 9)
            pe.wait_ge(S("counted"), 1)
            pe.wait_ge(S("widx"), 1)
            pe.transpose(ps[:, 0, 0:P], stack, ident).then_inc(S("colsT"), 1)
            pe.wait_ge(S("wkvc"), 1)
            pe.wait_ge(S("bad"), 1)
            for G in range(KD):
                for k in range(KD):
                    ins = pe.transpose(ps[:, 1, G * D + k * P:G * D + (k + 1) * P], wq[:, k, G * P:(G + 1) * P], ident)
            ins.then_inc(S("wqT"), 1)
            pe.wait_ge(S("keys"), 1)
            for b in range(2):
                for j in range(3):
                    o = j * NG + b * GB
                    pe.transpose(ps[:, 4, o:o + GB], kc[0:GB, b, j * P:(j + 1) * P], ident[0:GB, 0:GB])
                    ins = pe.transpose(ps[:, 5, o:o + GB], klo[0:GB, b, j * P:(j + 1) * P], ident[0:GB, 0:GB])
            ins.then_inc(S("keysT"), 1)

            def sums(g0, n):
                with pe.Fori(0, n // SETS) as k:
                    for u in range(SETS):
                        pe.wait_ge(S("hot"), SETS * k + (g0 + u + 2))
                        pe.wait_ge(S("grp_free"), SETS * k + (g0 + u + 1))
                        for j in range(3):
                            ins = pe.matmul(ps[:, 6 + u % 2, 0:KEYS], src_hot[:, u // 2, :, 3 * (u % 2) + j], key_hot[:, u, j, :], start=j == 0, stop=j == 2)
                        ins.then_inc(S("grp_sum"), 1)

            def degrees(c):
                pe.wait_ge(S("grp_free"), GC * (c + 1) + 2)
                for s_ in range(NT):
                    pe.matmul(ps[:, DEG_BANK[c], :], onesq, at[:, c * NT + s_, :], start=s_ == 0, stop=s_ == NT - 1)

            pe.wait_ge(S("wqT_in"), 1)
            pe.wait_ge(S("xt_lo"), 2 * NC)
            pe.wait_ge(S("w_lo"), 2)
            def keys_values(b):
                if b:
                    pe.wait_ge(S("kv_z"), b)
                for t in range(4):
                    o = (4 * b + t) * P
                    for k in range(KD):
                        ins = three(ps[:, t, :], ht_hi[:, k, o:o + P], ht_lo[:, k, o:o + P], wkv_hi[:, k], wkv_lo[:, k], k == 0, k == KD - 1)
                ins.then_inc(S("kv"), 1)

            keys_values(0)
            for b in range(NT // 4 + 1):
                if b < NT // 4:
                    g0 = sum(G_BATCH) * b
                    sums(g0, G_BATCH[0])
                else:
                    sums(FOLD0, G_FOLD[0])
                if b:
                    pe.wait_ge(S("k_ready"), b)
                    pe.wait_ge(S("keycols"), 1)
                    for t in range(4):
                        n = P if 4 * (b - 1) + t < NT - 1 else LAST
                        first, last = b == 1 and t == 0, b == NT // 4 and t == 3
                        for G in range(KD):
                            ins = pe.matmul(ps[:, 4 + G, 0:P + 1], kv_n[0:n, t, G * P:(G + 1) * P], kv_n[0:n, t, D + G * (P + 1):D + (G + 1) * (P + 1)], start=first, stop=last)
                    ins.then_inc(S("kv_used"), 1)
                if b < NT // 4:
                    sums(g0 + G_BATCH[0], G_BATCH[1])
                    if b + 1 < NT // 4:
                        keys_values(b + 1)
                    sums(g0 + sum(G_BATCH[:2]), G_BATCH[2])
            pe.wait_ge(S("kvm"), 1)
            for G in range(KD):
                ins = pe.matmul(ps[:, 2 + G, 0:D + 1], kvm[:, G], wqT[:, G], start=True, stop=True)
            ins.then_inc(S("mT"), 1)
            sums(FOLD0 + G_FOLD[0], G_FOLD[1])
            pe.wait_ge(S("mT_in"), 1)
            pe.wait_ge(S("w1_in"), 16)
            for k in range(KD):
                for G in range(KD):
                    pe.matmul(ps[:, 0, k * D:(k + 1) * D], mT[:, G, k * P:(k + 1) * P], w1[:, G], start=G == 0, stop=G == KD - 1)
            for j in range(KD):
                for G in range(KD):
                    ins = pe.matmul(ps[:, 1, j:j + 1], w1[:, G, j * P:(j + 1) * P], retb[:, G:G + 1], start=G == 0, stop=G == KD - 1)
            ins.then_inc(S("m1"), 1)
            sums(FOLD0 + sum(G_FOLD[:2]), G_FOLD[2])
            pe.wait_ge(S("m1_lo"), 1)
            for i in range(2 * NC):
                c, f = divmod(i, 2)
                if i >= 4:
                    pe.wait_ge(S("h1f"), i - 3)
                for k in range(KD):
                    fs, cs = slice(f * P, (f + 1) * P), slice(c * 512, (c + 1) * 512)
                    ins = three(ps[:, 2 + i % 4, :], m1_hi[:, k, fs], m1_lo[:, k, fs], ht_hi[:, k, cs], ht_lo[:, k, cs], k == 0, k == KD - 1)
                ins.then_inc(S("h1"), 1)
                if f == 1:
                    sums(H10 + G_H1 * c, G_H1)
            pe.wait_ge(S("h1_lo"), 2 * NC)
            for t in range(NT):
                if t >= 3:
                    pe.wait_ge(S("mix_acc"), t - 2)
                for k in range(KD):
                    n = slice(t * P, (t + 1) * P)
                    ins = three(ps[:, OUT_BANK[t % 3], 0:D], h1_hi[:, k, n], h1_lo[:, k, n], w2_hi[:, k], w2_lo[:, k], k == 0, k == KD - 1)
                ins.then_inc(S("mix_out"), 1)
                if t % 2:
                    sums(OUT0 + G_OUT * (t // 2), G_OUT)
                if t in (5, 9, 13):
                    degrees((t - 5) // 4)
            pe.wait_ge(S("mix_acc"), NT)
            sums(LAST0, NG - LAST0)
            degrees(3)
            degrees(4)
            barrier(pe)
            with pe.If(unsorted(pe) > 0):
                pe.wait_ge(S("any_zero"), 1)
                with pe.Fori(0, PASSES) as q:
                    pe.wait_ge(S("any_keys"), q + 1)
                    for b in range(2):
                        for j in range(3):
                            o = j * NG + b * GB
                            pe.transpose(ps[:, 4, o:o + GB], any_c[0:GB, b, j * P:(j + 1) * P], ident[0:GB, 0:GB])
                            ins = pe.transpose(ps[:, 5, o:o + GB], any_lo[0:GB, j * P:(j + 1) * P], ident[0:GB, 0:GB])
                    ins.then_inc(S("any_keysT"), 1)
                    for c in range(NC):
                        with pe.Fori(0, GC) as gi:
                            pe.wait_ge(S("any_hot"), NG * q + GC * c + gi + 1)
                            pe.matmul(ps[:, 0, 0:KEYS].rearrange("p (s d) -> p s d", d=GW), ident16, at[:, c * NT:(c + 1) * NT, bass.ds(GW * gi, GW)], start=True, stop=False)
                            for j in range(3):
                                ins = pe.matmul(ps[:, 0, 0:KEYS], src_hot[:, 0, :, j], key_hot[:, 0, j, :], start=False, stop=j == 2)
                            ins.then_inc(S("any_sum"), 1)
                pe.wait_ge(S("any_out"), NG * PASSES + 1)
                for c in range(NC):
                    degrees(c)
            pe.nop()
            barrier(pe)
            for l in range(3):
                with pe.Fori(0, NC) as c:
                    if l:
                        pe.wait_ge(S("h_lo"), 2 * NC * (l - 1) + 2 * c + 6)
                        pe.wait_ge(S("mean"), 2 * NC * l - 2)
                    for u in range(4):
                        t = 4 * c + u
                        if l == 0:
                            pe.wait_ge(S("rcnt"), u + 1)
                        if l and u == 2:
                            pe.wait_ge(S("mean"), 2 * NC * l)
                        pe.wait_ge(S("g_lo"), NT * l + t + 1)
                        n = bass.ds(t * P, P)
                        for k in range(KD):
                            wbh, wbl = (w[:, l, k].rearrange("p w d -> p (w d)") for w in (wbf_hi, wbf_lo))
                            ins = three(ps[:, BANK[u], :], ht_hi[:, k, n], ht_lo[:, k, n], wbh, wbl, k == 0, k == KD - 1)
                        ins.then_inc(S("g"), 1)
                def sums_of(c, n):
                    cs = bass.ds(c * 512, n)
                    pe.wait_ge(S("h_lo"), 2 * (NC * l + c) + 2)
                    for f in range(2):
                        fs = slice(f * P, (f + 1) * P)
                        for k in range(KD):
                            ins = three(ps[:, bass.ds(4 + 2 * (c % 2) + f, 1), 0:n], wd_hi[:, l, k, fs], wd_lo[:, l, k, fs], ht_hi[:, k:k + 1, cs], ht_lo[:, k:k + 1, cs], k == 0, k == KD - 1)
                    ins.then_inc(S("own_sum"), 1)
                    pe.wait_ge(S("g_lo"), NT * (l + 1) + 4)
                    for s_ in range(NT):
                        for f in range(2):
                            for part, g_ in enumerate((g_hi, g_lo)):
                                ins = pe.matmul(ps[:, bass.ds(2 * (c % 2) + f, 1), 0:n], g_[:, s_, f * P:(f + 1) * P], at[:, bass.ds(c * NT + s_, 1), 0:n],
                                                start=s_ == 0 and part == 0, stop=s_ == NT - 1 and part == 1)
                    ins.then_inc(S("agg"), 1)

                with pe.Fori(0, NC - 1) as c:
                    sums_of(c, 512)
                sums_of(NC - 1, LASTC)
            for t in range(NT):
                if t % 4 == 0:
                    pe.wait_ge(S("h_lo"), 2 * NC * 2 + 2 * (t // 4) + 6)
                if t % 4 == 0:
                    pe.wait_ge(S("mean"), 2 * NC * 3 - 2)
                if t % 4 == 2:
                    pe.wait_ge(S("mean"), 2 * NC * 3)
                pe.wait_ge(S("f3_acc"), t + 1)
                n = slice(t * P, (t + 1) * P)
                for k in range(KD):
                    ins = three(ps[:, BANK[t % 4], 0:D], ht_hi[:, k, n], ht_lo[:, k, n], wf3_hi[:, k], wf3_lo[:, k], k == 0, k == KD - 1)
                ins.then_inc(S("f3"), 1)
            barrier(pe)
            pe.wait_ge(S("wr_in"), 32)
            for h in range(NT // 2 + 1):
                if h < NT // 2:
                    if 2 * h < Y_DVE:
                        pe.wait_ge(S("y_first"), 2 * h + 2)
                    else:
                        pe.wait_ge(S("y"), 2 * h + 2 - Y_DVE)
                    if h >= 2:
                        pe.wait_ge(S("yT_in"), h - 1)
                    for i in range(2 * KD):
                        t, k = 2 * h + i // KD, i % KD
                        ins = pe.transpose(ps[:, h % 2, i * P:(i + 1) * P], xn2[:, t, k * P:(k + 1) * P], ident)
                    ins.then_inc(S("yT"), 1)
                if h:
                    pe.wait_ge(S("yT_in"), h)
                    for i in range(2 * KD):
                        t, k = 2 * (h - 1) + i // KD, i % KD
                        ins = pe.matmul(ps[:, 2, t * NE:(t + 1) * NE], yT[:, (h - 1) % 2, i], wr[:, k], start=k == 0, stop=k == KD - 1)
                    ins.then_inc(S("logits"), 1)
            pe.wait_ge(S("hot12"), 1)
            h12 = hot12.rearrange("p t e -> p (t e)")
            pe.matmul(ps[:, 3, 0:NT * NE], below, h12, start=True, stop=True)
            pe.matmul(ps[:, 4, 0:NT * NE], ones, h12, start=True, stop=True).then_inc(S("ranks"), 1)
            for c in range(NC):
                pe.wait_ge(S("place"), c + 1)
                for i in range(TQ):
                    n = P if 4 * c + i % 4 < NT - 1 else LAST
                    ins = pe.matmul(ps[:, 5, 0:NB], place_hot[c % 2][0:n, i], blk_hot[c % 2][0:n, i],
                                    start=c == 0 and i == 0, stop=c == NC - 1 and i == TQ - 1)
                ins.then_inc(S("found"), 1)
            pe.sem_inc(S("e_turned"), 2)
            pe.sem_inc(S("e_h"), 2)
            pe.sem_inc(S("e_yp"), 2)
            barrier(pe)

            def turn(b, bb, u):
                pe.wait_ge(S(f"e_x{u}"), 16 * (bb + 1))
                pe.wait_ge(S("e_xe"), b + 1)
                for k in range(KD):
                    ins = pe.transpose(ps[:, 4 + u, k * P:(k + 1) * P], x_in[:, u, k * P:(k + 1) * P], ident)
                ins.then_inc(S("e_turned"), 1)

            def hidden(b, u):
                pe.wait_ge(S("e_w1"), b + 1)
                pe.wait_ge(S("e_xe"), b + 3)
                pe.wait_ge(S("e_gelu"), b + 1)
                for j in range(KH):
                    for k in range(KD):
                        js = slice(j * P, (j + 1) * P)
                        ins = three(ps[:, 2 * u + j // 4, (j % 4) * P:(j % 4 + 1) * P], w1_now[:, u, 0, k, js], w1_now[:, u, 1, k, js],
                                    xe_hi[:, u, k], xe_lo[:, u, k], k == 0, k == KD - 1)
                ins.then_inc(S("e_h"), 1)

            def outward(b, u):
                e = pe.value_load(blk_e[0:1, bass.ds(b, 1)], min_val=0, max_val=NE - 1)
                pe.wait_ge(S("e_lo"), b + 3)
                pe.wait_ge(S("e_out"), b + 1)
                for j in range(KH):
                    o = e * EWN + j * D
                    ins = three(ps[:, 6 + u, 0:D], h_hi[:, u, j], h_lo[:, u, j], mem[:, bass.ds(o + W2_HI, D)], mem[:, bass.ds(o + W2_LO, D)],
                                j == 0, j == KH - 1)
                ins.then_inc(S("e_yp"), 1)

            turn(0, 0, 0)
            turn(1, 0, 1)
            hidden(0, 0)
            with pe.Fori(0, NPAIR - 1) as bb:
                turn(2 * bb + 2, bb + 1, 0)
                hidden(2 * bb + 1, 1)
                outward(2 * bb, 0)
                turn(2 * bb + 3, bb + 1, 1)
                hidden(2 * bb + 2, 0)
                outward(2 * bb + 1, 1)
            hidden(NB_MAIN - 1, 1)
            outward(NB_MAIN - 2, 0)
            outward(NB_MAIN - 1, 1)
            with pe.If(blocks(pe) > NB_MAIN):
                for b in range(NB_MAIN, NB):
                    turn(b, b // 2, b % 2)
                    hidden(b, b % 2)
                    outward(b, b % 2)
            pe.nop()
            barrier(pe)



def lay_out(inputs):
    arrays = {k: np.ascontiguousarray(v) for k, v in inputs.items() if k not in ("src", "dst")}
    src, dst = np.asarray(inputs["src"]), np.asarray(inputs["dst"])
    size = STEP * (NWIN - 1) + WIN
    src_p = np.concatenate([src, np.zeros(size - E_ALL, src.dtype)])
    dst_p = np.concatenate([dst, np.full(size - E_ALL, NOWHERE, dst.dtype)])
    arrays["srcw"] = np.stack([src_p[i:i + WIN] for i in range(0, STEP * NWIN, STEP)])
    arrays["dstw"] = np.stack([dst_p[i:i + WIN] for i in range(0, STEP * NWIN, STEP)])
    arrays["dsamp"] = np.ascontiguousarray(dst_p[:STEP * NWIN:STEP].reshape(P, NS))
    arrays["dpair"] = np.stack([dst_p[i:i + EC + 1] for i in range(0, EC * P, EC)])
    return arrays


def kernel(**inputs):
    import concourse.bacc as bacc
    from concourse.bass_utils import run_bass_kernel_spmd

    nc = bacc.Bacc("TRN2", target_bir_lowering=False, num_devices=1)
    arrays = lay_out(inputs)
    aps = {k: nc.dram_tensor(k, a.shape, mybir.dt.from_np(a.dtype), kind="ExternalInput").ap() for k, a in arrays.items()}
    out = nc.dram_tensor("out", (N, D), F32, kind="ExternalOutput").ap()
    build(nc, aps, out)
    r = run_bass_kernel_spmd(nc, [arrays], core_ids=[0])
    return r.results[0]["out"]
```
